# Optimizing a Trainium2 kernel written in Bass

```python
import numpy as np
import jax
import jax.numpy as jnp

def _softmax(x, axis=-1):
    return jax.nn.softmax(x, axis=axis)

def _gelu(x):
    return jax.nn.gelu(x, approximate=True)

def _silu(x):
    return jax.nn.silu(x)

def _sigmoid(x):
    return jax.nn.sigmoid(x)

def _layernorm(x, axis=-1, eps=1e-05):
    m = jnp.mean(x, axis=axis, keepdims=True)
    v = jnp.var(x, axis=axis, keepdims=True)
    return (x - m) / jnp.sqrt(v + eps)

def _scatter_add(tgt, idx, src, axis=0):
    return tgt.at[idx].add(src)

def _segment_sum(src, seg, n):
    return jax.ops.segment_sum(src, seg, n)
kernel_name = 'mk_adaln_d1_jaxref_r8_5d3679'

def setup_inputs(seed: int=0):
    np.random.seed(seed)
    _w = jnp.asarray

    def _L0_attn_setup():
        import jax, jax.numpy as jnp
        import numpy as np
        H_SIZE = 256
        N_HEADS = 32
        D_HEAD = 64
        D_STATE = 64
        D_CONV = 4
        N_GROUPS = 1
        INTER = 1024
        D_INNER = N_HEADS * D_HEAD
        D_BC = N_GROUPS * D_STATE
        XBC_LEN = D_INNER + 2 * D_BC
        PROJ = D_INNER + XBC_LEN + N_HEADS
        EPS = 1e-05

        def rmsnorm(x, w):
            var = jnp.mean(x * x, axis=-1, keepdims=True)
            return w * (x * jax.lax.rsqrt(var + EPS))

        def mamba2(xn, in_proj_w, conv_w, conv_b, A_log, D_param, dt_bias, mnorm_w, out_proj_w):
            B, L, _ = xn.shape
            xz = xn @ in_proj_w.T
            z = xz[..., :D_INNER]
            xBC = xz[..., D_INNER:D_INNER + XBC_LEN]
            dt_proj = xz[..., D_INNER + XBC_LEN:]
            xc = jnp.transpose(xBC, (0, 2, 1))
            xc = jax.lax.conv_general_dilated(xc, conv_w, window_strides=(1,), padding=[(D_CONV - 1, 0)], dimension_numbers=('NCH', 'OIH', 'NCH'), feature_group_count=XBC_LEN)
            xc = jax.nn.silu(xc + conv_b[None, :, None])
            xc = jnp.transpose(xc, (0, 2, 1))
            x_conv = xc[..., :D_INNER]
            B_proj = xc[..., D_INNER:D_INNER + D_BC]
            C_proj = xc[..., D_INNER + D_BC:]
            dt = jax.nn.softplus(dt_proj + dt_bias)
            A = -jnp.exp(A_log)
            x_heads = x_conv.reshape(B, L, N_HEADS, D_HEAD)
            xs = jnp.moveaxis(x_heads, 1, 0)
            dts = jnp.moveaxis(dt, 1, 0)
            Bs = jnp.moveaxis(B_proj, 1, 0)
            Cs = jnp.moveaxis(C_proj, 1, 0)
            h0 = jnp.zeros((B, N_HEADS, D_HEAD, D_STATE), xn.dtype)

            def step(h, inp):
                x_t, dt_t, B_t, C_t = inp
                dA = jnp.exp(A[None, :] * dt_t)
                dBx = dt_t[..., None, None] * x_t[..., None] * B_t[:, None, None, :]
                h = dA[..., None, None] * h + dBx
                y = jnp.einsum('bhps,bs->bhp', h, C_t) + D_param[None, :, None] * x_t
                return (h, y)
            _, ys = jax.lax.scan(step, h0, (xs, dts, Bs, Cs))
            y = jnp.moveaxis(ys, 0, 1).reshape(B, L, D_INNER)
            y = y * jax.nn.silu(z)
            y = rmsnorm(y, mnorm_w)
            return y @ out_proj_w.T
        key = jax.random.key(seed)
        ks = jax.random.split(key, 10)
        s = 0.02
        B, L = (1, 128)
        return {'x': jax.random.normal(ks[0], (B, L, H_SIZE), jnp.float32), 'ln1_w': jnp.ones((H_SIZE,), jnp.float32), 'in_proj_w': jax.random.normal(ks[1], (PROJ, H_SIZE), jnp.float32) * s, 'conv_w': jax.random.normal(ks[2], (XBC_LEN, 1, D_CONV), jnp.float32) * 0.2, 'conv_b': jnp.zeros((XBC_LEN,), jnp.float32), 'A_log': jax.random.uniform(ks[3], (N_HEADS,), jnp.float32, 0.0, 1.0), 'D_param': jnp.ones((N_HEADS,), jnp.float32), 'dt_bias': jax.random.normal(ks[4], (N_HEADS,), jnp.float32) * s, 'mnorm_w': jnp.ones((D_INNER,), jnp.float32), 'out_proj_w': jax.random.normal(ks[5], (H_SIZE, D_INNER), jnp.float32) * s, 'ln2_w': jnp.ones((H_SIZE,), jnp.float32), 'mlp_in_w': jax.random.normal(ks[6], (2 * INTER, H_SIZE), jnp.float32) * s, 'mlp_out_w': jax.random.normal(ks[7], (H_SIZE, INTER), jnp.float32) * s}
    _L0_attn_in = _L0_attn_setup()

    def _L0_ffn_setup():
        import jax, jax.numpy as jnp
        import numpy as np

        def ternary_quantize(t, threshold, scale):
            return jnp.where(t > threshold, scale, jnp.where(t < -threshold, -scale, 0.0)).astype(t.dtype)
        key = jax.random.key(seed)
        k1, k2, k3 = jax.random.split(key, 3)
        B, S, D = (4, 512, 256)
        x = jax.random.normal(k1, (B, S, D), dtype=jnp.float32)
        weight = jax.random.normal(k2, (D, D), dtype=jnp.float32) * 0.02
        rram_variation = jax.random.normal(k3, (D, D), dtype=jnp.float32) * 0.05
        return {'x': x, 'weight': weight, 'rram_variation': rram_variation}
    _L0_ffn_in = _L0_ffn_setup()
    _L0_c = _w((lambda *s: np.random.randn(*s).astype(np.float32) * 0.05)(4, 256))
    _L0_wmod = _w((lambda *s: np.random.randn(*s).astype(np.float32) * 0.05)(256, 6 * 256) * 256 ** (-0.5))
    _d = {'L0_attn_x': _L0_attn_in['x'], 'L0_attn_ln1_w': _L0_attn_in['ln1_w'], 'L0_attn_in_proj_w': _L0_attn_in['in_proj_w'], 'L0_attn_conv_w': _L0_attn_in['conv_w'], 'L0_attn_conv_b': _L0_attn_in['conv_b'], 'L0_attn_A_log': _L0_attn_in['A_log'], 'L0_attn_D_param': _L0_attn_in['D_param'], 'L0_attn_dt_bias': _L0_attn_in['dt_bias'], 'L0_attn_mnorm_w': _L0_attn_in['mnorm_w'], 'L0_attn_out_proj_w': _L0_attn_in['out_proj_w'], 'L0_attn_ln2_w': _L0_attn_in['ln2_w'], 'L0_attn_mlp_in_w': _L0_attn_in['mlp_in_w'], 'L0_attn_mlp_out_w': _L0_attn_in['mlp_out_w'], 'L0_ffn_weight': _L0_ffn_in['weight'], 'L0_ffn_rram_variation': _L0_ffn_in['rram_variation'], 'L0_c': _L0_c, 'L0_wmod': _L0_wmod}
    _x0 = _d['L0_attn_x']
    _d['L0_attn_x'] = jax.random.normal(jax.random.fold_in(jax.random.key(seed), 1), (4, 1024, 256), dtype=_x0.dtype)
    del _x0
    return _d

def reference(L0_attn_x, L0_attn_ln1_w, L0_attn_in_proj_w, L0_attn_conv_w, L0_attn_conv_b, L0_attn_A_log, L0_attn_D_param, L0_attn_dt_bias, L0_attn_mnorm_w, L0_attn_out_proj_w, L0_attn_ln2_w, L0_attn_mlp_in_w, L0_attn_mlp_out_w, L0_ffn_weight, L0_ffn_rram_variation, L0_c, L0_wmod):

    def _L0_attn_ref(x, ln1_w, in_proj_w, conv_w, conv_b, A_log, D_param, dt_bias, mnorm_w, out_proj_w, ln2_w, mlp_in_w, mlp_out_w):
        import jax, jax.numpy as jnp
        import numpy as np
        H_SIZE = 256
        N_HEADS = 32
        D_HEAD = 64
        D_STATE = 64
        D_CONV = 4
        N_GROUPS = 1
        INTER = 1024
        D_INNER = N_HEADS * D_HEAD
        D_BC = N_GROUPS * D_STATE
        XBC_LEN = D_INNER + 2 * D_BC
        PROJ = D_INNER + XBC_LEN + N_HEADS
        EPS = 1e-05

        def rmsnorm(x, w):
            var = jnp.mean(x * x, axis=-1, keepdims=True)
            return w * (x * jax.lax.rsqrt(var + EPS))

        def mamba2(xn, in_proj_w, conv_w, conv_b, A_log, D_param, dt_bias, mnorm_w, out_proj_w):
            B, L, _ = xn.shape
            xz = xn @ in_proj_w.T
            z = xz[..., :D_INNER]
            xBC = xz[..., D_INNER:D_INNER + XBC_LEN]
            dt_proj = xz[..., D_INNER + XBC_LEN:]
            xc = jnp.transpose(xBC, (0, 2, 1))
            xc = jax.lax.conv_general_dilated(xc, conv_w, window_strides=(1,), padding=[(D_CONV - 1, 0)], dimension_numbers=('NCH', 'OIH', 'NCH'), feature_group_count=XBC_LEN)
            xc = jax.nn.silu(xc + conv_b[None, :, None])
            xc = jnp.transpose(xc, (0, 2, 1))
            x_conv = xc[..., :D_INNER]
            B_proj = xc[..., D_INNER:D_INNER + D_BC]
            C_proj = xc[..., D_INNER + D_BC:]
            dt = jax.nn.softplus(dt_proj + dt_bias)
            A = -jnp.exp(A_log)
            x_heads = x_conv.reshape(B, L, N_HEADS, D_HEAD)
            xs = jnp.moveaxis(x_heads, 1, 0)
            dts = jnp.moveaxis(dt, 1, 0)
            Bs = jnp.moveaxis(B_proj, 1, 0)
            Cs = jnp.moveaxis(C_proj, 1, 0)
            h0 = jnp.zeros((B, N_HEADS, D_HEAD, D_STATE), xn.dtype)

            def step(h, inp):
                x_t, dt_t, B_t, C_t = inp
                dA = jnp.exp(A[None, :] * dt_t)
                dBx = dt_t[..., None, None] * x_t[..., None] * B_t[:, None, None, :]
                h = dA[..., None, None] * h + dBx
                y = jnp.einsum('bhps,bs->bhp', h, C_t) + D_param[None, :, None] * x_t
                return (h, y)
            _, ys = jax.lax.scan(step, h0, (xs, dts, Bs, Cs))
            y = jnp.moveaxis(ys, 0, 1).reshape(B, L, D_INNER)
            y = y * jax.nn.silu(z)
            y = rmsnorm(y, mnorm_w)
            return y @ out_proj_w.T
        h = mamba2(rmsnorm(x, ln1_w), in_proj_w, conv_w, conv_b, A_log, D_param, dt_bias, mnorm_w, out_proj_w)
        x = x + h
        hh = rmsnorm(x, ln2_w) @ mlp_in_w.T
        gate, up = (hh[..., :INTER], hh[..., INTER:])
        h2 = jax.nn.silu(gate) * up @ mlp_out_w.T
        return x + h2

    def _L0_ffn_ref(x, weight, rram_variation):
        import jax, jax.numpy as jnp
        import numpy as np

        def ternary_quantize(t, threshold, scale):
            return jnp.where(t > threshold, scale, jnp.where(t < -threshold, -scale, 0.0)).astype(t.dtype)
        TH_X, SC_X = (0.33, 0.5)
        TH_W, SC_W = (0.2, 0.6)
        x_q = ternary_quantize(x, TH_X, SC_X)
        w_q = ternary_quantize(weight, TH_W, SC_W)
        w_rram = w_q + rram_variation
        return jnp.einsum('bsd,od->bso', x_q, w_rram)
    x = L0_attn_x
    mod = (_silu(L0_c) @ L0_wmod).reshape(L0_c.shape[0], 6, 1, -1)
    sa, ca, ga, sb, cb, gb = (mod[:, 0], mod[:, 1], mod[:, 2], mod[:, 3], mod[:, 4], mod[:, 5])
    ga = (2 * (ga >= 0) - 1) * jnp.maximum(jnp.abs(ga), 0.25)
    gb = (2 * (gb >= 0) - 1) * jnp.maximum(jnp.abs(gb), 0.25)
    h = _layernorm(x, axis=-1) * (1 + ca) + sa
    x = x + ga * _L0_attn_ref(h, L0_attn_ln1_w, L0_attn_in_proj_w, L0_attn_conv_w, L0_attn_conv_b, L0_attn_A_log, L0_attn_D_param, L0_attn_dt_bias, L0_attn_mnorm_w, L0_attn_out_proj_w, L0_attn_ln2_w, L0_attn_mlp_in_w, L0_attn_mlp_out_w)
    h = _layernorm(x, axis=-1) * (1 + cb) + sb
    x = x + gb * _L0_ffn_ref(h, L0_ffn_weight, L0_ffn_rram_variation)
    return x

_drawn_inputs = setup_inputs


def setup_inputs(seed=0):
    import zlib

    import numpy as np

    out = dict(_drawn_inputs(seed))
    spreads = {'L0_attn_ln1_w': (1.0, 0.2),
     'L0_attn_conv_b': (0.0, 0.1),
     'L0_attn_D_param': (1.0, 0.2),
     'L0_attn_mnorm_w': (1.0, 0.2),
     'L0_attn_ln2_w': (1.0, 0.6)}
    factors = {'L0_attn_A_log': 64.0,
     'L0_attn_dt_bias': 64.0,
     'L0_attn_mlp_in_w': 5.235,
     'L0_attn_mlp_out_w': 5.23}
    for name, (base, spread) in spreads.items():
        noise = np.random.default_rng([zlib.crc32(name.encode()), seed]).standard_normal(out[name].shape)
        drawn = base * np.exp(spread * noise) if base else spread * noise
        out[name] = jnp.asarray(drawn.astype(out[name].dtype))
    for name, factor in factors.items():
        out[name] = (out[name] * factor).astype(out[name].dtype)
    return out
```

```python
from contextlib import ExitStack

import concourse.bass as bass
from concourse import mybir

F32 = mybir.dt.float32
F32R = mybir.dt.float32r
BF16 = mybir.dt.bfloat16
ALU = mybir.AluOpType
ACT = mybir.ActivationFunctionType

P = 128
HID = 256
KH = HID // P
BATCH, SEQ = 4, 1024
HEADS, HD, NS = 32, 64, 64
DIN = HEADS * HD
TAPS = 4
INTER = 1024
EPS = 1e-5
T = 512
CH = 128
NC = T // CH
IPB = SEQ // T
NI = BATCH * IPB
YT = DIN // P
TPS = 2
HPS = 2 * TPS
SPI = YT // TPS
SPB = SPI * IPB
NSTEP = SPB * BATCH
WT = 2 + 2 * YT
MOD = 6 * HID
THX, SCX, THW, SCW = 0.33, 0.5, 0.2, 0.6


def wait(eng, sem, value):
    if isinstance(value, int) and value <= 0:
        return
    eng.wait_ge(sem, value)


def wait_apart(eng, sem, value):
    if not isinstance(value, int):
        value = eng.to_reg(value)
        eng.wait_ge(sem, 1)
    eng.wait_ge(sem, value)


def mamba_phase(nc, x, w_in, ln1, conv_w, conv_b, a_log, d_par, dt_bias, w_out, mnorm, c_t, w_mod,
                h_dram, o_dram, mod_dram):
    ctx = ExitStack()
    with ctx:
        def sb(name, shape, dt=F32):
            return ctx.enter_context(nc.sbuf_tensor(name, shape, dt))

        def sem(name):
            return ctx.enter_context(nc.semaphore(name))

        inject = sb("inject", [P, NC, CH])
        ident = inject[:, 0, :]
        select = sb("select", [96, HEADS, P // 2], BF16)
        ones = sb("ones", [P, 1])
        neg_half = sb("neg_half", [P, NC])
        w_hi = sb("w_hi", [P, KH, WT * P], F32R)
        w_lo = sb("w_lo", [P, KH, WT * P], F32R)
        w_o = sb("w_o", [P, YT, HID])
        ln1_c = sb("ln1_c", [P, KH])
        mn_c = sb("mn_c", [P, YT])
        cw = sb("cw", [P, YT + 2, TAPS])
        cb = sb("cb", [P, YT + 2])
        dpar = sb("dpar", [P, YT])
        dtb = sb("dtb", [P, HEADS])
        neg_a = sb("neg_a", [P, HEADS])
        cs_t = sb("cs_t", [P, KH, BATCH])
        mod_row = sb("mod_row", [P, 2, HID])
        xt = sb("xt", [P, NC, HID])
        hs = sb("hs", [P, NC, HID])
        stats = sb("stats", [P, NC, 6])
        mv = sb("mv", [P, NC, 2])
        ve = sb("ve", [P, NC])
        rstd = sb("rstd", [P, NC])
        ssq = sb("ssq", [P, NC])
        ms = sb("ms", [P, NC])
        r1 = sb("r1", [P, NC])
        h_hi = sb("h_hi", [P, KH, T], F32R)
        h_lo = sb("h_lo", [P, KH, T], F32R)
        raw = sb("raw", [P, 2, TAPS - 1 + T])
        tail = sb("tail", [P, YT + 2, TAPS - 1])
        xc = sb("xc", [P, 2, TPS, T])
        cc = sb("cc", [P, 2, T])
        bb = sb("bb", [NS, T])
        u_t = hs[:, :, 0 * HEADS:1 * HEADS]
        a_t = hs[:, :, 1 * HEADS:2 * HEADS]
        e_t = hs[:, :, 2 * HEADS:3 * HEADS]
        l_t = hs[:, :, 3 * HEADS:4 * HEADS]
        m_t = hs[:, :, 4 * HEADS:5 * HEADS]
        dt_s = sb("dt_s", [P, NC, HEADS])
        tl = sb("tl", [96, 2, T])
        zero = sb("zero", [HEADS, CH])
        parts = sb("parts", [96, 2, T], BF16)
        g_s = sb("g_s", [P, 2, NC, CH])
        b_tok = sb("b_tok", [P, 2, NC, NS])
        xdt = sb("xdt", [P, 2, NC, TPS * P])
        xw = sb("xw", [P, NC, TPS * P])
        dec = sb("dec", [P, 2, HPS, T])
        w_end = sb("w_end", [P, NC, HPS])
        p_end = sb("p_end", [P, TPS, NC])
        cp = sb("cp", [P, TPS, T])
        state = sb("state", [P, SPI, TPS, HD])
        s_ch = sb("s_ch", [P, NC - 1, TPS, HD])
        s_blk = sb("s_blk", [P, NC, TPS, P])
        yb = sb("yb", [P, YT, T])
        sq = sb("sq", [P, T])
        acc = sb("acc", [P, T])
        o_acc = sb("o_acc", [P, NC, HID])
        o_ms = sb("o_ms", [P, NC])
        r_y = sb("r_y", [P, NC])
        w_stage = dec[:, :, :, :].rearrange("p a h t -> p (a h t)")
        wm = yb[:, 0:KH * MOD // T, :].rearrange("p a t -> p (a t)")
        mod_s = yb[0:BATCH, 8:11, :].rearrange("p a t -> p (a t)")
        mod_a = yb[0:BATCH, 11:14, :].rearrange("p a t -> p (a t)")

        pj = [ctx.enter_context(nc.psum_tensor(f"pj{i}", [P, T], F32)) for i in range(2)]
        da = [ctx.enter_context(nc.psum_tensor(f"da{i}", [P, T], F32)) for i in range(2)]
        yp = [ctx.enter_context(nc.psum_tensor(f"yp{i}", [P, T], F32)) for i in range(2)]
        ma = ctx.enter_context(nc.psum_tensor("ma", [P, T], F32))
        mb = ctx.enter_context(nc.psum_tensor("mb", [P, T], F32))

        s = {n: sem(n) for n in (
            "const_set consts small_loaded c_silu w_head mod_sign mod_ready mod_fix mod_stored wo_loaded "
            "w_ready wo_ready neg_a_ready misc_set "
            "x_loaded row_loaded bn_done ve_done rstd_done xn_done h_done h_stored ssq_done ms_done r1_done "
            "hs_done ht_ready hh_done hl_done "
            "pj_ready pj_taken halo_done conv_tap x_ready bc_tap bc_halo bc_ready dt_copied "
            "dtt_ready u_done a_done e_done l_done dtc dt_done da_exp dat_ready dat_taken parts_done "
            "g_ready g_taken bt_ready bt_taken "
            "xt_ready xdt_done da_ready scan_done wend_done pend_done cp_done xw_done m_done "
            "ds_ready chain_done blk_done y_ready skip_done gate_done sq_done acc_done "
            "o_ready o_taken q_ready oms_done ry_done o_scaled o_stored").split()}

        w_loaded = [sem(f"w_loaded{n}") for n in range(4)]

        def tile_count(i, idx):
            return WT * i + idx + 1

        class At:

            def __init__(self, b, j):
                self.k = SPB * b + j if not isinstance(b, int) or b else j
                self.js = j % SPB
                self.i = IPB * b + j // SPI if not isinstance(b, int) or b else j // SPI
                self.q = (j // SPI) % IPB
                self.st = j % SPI
                self.b = b

        block = ctx.enter_context(nc.Block())

        HEAD = 4
        TAIL = SPB + 4

        def run(eng, slot):
            for j in range(HEAD):
                slot(0, j)
            with eng.Fori(0, BATCH - 1) as b:
                for j in range(HEAD, HEAD + SPB):
                    slot(b, j)
            for j in range(HEAD, TAIL):
                slot(BATCH - 1, j)

        def exists(b, j, back):
            if isinstance(b, int):
                return 0 <= SPB * b + j - back < NSTEP
            return True

        def out_slot(b, j):
            at = At(b, j)
            if at.st == 6 and exists(b, j, 0):
                return True, 0, at.i
            if at.st == 2 and exists(b, j, SPI) :
                return True, 1, at.i - 1
            return None

        def blk_count(b, j):
            base = (2 * SPB + 2 * SPI) * b if not isinstance(b, int) or b else 0
            full = j // SPB
            js = j % SPB
            return base + (2 * SPB + 2 * SPI) * full + 2 * (js + 1) + 2 * max(0, js + 1 - SPI)

        @block.sync
        def _(sp):
            sp.sem_inc(s["o_stored"], 16)
            sp.dma_start(cs_t[:, :, :], c_t).then_inc(s["small_loaded"], 16)
            sp.dma_start(wm.rearrange("p (k n) -> p k n", k=KH), w_mod.rearrange("(k p) n -> p k n", p=P)
                         ).then_inc(s["small_loaded"], 16)
            sp.dma_start(ln1_c[:, :], ln1).then_inc(s["small_loaded"], 16)
            sp.dma_start(neg_a[:, :], a_log.broadcast_to([P, HEADS])
                         ).then_inc(s["small_loaded"], 16)
            sp.dma_start(xt[:, :, :], x[0:T, :].rearrange("(c p) n -> p c n", p=P)).then_inc(s["x_loaded"], 16)
            for n in range(WT // 2):
                if n == 4:
                    sp.wait_ge(s["mod_fix"], 7)
                    sp.dma_start(mod_dram, mod_s).then_inc(s["mod_stored"], 16)
                    sp.wait_ge(s["mod_stored"], 16)
                    sp.dma_start(mod_row[:, :, :].rearrange("p a n -> p (a n)"),
                                 mod_dram[0:1, 0:2 * HID].broadcast_to([P, 2 * HID])).then_inc(s["row_loaded"], 16)
                if n >= 4:
                    sp.wait_ge(s["w_ready"], 2 * (n - 3))
                sp.dma_start(w_stage[:, (n % 4) * 2 * P * KH:(n % 4 + 1) * 2 * P * KH].rearrange("p (k n) -> p k n", k=KH),
                             w_in.rearrange("(k p) n -> p k n", p=P)[:, :, n * 2 * P:(n + 1) * 2 * P]
                             ).then_inc(w_loaded[n % 4], 16)
                if n == 0:
                    for dst, src in ((cw[:, :, :], conv_w),
                                     (cb[:, :], conv_b),
                                     (dpar[:, :], d_par),
                                     (dtb[:, :], dt_bias.broadcast_to([P, HEADS])),
                                     (mn_c[:, :], mnorm)):
                        sp.dma_start(dst, src).then_inc(s["small_loaded"], 16)
            sp.dma_start(w_o[:, :, :], w_out.rearrange("(t p) n -> p t n", p=P)).then_inc(s["wo_loaded"], 16)
            def store_h(i):
                sp.wait_ge(s["h_done"], 2 * i + 2)
                sp.dma_start(h_dram[bass.ds(i * T, T), :].rearrange("(c p) n -> p c n", p=P), xt[:, :, :]
                             ).then_inc(s["h_stored"], 16)

            store_h(0)

            def slot(b, j):
                at = At(b, j)
                if at.st == 3 and (exists(b, j, -5)):
                    nxt = at.i + 1
                    wait_apart(sp, s["h_stored"], 16 * nxt)
                    sp.wait_ge(s["hs_done"], 4 * nxt)
                    sp.dma_start(xt[:, :, :], x[bass.ds(nxt * T, T), :].rearrange("(c p) n -> p c n", p=P)
                                 ).then_inc(s["x_loaded"], 16)
                    if at.q == IPB - 1:
                        row = at.b + 1 + (j // SPB)
                        sp.wait_ge(s["h_done"], 2 * nxt)
                        sp.dma_start(mod_row[:, :, :].rearrange("p a n -> p (a n)"),
                                     mod_dram[bass.ds(row, 1), 0:2 * HID].broadcast_to([P, 2 * HID])
                                     ).then_inc(s["row_loaded"], 16)
                if at.st == 6 and exists(b, j, -2):
                    store_h(at.i + 1)
                if at.st == 3 and exists(b, j, 4):
                    if not isinstance(b, int) or b or j >= SPI:
                        sp.wait_ge(s["o_scaled"], 4 * at.i)
                        sp.dma_start(o_dram[bass.ds((at.i - 1) * T, T), :].rearrange("(c p) n -> p c n", p=P),
                                     o_acc[:, :, :]).then_inc(s["o_stored"], 16)

            run(sp, slot)
            sp.wait_ge(s["o_stored"], 16 * (NI + 1))
            sp.wait_ge(s["h_stored"], 16 * NI)

        @block.gpsimd
        def _(pool):
            pool.memset(inject[:, :, :], 0.0).then_inc(s["const_set"], 1)
            pool.memset(select[:, :, :], 0.0).then_inc(s["const_set"], 1)
            pool.memset(ones[:, :], 1.0).then_inc(s["consts"], 1)
            pool.memset(neg_half[:, :], -0.5).then_inc(s["consts"], 1)
            pool.memset(zero[:, :], 0.0).then_inc(s["consts"], 1)
            pool.memset(s_blk[:, :, :, :], 0.0).then_inc(s["consts"], 1)
            pool.wait_ge(s["const_set"], 2)
            pool.affine_select(out=inject[:, :, :], in_=inject[:, :, :], compare_op=ALU.not_equal, fill=1.0, base=0,
                               pattern=[[0, NC], [-1, CH]], channel_multiplier=1).then_inc(s["consts"], 1)
            for r in range(3):
                third = select[32 * r:32 * r + 32, :, :]
                pool.wait_ge(s["consts"], 5 + r)
                pool.affine_select(out=third, in_=third, compare_op=ALU.not_equal, fill=1.0, base=0,
                                   pattern=[[-1, HEADS], [0, P // 2]], channel_multiplier=1).then_inc(s["consts"], 1)
            pool.wait_ge(s["consts"], 8)

            def norm_power(i):
                pool.wait_ge(s["ve_done"], i + 1)
                if not isinstance(i, int) or i:
                    pool.wait_ge(s["xn_done"], 4 * i)
                pool.tensor_tensor(rstd[:, :], ve[:, :], neg_half[:, :], ALU.pow).then_inc(s["rstd_done"], 1)

            def modulate(i, row):
                pool.wait_ge(s["xn_done"], 4 * i + 4)
                pool.wait_ge(s["row_loaded"], 16 * (row + 1))
                pool.tensor_tensor(xt[:, :, :], xt[:, :, :], mod_row[:, 1:2, :].broadcast_to([P, NC, HID]), ALU.mult
                                   ).then_inc(s["h_done"], 1)
                pool.wait_ge(s["h_done"], 2 * i + 1)
                pool.tensor_tensor(xt[:, :, :], xt[:, :, :], mod_row[:, 0:1, :].broadcast_to([P, NC, HID]), ALU.add
                                   ).then_inc(s["h_done"], 1)

            def rms_power(i):
                pool.wait_ge(s["ms_done"], i + 1)
                if not isinstance(i, int) or i:
                    pool.wait_ge(s["hs_done"], 4 * i)
                pool.tensor_tensor(r1[:, :], ms[:, :], neg_half[:, :], ALU.pow).then_inc(s["r1_done"], 1)

            norm_power(0)
            modulate(0, 0)
            rms_power(0)

            def slot(b, j):
                at = At(b, j)
                k = at.k
                nxt = at.st >= 4 and exists(b, j, at.st - SPI)
                if nxt and at.st == 5:
                    norm_power(at.i + 1)
                if nxt and at.st == 6:
                    modulate(at.i + 1, at.b + ((j // SPI + 1) // IPB))
                if exists(b, j, 1):
                    m = At(b, j - 1)
                    buf = m.js % 2
                    pool.wait_ge(s["wend_done"], k)
                    if exists(b, j, 2):
                        pool.wait_ge(s["ds_ready"], k - 1)
                    pool.tensor_tensor(
                        xw[:, :, :].rearrange("p c (h d) -> p (c h) d", d=HD),
                        xdt[:, buf, :, :].rearrange("p c (h d) -> p (c h) d", d=HD),
                        w_end[:, :, :].rearrange("p c h -> p (c h)").unsqueeze(2).broadcast_to([P, NC * HPS, HD]),
                        ALU.mult).then_inc(s["xw_done"], 1)
                    pool.wait_ge(s["g_taken"], m.i + 1)
                    for h in range(HPS):
                        d = dec[:, buf, h, :]
                        pool.tensor_tensor(d, d, g_s[:, m.q, :, :].rearrange("p c t -> p (c t)"), ALU.mult
                                           ).then_inc(s["m_done"], 1)
                if exists(b, j, 2):
                    o = At(b, j - 2)
                    for t in range(TPS):
                        pool.wait_ge(s["skip_done"], 2 * (k - 2) + t + 1)
                        pool.wait_ge(s["pj_taken"], tile_count(o.i, 2 + 4 * o.st + t))
                        ytile = yb[:, TPS * o.st + t, :]
                        pool.tensor_tensor(ytile, ytile, xc[:, o.js % 2, t, :], ALU.mult).then_inc(s["gate_done"], 1)
                if exists(b, j, 3):
                    o = At(b, j - 3)
                    for t in range(TPS):
                        wait_apart(pool, s["sq_done"], 2 * (k - 3) + t + 1)
                        if o.st == 0 and t == 0:
                            if not isinstance(b, int) or k >= SPI:
                                wait_apart(pool, s["q_ready"], o.i)
                            pool.tensor_copy(acc[:, :], sq[:, :]).then_inc(s["acc_done"], 1)
                        else:
                            pool.wait_ge(s["acc_done"], 2 * (k - 3) + t)
                            pool.tensor_tensor(acc[:, :], acc[:, :], sq[:, :], ALU.add).then_inc(s["acc_done"], 1)
                if at.st == 3 and exists(b, j, 4) and (not isinstance(b, int) or k >= SPI):
                    pool.wait_ge(s["oms_done"], at.i)
                    pool.tensor_tensor(r_y[:, :], o_ms[:, :], neg_half[:, :], ALU.pow).then_inc(s["ry_done"], 1)
                if nxt and at.st == 7:
                    rms_power(at.i + 1)

            run(pool, slot)

        @block.scalar
        def _(act):
            act.wait_ge(s["small_loaded"], 16 * 9)
            act.activation(cs_t[:, :, :], cs_t[:, :, :], ACT.Silu).then_inc(s["c_silu"], 1)
            act.activation(neg_a[:, :], neg_a[:, :], ACT.Exp).then_inc(s["neg_a_ready"], 1)
            act.wait_ge(s["neg_a_ready"], 1)
            act.mul(neg_a[:, :], neg_a[:, :], -1.0).then_inc(s["neg_a_ready"], 1)

            def squares(i):
                act.wait_ge(s["h_done"], 2 * i + 2)
                for c in range(NC):
                    act.activation(hs[:, c, :], xt[:, c, :], ACT.Square, accum_out=ssq[:, c:c + 1]
                                   ).then_inc(s["ssq_done"], 1)

            def scale_h(i):
                act.wait_ge(s["r1_done"], i + 1)
                act.wait_ge(s["ssq_done"], 4 * i + 4)
                for c in range(NC):
                    act.activation(hs[:, c, :], xt[:, c, :], ACT.Copy, scale=r1[:, c:c + 1]).then_inc(s["hs_done"], 1)

            squares(0)
            scale_h(0)

            def slot(b, j):
                at = At(b, j)
                k = at.k
                new = exists(b, j, 0)
                if exists(b, j, 2):
                    o = At(b, j - 2)
                    wait(act, s["y_ready"], 2 * (k - 2))
                    if o.q:
                        for half in range(2):
                            r = slice(64 * half, 64 * half + 64)
                            act.activation(s_blk[r, 0, :, 64 * half:64 * half + 64], state[r, o.st, :, :], ACT.Copy
                                           ).then_inc(s["blk_done"], 1)
                if new and at.st == 0:
                    for n, rows in ((0, P), (1, NS)):
                        idx = n
                        act.wait_ge(s["pj_ready"], tile_count(at.i, idx))
                        prev_taps(act, b, j, n)
                        act.activation(raw[0:rows, n, TAPS - 1:], pj[idx % 2][0:rows, :], ACT.Copy).then_inc(s["misc_set"], 1)
                        dst = cc[:, at.q, :] if n == 0 else bb[:, :]
                        if n == 1 and (not isinstance(b, int) or at.k):
                            act.wait_ge(s["bt_ready"], at.i)
                            act.wait_ge(s["g_ready"], at.i)
                        if n == 0 and (not isinstance(b, int) or at.k):
                            act.wait_ge(s["cp_done"], 2 * (k - 2))
                        if n == 1:
                            if not isinstance(b, int) or at.k:
                                act.wait_ge(s["parts_done"], 5 * at.i)
                            act.activation(tl[64:96, 0, :], pj[idx % 2][64:96, :], ACT.Copy).then_inc(s["dt_copied"], 1)
                        act.activation(dst, pj[idx % 2][0:rows, :], ACT.Identity,
                                       bias=cb[0:rows, YT + n:YT + n + 1], scale=cw[0:rows, YT + n, TAPS - 1:TAPS]
                                       ).then_inc(s["pj_taken"], 1)
                if exists(b, j, 2):
                    o = At(b, j - 2)
                    act.wait_ge(s["chain_done"], 8 * (k - 2) + 6)
                    for half in range(2):
                        r = slice(64 * half, 64 * half + 64)
                        dst = s_blk[r, 1:NC, :, 64 * half:64 * half + 64].rearrange("p c a d -> p (c a) d")
                        act.activation(dst, s_ch[r, :, :, :].rearrange("p c a d -> p (c a) d"), ACT.Copy
                                       ).then_inc(s["blk_done"], 1)
                if isinstance(b, int) and k == HEAD - 1:
                    act.wait_ge(s["mod_stored"], 16)
                if new:
                    for t in range(TPS):
                        idx = 2 + 4 * at.st + t
                        act.wait_ge(s["pj_ready"], tile_count(at.i, idx))
                        act.activation(yb[:, TPS * at.st + t, :], pj[idx % 2][:, :], ACT.Silu).then_inc(s["pj_taken"], 1)
                if new and at.st == 0:
                    for n, dst in ((0, cc[:, at.q, :]), (1, bb[:, :])):
                        act.wait_ge(s["bc_tap"], 6 * at.i + 5 + n)
                        act.activation(dst, dst, ACT.Silu).then_inc(s["bc_ready"], 1)
                if exists(b, j, 3):
                    o = At(b, j - 3)
                    for t in range(TPS):
                        act.wait_ge(s["gate_done"], 2 * (k - 3) + t + 1)
                        wait(act, s["acc_done"], 2 * (k - 3) + t)
                        act.activation(sq[:, :], yb[:, TPS * o.st + t, :], ACT.Square).then_inc(s["sq_done"], 1)
                if new:
                    for t in range(TPS):
                        idx = 2 + 4 * at.st + TPS + t
                        ch = TPS * at.st + t
                        act.wait_ge(s["pj_ready"], tile_count(at.i, idx))
                        if at.st == 0:
                            act.wait_ge(s["bc_tap"], 6 * at.i + 5 + t)
                            act.wait_ge(s["bc_halo"], 4 * at.i + 4)
                        else:
                            act.wait_ge(s["conv_tap"], 6 * (k - 1) + 5 + t)
                            act.wait_ge(s["halo_done"], 4 * k)
                        act.activation(raw[:, t, TAPS - 1:], pj[idx % 2][:, :], ACT.Copy).then_inc(s["misc_set"], 1)
                        if not (isinstance(b, int) and k < 2):
                            act.wait_ge(s["gate_done"], 2 * (k - 2) + t + 1)
                        act.activation(xc[:, at.js % 2, t, :], pj[idx % 2][:, :], ACT.Identity,
                                       bias=cb[:, ch:ch + 1], scale=cw[:, ch, TAPS - 1:TAPS]).then_inc(s["pj_taken"], 1)
                if new and at.st == 0:
                    act.wait_ge(s["a_done"], at.i + 1)
                    act.activation(e_t[:, :, :], a_t[:, :, :], ACT.Exp, scale=-1.0).then_inc(s["e_done"], 1)
                    act.wait_ge(s["e_done"], at.i + 1)
                    act.activation(l_t[:, :, :], e_t[:, :, :], ACT.Ln, bias=1.0).then_inc(s["l_done"], 1)
                if new:
                    for t in range(TPS):
                        act.wait_ge(s["conv_tap"], 6 * k + 5 + t)
                        act.activation(xc[:, at.js % 2, t, :], xc[:, at.js % 2, t, :], ACT.Silu).then_inc(s["x_ready"], 1)
                if new and at.st == 0:
                    act.wait_ge(s["dtc"], 8 * at.i + 8)
                    act.activation(a_t[:, :, :], a_t[:, :, :], ACT.Exp).then_inc(s["da_exp"], 1)
                if at.st == 6 and exists(b, j, -2):
                    squares(at.i + 1)
                if at.st == 7 and exists(b, j, -1):
                    scale_h(at.i + 1)

            def prev_taps(eng, b, j, n):
                at = At(b, j)
                if not isinstance(b, int) or at.k:
                    eng.wait_ge(s["conv_tap"], 6 * (at.k - 1) + 5 + n)
                    eng.wait_ge(s["halo_done"], 4 * at.k)

            run(act, slot)

        @block.vector
        def _(dve):
            def token_norm_a(i):
                dve.wait_ge(s["x_loaded"], 16 * (i + 1))
                for c in range(NC):
                    dve.bn_stats(stats[:, c, :], xt[:, c, :]).then_inc(s["bn_done"], 1)
                wait_apart(dve, s["bn_done"], 8 * i + 4)
                for c in range(NC):
                    dve.bn_aggr(mv[:, c, :], stats[:, c, :]).then_inc(s["bn_done"], 1)
                dve.wait_ge(s["bn_done"], 8 * i + 8)
                dve.tensor_scalar(ve[:, :], mv[:, :, 1], EPS, None, ALU.add).then_inc(s["ve_done"], 1)

            def token_norm_b(i):
                dve.wait_ge(s["rstd_done"], i + 1)
                for c in range(NC):
                    dve.tensor_scalar(xt[:, c, :], xt[:, c, :], mv[:, c, 0:1], rstd[:, c:c + 1], ALU.subtract, ALU.mult
                                      ).then_inc(s["xn_done"], 1)

            def token_ms(i):
                dve.wait_ge(s["ssq_done"], 4 * i + 4)
                dve.tensor_scalar(ms[:, :], ssq[:, :], 1.0 / HID, EPS, ALU.mult, ALU.add).then_inc(s["ms_done"], 1)

            token_norm_a(0)
            dve.wait_ge(s["small_loaded"], 16 * 9)
            dve.wait_ge(s["mod_ready"], 3)
            for n in range(3):
                dve.tensor_copy(mod_s[:, n * T:(n + 1) * T], [ma, mb, yp[0]][n][0:BATCH, :]).then_inc(s["mod_fix"], 1)
            dve.wait_ge(s["mod_fix"], 3)
            for o in (1, 4):
                dve.tensor_scalar(mod_s[:, o * HID:(o + 1) * HID], mod_s[:, o * HID:(o + 1) * HID], 1.0, None, ALU.add
                                  ).then_inc(s["mod_fix"], 1)
            for n, o in enumerate((2, 5)):
                g = mod_s[:, o * HID:(o + 1) * HID]
                mag = mod_a[:, 2 * n * HID:(2 * n + 1) * HID]
                sgn = mod_a[:, (2 * n + 1) * HID:(2 * n + 2) * HID]
                dve.scalar_tensor_tensor(mag, g, -1.0, g, ALU.mult, ALU.max).then_inc(s["mod_sign"], 1)
                dve.wait_ge(s["mod_sign"], 3 * n + 1)
                dve.tensor_scalar(mag, mag, 0.25, None, ALU.max).then_inc(s["mod_sign"], 1)
                dve.tensor_scalar(sgn, g, 0.0, 2.0, ALU.is_ge, ALU.mult).then_inc(s["mod_sign"], 1)
                dve.wait_ge(s["mod_sign"], 3 * n + 3)
                dve.scalar_tensor_tensor(g, sgn, -1.0, mag, ALU.add, ALU.mult).then_inc(s["mod_fix"], 1)
            for n in range(WT // 2):
                dve.wait_ge(w_loaded[n % 4], 16 * (n // 4 + 1))
                st_n = w_stage[:, (n % 4) * 2 * P * KH:(n % 4 + 1) * 2 * P * KH].rearrange("p (k n) -> p k n", k=KH)
                for kk in range(KH):
                    dve.tensor_scalar(w_hi[:, kk, n * 2 * P:(n + 1) * 2 * P], st_n[:, kk, :], ln1_c[:, kk:kk + 1], None,
                                      ALU.mult).then_inc(s["w_head"], 1)
                for kk in range(KH):
                    dve.wait_ge(s["w_head"], KH * n + kk + 1)
                    dve.scalar_tensor_tensor(w_lo[:, kk, n * 2 * P:(n + 1) * 2 * P], st_n[:, kk, :], ln1_c[:, kk:kk + 1],
                                             w_hi[:, kk, n * 2 * P:(n + 1) * 2 * P].bitcast(F32), ALU.mult, ALU.subtract
                                             ).then_inc(s["w_ready"], 1)
                if n == 1:
                    token_norm_b(0)
                if n == 8:
                    token_ms(0)
            dve.wait_ge(s["wo_loaded"], 16)
            for t in range(YT):
                dve.tensor_scalar(w_o[:, t, :], w_o[:, t, :], mn_c[:, t:t + 1], None, ALU.mult).then_inc(s["wo_ready"], 1)


            def conv_pair(tiles, halo, taps, halo0, tap0, q):
                if q:
                    dve.wait_ge(halo, halo0)
                for n, (ch, rows, dst) in enumerate(tiles):
                    if q == 0:
                        dve.memset(raw[0:rows, n, 0:TAPS - 1], 0.0).then_inc(halo, 1)
                    else:
                        dve.tensor_copy(raw[0:rows, n, 0:TAPS - 1], tail[0:rows, ch, :]).then_inc(halo, 1)
                for k in range(TAPS - 1):
                    for n, (ch, rows, dst) in enumerate(tiles):
                        dve.wait_ge(halo, halo0 + n + 1) if k == 0 else dve.wait_ge(taps, tap0 + 2 * (k - 1) + n + 1)
                        dve.scalar_tensor_tensor(dst, raw[0:rows, n, k:k + T], cw[0:rows, ch, k:k + 1], dst,
                                                 ALU.mult, ALU.add).then_inc(taps, 1)
                for n, (ch, rows, dst) in enumerate(tiles):
                    dve.tensor_copy(tail[0:rows, ch, :], raw[0:rows, n, T:T + TAPS - 1]).then_inc(halo, 1)

            def slot(b, j):
                at = At(b, j)
                k = at.k
                new, mid, old = exists(b, j, 0), exists(b, j, 1), exists(b, j, 2)
                if new and at.st == 0:
                    for kk, bank in ((0, mb), (1, ma)):
                        dve.wait_ge(s["ht_ready"], 2 * at.i + kk + 1)
                        if not (isinstance(b, int) and k == 0):
                            dve.wait_ge(s["pj_ready"], WT * at.i)
                        dve.tensor_copy(h_hi[:, kk, :], bank[:, :]).then_inc(s["hh_done"], 1)
                        dve.wait_ge(s["hh_done"], 2 * at.i + kk + 1)
                        dve.tensor_tensor(h_lo[:, kk, :], bank[:, :], h_hi[:, kk, :].bitcast(F32), ALU.subtract
                                          ).then_inc(s["hl_done"], 1)
                if old:
                    o = At(b, j - 2)
                    dve.wait_ge(s["ds_ready"], k - 1)
                    dve.wait_ge(s["pend_done"], 2 * (k - 1))
                    if not (isinstance(b, int) and k - 2 <= 0):
                        dve.wait_ge(s["blk_done"], blk_count(b, j - 3))
                    for c in range(NC):
                        for t in range(TPS):
                            src = state[:, o.st, t, :] if c == 0 else s_ch[:, c - 1, t, :]
                            dst = state[:, o.st, t, :] if c == NC - 1 else s_ch[:, c, t, :]
                            add = ma[:, (c * TPS + t) * HD:(c * TPS + t + 1) * HD]
                            if c == NC - 1 and t == 0 and o.q:
                                dve.wait_ge(s["blk_done"], blk_count(b, j - 2) - 2)
                            if c == 0 and o.q == 0:
                                dve.tensor_copy(dst, add).then_inc(s["chain_done"], 1)
                            else:
                                if c:
                                    dve.wait_ge(s["chain_done"], 8 * (k - 2) + 2 * (c - 1) + t + 1)
                                dve.scalar_tensor_tensor(dst, src, p_end[:, t, c:c + 1], add, ALU.mult, ALU.add
                                                         ).then_inc(s["chain_done"], 1)
                if mid:
                    m = At(b, j - 1)
                    buf = m.js % 2
                    for n, bank in ((0, mb), (1, ma)):
                        dve.wait_ge(s["xt_ready"], 2 * (k - 1) + n + 1)
                        dve.tensor_tensor(
                            xdt[:, buf, 2 * n:2 * n + 2, :].rearrange("p c (h d) -> p c h d", d=HD),
                            bank[:, :].rearrange("p (c h d) -> p c h d", c=2, d=HD),
                            dt_s[:, 2 * n:2 * n + 2, HPS * m.st:HPS * (m.st + 1)].unsqueeze(3).broadcast_to([P, 2, HPS, HD]),
                            ALU.mult).then_inc(s["xdt_done"], 1)
                    for h in range(HPS):
                        dve.wait_ge(s["da_ready"], 6 * (k - 1) + h + 1)
                        dve.tensor_tensor_scan(dec[:, buf, h, :], da[h % 2][:, :], inject[:, :, :].rearrange("p c t -> p (c t)"),
                                               0.0, ALU.mult, ALU.add).then_inc(s["scan_done"], 1)
                    dve.wait_ge(s["scan_done"], 4 * (k - 1) + 4)
                    if not (isinstance(b, int) and k - 1 <= 0):
                        dve.wait_ge(s["xw_done"], k - 1)
                    dve.tensor_copy(w_end[:, :, :], dec[:, buf, :, CH - 1::CH].rearrange("p h c -> p c h")
                                    ).then_inc(s["wend_done"], 1)
                if old:
                    o = At(b, j - 2)
                    for t in range(TPS):
                        dve.wait_ge(s["y_ready"], 2 * (k - 2) + t + 1)
                        ch = TPS * o.st + t
                        dve.scalar_tensor_tensor(xc[:, o.js % 2, t, :], xc[:, o.js % 2, t, :], dpar[:, ch:ch + 1],
                                                 yp[t][:, :], ALU.mult, ALU.add).then_inc(s["skip_done"], 1)
                if mid:
                    m = At(b, j - 1)
                    for t in range(TPS):
                        dve.wait_ge(s["da_ready"], 6 * (k - 1) + HPS + t + 1)
                        dve.tensor_copy(p_end[:, t, :], da[t % 2][:, CH - 1::CH]).then_inc(s["pend_done"], 1)
                        dve.wait_ge(s["bc_ready"], 2 * m.i + 1)
                        dve.tensor_tensor(cp[:, t, :], da[t % 2][:, :], cc[:, m.q, :], ALU.mult).then_inc(s["cp_done"], 1)
                if at.st == 7 and exists(b, j, -1):
                    token_ms(at.i + 1)
                if new and at.st == 0:
                    dve.wait_ge(s["pj_taken"], tile_count(at.i, 1))
                    conv_pair([(YT, P, cc[:, at.q, :]), (YT + 1, NS, bb[:, :])], s["bc_halo"], s["bc_tap"],
                              4 * at.i, 6 * at.i, at.q)
                    dve.wait_ge(s["dtt_ready"], at.i + 1)
                    dve.tensor_tensor(u_t[:, :, :], mb[:, 0:NC * HEADS].rearrange("p (c h) -> p c h", c=NC),
                                      dtb[:, :].unsqueeze(1).broadcast_to([P, NC, HEADS]), ALU.add).then_inc(s["u_done"], 1)
                    dve.wait_ge(s["u_done"], at.i + 1)
                    dve.scalar_tensor_tensor(a_t[:, :, :], u_t[:, :, :], -1.0, u_t[:, :, :], ALU.mult, ALU.max).then_inc(s["a_done"], 1)
                if new:
                    dve.wait_ge(s["pj_taken"], tile_count(at.i, 2 + 4 * at.st + TPS + 1))
                    conv_pair([(TPS * at.st + t, P, xc[:, at.js % 2, t, :]) for t in range(TPS)],
                              s["halo_done"], s["conv_tap"], 4 * k, 6 * k, at.q)
                if new and at.st == 0:
                    i = at.i
                    c0 = 8 * i

                    def link(n, ins):
                        ins.then_inc(s["dtc"], 1)
                        dve.wait_ge(s["dtc"], c0 + n)

                    dve.wait_ge(s["l_done"], i + 1)
                    link(1, dve.tensor_scalar(m_t[:, :, :], e_t[:, :, :], 1.0, 1.0, ALU.add, ALU.is_equal))
                    dve.tensor_tensor(l_t[:, :, :], l_t[:, :, :], m_t[:, :, :], ALU.add).then_inc(s["dtc"], 1)
                    link(3, dve.tensor_scalar(a_t[:, :, :], e_t[:, :, :], 1.0, 1.0, ALU.add, ALU.subtract))
                    link(4, dve.tensor_tensor(a_t[:, :, :], a_t[:, :, :], m_t[:, :, :], ALU.add))
                    dve.tensor_tensor(l_t[:, :, :], l_t[:, :, :], e_t[:, :, :], ALU.mult).then_inc(s["dtc"], 1)
                    link(6, dve.reciprocal(m_t[:, :, :], a_t[:, :, :]))
                    link(7, dve.tensor_tensor(l_t[:, :, :], l_t[:, :, :], m_t[:, :, :], ALU.mult))
                    dve.scalar_tensor_tensor(dt_s[:, :, :], u_t[:, :, :], 0.0, l_t[:, :, :], ALU.max, ALU.add
                                             ).then_inc(s["dt_done"], 1)
                    dve.wait_ge(s["dt_done"], i + 1)
                    dve.tensor_tensor(a_t[:, :, :], dt_s[:, :, :], neg_a[:, :].unsqueeze(1).broadcast_to([P, NC, HEADS]),
                                      ALU.mult).then_inc(s["dtc"], 1)
                    dve.wait_ge(s["bt_ready"], i + 1)
                    dve.tensor_copy(b_tok[:, at.q, :, :], mb[:, 0:NC * NS].rearrange("p (c n) -> p c n", c=NC)
                                    ).then_inc(s["bt_taken"], 1)
                    dve.wait_ge(s["g_ready"], i + 1)
                    if not (isinstance(b, int) and i < 1):
                        dve.wait_ge(s["m_done"], 4 * (k - 2))
                    dve.tensor_copy(g_s[:, at.q, :, :], ma[:, :].rearrange("p (c t) -> p c t", c=NC)
                                    ).then_inc(s["g_taken"], 1)
                    dve.wait_ge(s["dat_ready"], i + 1)
                    dve.tensor_copy(tl[0:32, 0, :], mb[0:32, :]).then_inc(s["dat_taken"], 1)
                    dve.wait_ge(s["dat_taken"], 6 * i + 1)
                    for c in range(NC):
                        dve.tensor_tensor_scan(tl[0:32, 1, c * CH:(c + 1) * CH], tl[0:32, 0, c * CH:(c + 1) * CH], zero[:, :],
                                               1.0, ALU.mult, ALU.add).then_inc(s["dat_taken"], 1)
                    dve.wait_ge(s["dat_taken"], 6 * i + 5)
                    dve.memset(tl[0:32, 0, 0::CH], 0.0).then_inc(s["dat_taken"], 1)
                    dve.wait_ge(s["dat_taken"], 6 * i + 6)
                    if not (isinstance(b, int) and k == 0):
                        dve.wait_ge(s["da_ready"], 6 * k)

                    def link_part(n, ins):
                        ins.then_inc(s["parts_done"], 1)
                        dve.wait_ge(s["parts_done"], 5 * i + n)

                    link_part(1, dve.tensor_copy(parts[0:32, :, :], tl[0:32, :, :]))
                    link_part(2, dve.tensor_tensor(tl[32:64, :, :], tl[0:32, :, :], parts[0:32, :, :], ALU.subtract))
                    link_part(3, dve.tensor_copy(parts[32:64, :, :], tl[32:64, :, :]))
                    link_part(4, dve.tensor_tensor(tl[64:96, :, :], tl[32:64, :, :], parts[32:64, :, :], ALU.subtract))
                    dve.tensor_copy(parts[64:96, :, :], tl[64:96, :, :]).then_inc(s["parts_done"], 1)
                if out_slot(b, j):
                    half, i = out_slot(b, j)[1:]
                    for n, bank in ((0, mb), (1, ma)):
                        dve.wait_ge(s["o_ready"], 4 * i + 2 * half + n + 1)
                        dst = o_acc[:, 2 * n:2 * n + 2, :].rearrange("p c d -> p (c d)")
                        if half == 0:
                            dve.wait_ge(s["o_stored"], 16 * (i + 1))
                            dve.tensor_copy(dst, bank[:, :]).then_inc(s["o_taken"], 1)
                        else:
                            dve.tensor_tensor(dst, dst, bank[:, :], ALU.add).then_inc(s["o_taken"], 1)
                if at.st == 3 and exists(b, j, 4) and (not isinstance(b, int) or k >= SPI):
                    i = at.i - 1
                    dve.wait_ge(s["q_ready"], i + 1)
                    dve.tensor_scalar(o_ms[:, :], mb[:, 0:NC], 1.0 / DIN, EPS, ALU.mult, ALU.add).then_inc(s["oms_done"], 1)
                    dve.wait_ge(s["ry_done"], i + 1)
                    for c in range(NC):
                        dve.tensor_scalar(o_acc[:, c, :], o_acc[:, c, :], r_y[:, c:c + 1], None, ALU.mult
                                          ).then_inc(s["o_scaled"], 1)
                if at.st == 4 and exists(b, j, -4):
                    token_norm_a(at.i + 1)
                if at.st == 5 and exists(b, j, -3):
                    token_norm_b(at.i + 1)

            run(dve, slot)

        @block.tensor
        def _(pe):
            pe.wait_ge(s["consts"], 8)
            pe.wait_ge(s["c_silu"], 1)
            for n, bank in enumerate((ma, mb, yp[0])):
                for kk in range(KH):
                    last = pe.matmul(bank[0:BATCH, :], cs_t[:, kk, :], wm[:, kk * MOD + n * T:kk * MOD + (n + 1) * T],
                                     start=(kk == 0), stop=(kk == KH - 1))
                last.then_inc(s["mod_ready"], 1)

            def project(at, idx, b):
                if not (isinstance(b, int) and at.k == 0 and idx < 2):
                    pe.wait_ge(s["pj_taken"], tile_count(at.i, idx) - 2)
                if isinstance(b, int) and b == 0:
                    pe.wait_ge(s["w_ready"], WT if at.k == HEAD - 1 else 2 * (idx // 2 + 1))
                cols = slice(idx * P, (idx + 1) * P)
                first = True
                for kk in range(KH):
                    for w, h in ((w_hi, h_hi), (w_hi, h_lo), (w_lo, h_hi)):
                        last = pe.matmul(pj[idx % 2][:, :], w[:, kk, cols], h[:, kk, :], start=first,
                                         stop=(kk == KH - 1 and w is w_lo))
                        first = False
                last.then_inc(s["pj_ready"], 1)

            def slot(b, j):
                at = At(b, j)
                k = at.k
                new, mid, old = exists(b, j, 0), exists(b, j, 1), exists(b, j, 2)
                if isinstance(b, int) and k == HEAD - 1:
                    pe.wait_ge(s["wo_ready"], YT)
                if new and at.st == 0:
                    pe.wait_ge(s["hs_done"], 4 * at.i + 4)
                    free_banks(b, j)
                    for kk, bank in ((0, mb), (1, ma)):
                        for c in range(NC):
                            last = pe.transpose(bank[:, c * CH:(c + 1) * CH], hs[:, c, kk * P:(kk + 1) * P], ident[:, :])
                        last.then_inc(s["ht_ready"], 1)
                else:
                    free_banks(b, j)
                if old:
                    o = At(b, j - 2)
                    pe.wait_ge(s["xw_done"], k - 1)
                    pe.wait_ge(s["bt_taken"], o.i + 1)
                    if new and at.st == 0:
                        pe.wait_ge(s["hl_done"], 2 * at.i + 2)
                    for c in range(NC):
                        for half in range(2):
                            last = pe.matmul(
                                ma[64 * half:64 * half + 64, c * TPS * HD:(c + 1) * TPS * HD].rearrange("p (t d) -> p t d", d=HD),
                                b_tok[:, o.q, c, :],
                                xw[:, c, :].rearrange("p (t e d) -> p t e d", t=TPS, e=2)[:, :, half, :],
                                start=True, stop=True)
                    last.then_inc(s["ds_ready"], 1)
                if mid:
                    m = At(b, j - 1)
                    pe.wait_ge(s["x_ready"], 2 * (k - 1) + 2)
                    if new and at.st == 0:
                        pe.wait_ge(s["hl_done"], 2 * at.i + 1)
                    for n, bank in ((0, mb), (1, ma)):
                        if n == 1 and old:
                            pe.wait_ge(s["chain_done"], 8 * (k - 2) + 8)
                        for c in range(2):
                            for t in range(TPS):
                                last = pe.transpose(bank[:, (c * TPS + t) * P:(c * TPS + t + 1) * P],
                                                    xc[:, m.js % 2, t, (2 * n + c) * CH:(2 * n + c + 1) * CH], ident[:, :])
                        last.then_inc(s["xt_ready"], 1)
                if new and at.st == 0:
                    pe.wait_ge(s["hl_done"], 2 * at.i + 2)
                    project(at, 0, b)
                    project(at, 1, b)

                def spread_decay(h):
                    m = At(b, j - 1)
                    head = HPS * m.st + h
                    if h < 2:
                        if not (isinstance(b, int) and k - 1 <= 0):
                            pe.wait_ge(s["cp_done"], 2 * (k - 2) + h + 1)
                        if h == 0:
                            pe.wait_ge(s["parts_done"], 5 * (m.i + 1))
                    else:
                        pe.wait_ge(s["scan_done"], 4 * (k - 1) + h - 1)
                    for half in range(2):
                        last = pe.matmul(da[h % 2][64 * half:64 * half + 64, :], select[:, head, :], parts[:, 0, :],
                                         start=True, stop=True)
                    last.then_inc(s["da_ready"], 1)

                if mid:
                    spread_decay(0)
                    spread_decay(1)
                if new:
                    project(at, 2 + 4 * at.st, b)
                    project(at, 3 + 4 * at.st, b)
                if new and at.st == 0:
                    pe.wait_ge(s["dt_copied"], at.i + 1)
                    if mid:
                        wait_apart(pe, s["xdt_done"], 2 * (k - 1) + 1)
                    else:
                        pe.wait_ge(s["hl_done"], 2 * at.i + 2)
                    for c in range(NC):
                        last = pe.transpose(mb[:, c * HEADS:(c + 1) * HEADS], tl[64:96, 0, c * CH:(c + 1) * CH],
                                            ident[64:96, 64:96])
                    last.then_inc(s["dtt_ready"], 1)
                if mid:
                    spread_decay(2)
                    spread_decay(3)
                if old:
                    o = At(b, j - 2)
                    buf = o.js % 2
                    pe.wait_ge(s["m_done"], 4 * (k - 2) + 4)
                    pe.wait_ge(s["blk_done"], blk_count(b, j - 2))
                    pe.wait_ge(s["cp_done"], 2 * (k - 2) + 2)
                    for t in range(TPS):
                        if not (isinstance(b, int) and k - 2 <= 0):
                            pe.wait_ge(s["skip_done"], 2 * (k - 3) + t + 1)
                        for c in range(NC):
                            for half in range(2):
                                h = 2 * t + half
                                pe.matmul(yp[t][64 * half:64 * half + 64, c * CH:(c + 1) * CH],
                                          xdt[:, buf, c, h * HD:(h + 1) * HD], dec[:, buf, h, c * CH:(c + 1) * CH],
                                          start=(c == 0), stop=False, skip_group_check=True)
                        for c in range(1 if o.q == 0 else 0, NC):
                            last = pe.matmul(yp[t][:, c * CH:(c + 1) * CH], s_blk[:, c, t, :], cp[:, t, c * CH:(c + 1) * CH],
                                             start=False, stop=True, skip_group_check=True)
                        last.then_inc(s["y_ready"], 1)
                if mid:
                    m = At(b, j - 1)
                    for t in range(TPS):
                        pe.wait_ge(s["scan_done"], 4 * (k - 1) + HPS - 1 + t)
                        pair = select[:, HPS * m.st + 2 * t:HPS * m.st + 2 * t + 2, :].rearrange("p h n -> p (h n)")
                        pe.matmul(da[t % 2][:, :], pair, parts[:, 1, :], start=True, stop=True
                                  ).then_inc(s["da_ready"], 1)
                if new:
                    project(at, 4 + 4 * at.st, b)
                    project(at, 5 + 4 * at.st, b)
                if new and at.st == 0:
                    i = at.i
                    wait_apart(pe, s["bc_ready"], 2 * i + 2)
                    pe.wait_ge(s["u_done"], i + 1)
                    for c in range(NC):
                        last = pe.transpose(mb[:, c * NS:(c + 1) * NS], bb[:, c * CH:(c + 1) * CH], ident[0:NS, 0:NS])
                    last.then_inc(s["bt_ready"], 1)
                    if mid:
                        pe.wait_ge(s["xdt_done"], 2 * (k - 1) + 2)
                    for c in range(NC):
                        last = pe.matmul(ma[:, c * CH:(c + 1) * CH], bb[:, c * CH:(c + 1) * CH],
                                         cc[0:NS, at.q, c * CH:(c + 1) * CH], start=True, stop=True)
                    last.then_inc(s["g_ready"], 1)
                    pe.wait_ge(s["da_exp"], i + 1)
                    pe.wait_ge(s["bt_taken"], i + 1)
                    for c in range(NC):
                        last = pe.transpose(mb[0:HEADS, c * CH:(c + 1) * CH], a_t[:, c, :], ident[:, :])
                    last.then_inc(s["dat_ready"], 1)
                if out_slot(b, j):
                    half, i = out_slot(b, j)[1:]
                    pe.wait_ge(s["gate_done"], 2 * SPI * i + SPI * (half + 1))
                    for n, bank in ((0, mb), (1, ma)):
                        if mid:
                            pe.wait_ge(s["xdt_done"], 2 * (k - 1) + n + 1)
                        for c in range(2):
                            for t in range(YT // 2):
                                tt = YT // 2 * half + t
                                last = pe.matmul(bank[:, c * HID:(c + 1) * HID], yb[:, tt, (2 * n + c) * CH:(2 * n + c + 1) * CH],
                                                 w_o[:, tt, :], start=(t == 0), stop=(t == YT // 2 - 1))
                        last.then_inc(s["o_ready"], 1)
                if at.st == 3 and exists(b, j, 4) and (not isinstance(b, int) or k >= SPI):
                    i = at.i - 1
                    pe.wait_ge(s["acc_done"], 2 * SPI * (i + 1))
                    if mid:
                        pe.wait_ge(s["xdt_done"], 2 * (k - 1) + 1)
                    pe.wait_ge(s["o_taken"], 4 * i + 4)
                    for c in range(NC):
                        last = pe.matmul(mb[:, c:c + 1], acc[:, c * CH:(c + 1) * CH], ones[:, :], start=True, stop=True)
                    last.then_inc(s["q_ready"], 1)

            def free_banks(b, j):
                at = At(b, j)
                if isinstance(b, int) and at.k == 0:
                    pe.wait_ge(s["mod_fix"], 3)
                    return
                p = At(b, j - 1)
                if exists(b, j - 1, 1):
                    pe.wait_ge(s["xdt_done"], 2 * (at.k - 1))
                if exists(b, j - 1, 2):
                    pe.wait_ge(s["chain_done"], 8 * (at.k - 2))
                if p.st == 0 and exists(b, j, 1):
                    pe.wait_ge(s["g_taken"], p.i + 1)
                    pe.wait_ge(s["dat_taken"], 6 * p.i + 1)
                if out_slot(b, j - 1):
                    half, i = out_slot(b, j - 1)[1:]
                    pe.wait_ge(s["o_taken"], 4 * i + 2 * half + 2)
                if p.st == 3 and exists(b, j - 1, 4) and (not isinstance(b, int) or p.k >= SPI):
                    pe.wait_ge(s["oms_done"], p.i)

            run(pe, slot)


def mlp_phase(nc, x, w_up, w_dn, ln2, w_ff, rram, h_dram, o_dram, mod_dram, out):
    ctx = ExitStack()
    with ctx:
        def sb(name, shape, dt=F32):
            return ctx.enter_context(nc.sbuf_tensor(name, shape, dt))

        def pb(name):
            return ctx.enter_context(nc.psum_tensor(name, [P, T], F32))

        KI = INTER // P

        ident = sb("ident2", [P, P])
        neg_half = sb("neg_half2", [P, NC])
        wu_hi = sb("wu_hi", [P, KH, 2 * INTER], F32R)
        wu_lo = sb("wu_lo", [P, KH, 2 * INTER], F32R)
        wd_hi = sb("wd_hi", [P, KI, HID], F32R)
        wd_lo = sb("wd_lo", [P, KI, HID], F32R)
        wf_hi = sb("wf_hi", [P, KH, HID], F32R)
        wf_lo = sb("wf_lo", [P, KH, HID], F32R)
        wu_st = sb("wu_st", [P, 2, KH, T])
        wd_st = sb("wd_st", [P, KI, HID])
        wf_st = sb("wf_st", [P, KH, HID])
        rr_st = sb("rr_st", [P, KH, HID])
        wf_a = sb("wf_a", [P, KH, HID])
        wf_b = sb("wf_b", [P, KH, HID])
        ln2_c = sb("ln2_c", [P, KH])
        rows = sb("rows", [P, 2, HID])
        cols = sb("cols", [P, BATCH, 2 * KH])
        x1 = sb("x1", [P, 2, NC, HID])
        hb = sb("hb", [P, NC, HID])
        xb = sb("xb", [P, 2, NC, HID])
        x1r = sb("x1r", [P, NC, HID])
        ssq = sb("ssq2", [P, NC])
        ms = sb("ms2", [P, NC])
        r2 = sb("r2", [P, NC])
        t_hi = sb("t_hi", [P, KH, T], F32R)
        t_lo = sb("t_lo", [P, KH, T], F32R)
        gate = sb("gate", [P, 2, T])
        mid = sb("mid", [P, 2, T])
        m_hi = sb("m_hi", [P, KI, T], F32R)
        m_lo = sb("m_lo", [P, KI, T], F32R)
        a_s = sb("a_s", [P, NC, HID])
        xn = sb("xn", [P, NC, HID])
        stats = sb("stats2", [P, NC, 6])
        mv = sb("mv2", [P, NC, 2])
        ve = sb("ve2", [P, NC])
        rstd = sb("rstd2", [P, NC])
        h2 = sb("h2", [P, KH, T])
        qn = sb("qn", [P, KH, T])
        q_t = sb("q_t", [P, KH, T], F32R)
        f_s = sb("f_s", [P, NC, HID])
        cg = [pb(f"cg{n}") for n in range(2)]
        cu = [pb(f"cu{n}") for n in range(2)]
        mo = [pb(f"mo{n}") for n in range(2)]
        mi = [pb(f"mi{n}") for n in range(2)]

        s = {n: ctx.enter_context(nc.semaphore("m_" + n)) for n in (
            "const_set consts small_loaded wu_loaded0 wu_loaded1 wd_loaded wf_loaded wu_head wu_ready wd_head "
            "wd_ready wf_step wf_ready o_loaded h_loaded x_loaded row_loaded x1_done ssq_done ms_done r2_done "
            "x1r_done bt_ready t_head t_ready c_ready gate_done mid_done head_done rest_done mo_ready a_done "
            "ga_done x2_done bn_done ve_done rstd_done xn_done dt_ready h2_done q_part q_done ff_ready f_done "
            "out_done out_stored").split()}
        block = ctx.enter_context(nc.Block())

        def run(eng, slot):
            slot(0, 0, 0)
            with eng.Fori(0, BATCH - 1) as b:
                for j in range(1, 1 + IPB):
                    slot(IPB * b + j, j, b)
            for j in range(1, 1 + IPB):
                slot(IPB * (BATCH - 1) + j, j, BATCH - 1)

        def known(i):
            return isinstance(i, int)

        def has(i):
            return not known(i) or 0 <= i < NI

        @block.sync
        def _(sp):
            def tokens(dram, i):
                return dram[bass.ds(i * T, T), :].rearrange("(c p) n -> p c n", p=P)

            def load_block(i, j):
                sp.dma_start(x1[:, j % 2, :, :], tokens(o_dram, i)).then_inc(s["o_loaded"], 16)
                sp.dma_start(hb[:, :, :], tokens(h_dram, i)).then_inc(s["h_loaded"], 16)

            def load_x(i, j):
                sp.dma_start(xb[:, j % 2, :, :], tokens(x, i)).then_inc(s["x_loaded"], 16)

            def load_rows(row):
                both = mod_dram.rearrange("b (g m n) -> b g m n", g=2, m=3)[bass.ds(row, 1), :, 2, :]
                sp.dma_start(rows[:, :, :], both.broadcast_to([P, 2, HID])).then_inc(s["row_loaded"], 16)

            sp.dma_start(ln2_c[:, :], ln2).then_inc(s["small_loaded"], 16)
            load_block(0, 0)
            load_x(0, 0)
            for bb in range(BATCH):
                for m, o in enumerate((3, 4)):
                    with nc.allow_non_contiguous_dma(reason="a few hundred numbers, once"):
                        sp.dma_start(cols[:, bb, m * KH:(m + 1) * KH],
                                     mod_dram[bb:bb + 1, o * HID:(o + 1) * HID].rearrange("b (k p) -> p (b k)", p=P)
                                     ).then_inc(s["small_loaded"], 16)
            for n in range(2 * INTER // T):
                if n >= 2:
                    sp.wait_ge(s["wu_ready"], KH * (n - 1))
                sp.dma_start(wu_st[:, n % 2, :, :], w_up.rearrange("(k p) n -> p k n", p=P)[:, :, n * T:(n + 1) * T]
                             ).then_inc(s[f"wu_loaded{n % 2}"], 16)
            sp.dma_start(wd_st[:, :, :], w_dn.rearrange("(k p) n -> p k n", p=P)).then_inc(s["wd_loaded"], 16)
            sp.dma_start(wf_st[:, :, :], w_ff.rearrange("(k p) n -> p k n", p=P)).then_inc(s["wf_loaded"], 16)
            sp.dma_start(rr_st[:, :, :], rram.rearrange("(k p) n -> p k n", p=P)).then_inc(s["wf_loaded"], 16)
            load_rows(0)

            def slot(i, j, row):
                new, nxt, old = has(i), has(i + 1), has(i - 1)
                if nxt:
                    if old:
                        wait_apart(sp, s["a_done"], 2 * i)
                    sp.wait_ge(s["x1_done"], i + 1)
                    load_block(i + 1, j + 1)
                if old:
                    sp.wait_ge(s["out_done"], i)
                    sp.dma_start(tokens(out, i - 1), a_s[:, :, :]).then_inc(s["out_stored"], 16)
                if nxt:
                    load_x(i + 1, j + 1)
                if old and new and j == IPB:
                    load_rows(row + 1)

            sp.sem_inc(s["out_stored"], 16)
            run(sp, slot)
            sp.wait_ge(s["out_stored"], 16 * (NI + 1))
            sp.wait_ge(s["row_loaded"], 16 * BATCH)

        @block.gpsimd
        def _(pool):
            pool.memset(ident[:, :], 0.0).then_inc(s["const_set"], 1)
            pool.memset(neg_half[:, :], -0.5).then_inc(s["consts"], 1)
            pool.wait_ge(s["const_set"], 1)
            pool.affine_select(out=ident[:, :], in_=ident[:, :], compare_op=ALU.not_equal, fill=1.0, base=0,
                               pattern=[[-1, P]], channel_multiplier=1).then_inc(s["consts"], 1)
            pool.wait_ge(s["consts"], 2)

            def residual(i, j):
                pool.wait_ge(s["o_loaded"], 16 * (i + 1))
                pool.wait_ge(s["h_loaded"], 16 * (i + 1))
                pool.tensor_tensor(x1[:, j % 2, :, :], x1[:, j % 2, :, :], hb[:, :, :], ALU.add).then_inc(s["x1_done"], 1)

            def rms_power(i):
                pool.wait_ge(s["ms_done"], i + 1)
                pool.tensor_tensor(r2[:, :], ms[:, :], neg_half[:, :], ALU.pow).then_inc(s["r2_done"], 1)

            residual(0, 0)
            rms_power(0)

            def slot(i, j, row):
                old = has(i - 1)
                if old:
                    p = (j - 1) % 2
                    pool.wait_ge(s["a_done"], 2 * i)
                    pool.wait_ge(s["row_loaded"], 16 * (row + 1))
                    pool.tensor_tensor(a_s[:, :, :], a_s[:, :, :], rows[:, 0:1, :].broadcast_to([P, NC, HID]), ALU.mult
                                       ).then_inc(s["ga_done"], 1)
                    pool.wait_ge(s["ga_done"], i)
                    pool.wait_ge(s["x_loaded"], 16 * i)
                    pool.tensor_tensor(xb[:, p, :, :], xb[:, p, :, :], a_s[:, :, :], ALU.add).then_inc(s["x2_done"], 1)
                    pool.wait_ge(s["ve_done"], i)
                    pool.tensor_tensor(rstd[:, :], ve[:, :], neg_half[:, :], ALU.pow).then_inc(s["rstd_done"], 1)
                if has(i + 1):
                    residual(i + 1, j + 1)
                    rms_power(i + 1)
                if old:
                    pool.wait_ge(s["f_done"], 2 * i)
                    pool.tensor_tensor(a_s[:, :, :], xb[:, p, :, :], f_s[:, :, :], ALU.add).then_inc(s["out_done"], 1)

            run(pool, slot)

        @block.scalar
        def _(act):
            def squares(i, j):
                act.wait_ge(s["x1_done"], i + 1)
                if j:
                    act.wait_ge(s["bt_ready"], 2 * i)
                for c in range(NC):
                    act.activation(x1r[:, c, :], x1[:, j % 2, c, :], ACT.Square, accum_out=ssq[:, c:c + 1]
                                   ).then_inc(s["ssq_done"], 1)

            def scale(i, j):
                act.wait_ge(s["r2_done"], i + 1)
                act.wait_ge(s["ssq_done"], 4 * i + 4)
                for c in range(NC):
                    act.activation(x1r[:, c, :], x1[:, j % 2, c, :], ACT.Copy, scale=r2[:, c:c + 1]
                                   ).then_inc(s["x1r_done"], 1)

            squares(0, 0)
            scale(0, 0)
            act.wait_ge(s["small_loaded"], 16 * 9)

            def slot(i, j, row):
                new = has(i)
                for t in range(KI):
                    if new:
                        n = KI * i + t
                        act.wait_ge(s["c_ready"], 2 * n + 1)
                        if t >= 2 or j:
                            act.wait_ge(s["mid_done"], n - 1)
                        act.activation(gate[:, t % 2, :], cg[t % 2][:, :], ACT.Silu).then_inc(s["gate_done"], 1)
                        act.wait_ge(s["mid_done"], n + 1)
                        if t == 0 and j:
                            act.wait_ge(s["mo_ready"], 2 * i)
                        act.activation(m_hi[:, t, :], mid[:, t % 2, :], ACT.Copy).then_inc(s["head_done"], 1)
                    if t == 2 and has(i + 1):
                        squares(i + 1, j + 1)
                    if t == 4 and has(i - 1):
                        for kk in range(KH):
                            wait_apart(act, s["dt_ready"], 2 * (i - 1) + kk + 1)
                            at = cols[:, bass.ds(row, 1), :].rearrange("p b k -> p (b k)")
                            act.activation(h2[:, kk, :], mi[kk][:, :], ACT.Identity, bias=at[:, kk:kk + 1],
                                           scale=at[:, KH + kk:KH + kk + 1]).then_inc(s["h2_done"], 1)
                    if t == 5 and has(i + 1):
                        scale(i + 1, j + 1)

            run(act, slot)

        @block.vector
        def _(dve):
            def mean_square(i):
                dve.wait_ge(s["ssq_done"], 4 * i + 4)
                dve.tensor_scalar(ms[:, :], ssq[:, :], 1.0 / HID, EPS, ALU.mult, ALU.add).then_inc(s["ms_done"], 1)

            mean_square(0)
            dve.wait_ge(s["small_loaded"], 16 * 9)
            for n in range(2 * INTER // T):
                dve.wait_ge(s[f"wu_loaded{n % 2}"], 16 * (n // 2 + 1))
                cut = slice(n * T, (n + 1) * T)
                for kk in range(KH):
                    dve.tensor_scalar(wu_hi[:, kk, cut], wu_st[:, n % 2, kk, :], ln2_c[:, kk:kk + 1], None, ALU.mult
                                      ).then_inc(s["wu_head"], 1)
                for kk in range(KH):
                    dve.wait_ge(s["wu_head"], KH * n + kk + 1)
                    dve.scalar_tensor_tensor(wu_lo[:, kk, cut], wu_st[:, n % 2, kk, :], ln2_c[:, kk:kk + 1],
                                             wu_hi[:, kk, cut].bitcast(F32), ALU.mult, ALU.subtract
                                             ).then_inc(s["wu_ready"], 1)
            dve.wait_ge(s["wd_loaded"], 16)
            dve.tensor_copy(wd_hi[:, :, :], wd_st[:, :, :]).then_inc(s["wd_head"], 1)
            dve.wait_ge(s["wd_head"], 1)
            dve.tensor_tensor(wd_lo[:, :, :], wd_st[:, :, :], wd_hi[:, :, :].bitcast(F32), ALU.subtract
                              ).then_inc(s["wd_ready"], 1)
            dve.wait_ge(s["wf_loaded"], 32)
            dve.tensor_scalar(wf_a[:, :, :], wf_st[:, :, :], THW, SCW, ALU.is_gt, ALU.mult).then_inc(s["wf_step"], 1)
            dve.tensor_scalar(wf_b[:, :, :], wf_st[:, :, :], -THW, SCW, ALU.is_lt, ALU.mult).then_inc(s["wf_step"], 1)
            dve.wait_ge(s["wf_step"], 2)
            dve.tensor_tensor(wf_a[:, :, :], wf_a[:, :, :], wf_b[:, :, :], ALU.subtract).then_inc(s["wf_step"], 1)
            dve.wait_ge(s["wf_step"], 3)
            dve.tensor_tensor(wf_a[:, :, :], wf_a[:, :, :], rr_st[:, :, :], ALU.add).then_inc(s["wf_step"], 1)
            dve.wait_ge(s["wf_step"], 4)
            dve.tensor_copy(wf_hi[:, :, :], wf_a[:, :, :]).then_inc(s["wf_step"], 1)
            dve.wait_ge(s["wf_step"], 5)
            dve.tensor_tensor(wf_lo[:, :, :], wf_a[:, :, :], wf_hi[:, :, :].bitcast(F32), ALU.subtract
                              ).then_inc(s["wf_ready"], 1)

            def split_tokens(i):
                for kk in range(KH):
                    dve.wait_ge(s["bt_ready"], 2 * i + kk + 1)
                    dve.tensor_copy(t_hi[:, kk, :], mi[kk][:, :]).then_inc(s["t_head"], 1)
                    dve.wait_ge(s["t_head"], 2 * i + kk + 1)
                    dve.tensor_tensor(t_lo[:, kk, :], mi[kk][:, :], t_hi[:, kk, :].bitcast(F32), ALU.subtract
                                      ).then_inc(s["t_ready"], 1)

            split_tokens(0)

            def slot(i, j, row):
                new, old = has(i), has(i - 1)
                if old:
                    p = (j - 1) % 2
                    for n in range(2):
                        dve.wait_ge(s["mo_ready"], 2 * (i - 1) + n + 1)
                        dve.wait_ge(s["out_stored"], 16 * i)
                        dve.tensor_tensor(a_s[:, 2 * n:2 * n + 2, :].rearrange("p c d -> p (c d)"),
                                          mo[n][:, :], x1[:, p, 2 * n:2 * n + 2, :].rearrange("p c d -> p (c d)"), ALU.add
                                          ).then_inc(s["a_done"], 1)
                for t in range(KI):
                    if new:
                        n = KI * i + t
                        dve.wait_ge(s["c_ready"], 2 * n + 2)
                        dve.wait_ge(s["gate_done"], n + 1)
                        if t >= 2 or j:
                            dve.wait_ge(s["rest_done"], n - 1)
                        dve.tensor_tensor(mid[:, t % 2, :], cu[t % 2][:, :], gate[:, t % 2, :], ALU.mult
                                          ).then_inc(s["mid_done"], 1)
                        if t:
                            rest(i, n - 1, t - 1)
                    if t == 1 and old:
                        dve.wait_ge(s["x2_done"], i)
                        for c in range(NC):
                            dve.bn_stats(stats[:, c, :], xb[:, p, c, :]).then_inc(s["bn_done"], 1)
                        wait_apart(dve, s["bn_done"], 8 * (i - 1) + 4)
                        for c in range(NC):
                            dve.bn_aggr(mv[:, c, :], stats[:, c, :]).then_inc(s["bn_done"], 1)
                        dve.wait_ge(s["bn_done"], 8 * i)
                        dve.tensor_scalar(ve[:, :], mv[:, :, 1], EPS, None, ALU.add).then_inc(s["ve_done"], 1)
                    if t == 3 and old:
                        dve.wait_ge(s["rstd_done"], i)
                        for c in range(NC):
                            dve.tensor_scalar(xn[:, c, :], xb[:, p, c, :], mv[:, c, 0:1], rstd[:, c:c + 1],
                                              ALU.subtract, ALU.mult).then_inc(s["xn_done"], 1)
                    if t == 3 and has(i + 1):
                        mean_square(i + 1)
                    if t == 5 and old:
                        dve.wait_ge(s["h2_done"], 2 * i)
                        dve.tensor_scalar(qn[:, :, :], h2[:, :, :], -THX, SCX, ALU.is_lt, ALU.mult).then_inc(s["q_part"], 1)
                        dve.tensor_scalar(h2[:, :, :], h2[:, :, :], THX, SCX, ALU.is_gt, ALU.mult).then_inc(s["q_part"], 1)
                        dve.wait_ge(s["q_part"], 2 * i)
                        dve.tensor_tensor(q_t[:, :, :], h2[:, :, :], qn[:, :, :], ALU.subtract).then_inc(s["q_done"], 1)
                if new:
                    rest(i, KI * i + KI - 1, KI - 1)
                if old:
                    for n in range(2):
                        dve.wait_ge(s["ff_ready"], 2 * (i - 1) + n + 1)
                        dve.tensor_tensor(f_s[:, 2 * n:2 * n + 2, :], mi[n][:, :].rearrange("p (c d) -> p c d", c=2),
                                          rows[:, 1:2, :].broadcast_to([P, 2, HID]), ALU.mult).then_inc(s["f_done"], 1)
                if has(i + 1):
                    split_tokens(i + 1)

            def rest(i, n, t):
                dve.wait_ge(s["head_done"], n + 1)
                dve.tensor_tensor(m_lo[:, t, :], mid[:, t % 2, :], m_hi[:, t, :].bitcast(F32), ALU.subtract
                                  ).then_inc(s["rest_done"], 1)

            run(dve, slot)

        @block.tensor
        def _(pe):
            pe.wait_ge(s["consts"], 2)

            def transpose_tokens(i):
                pe.wait_ge(s["x1r_done"], 4 * i + 4)
                for kk in range(KH):
                    for c in range(NC):
                        last = pe.transpose(mi[kk][:, c * CH:(c + 1) * CH], x1r[:, c, kk * P:(kk + 1) * P], ident[:, :])
                    last.then_inc(s["bt_ready"], 1)

            transpose_tokens(0)

            def slot(i, j, row):
                new, old = has(i), has(i - 1)
                for t in range(KI):
                    if new:
                        n = KI * i + t
                        if t == 0:
                            if j == 0:
                                pe.wait_ge(s["wu_ready"], KH * 2 * INTER // T)
                            pe.wait_ge(s["t_ready"], 2 * i + 2)
                        for bank, half in ((cg[t % 2], 0), (cu[t % 2], 1)):
                            if t >= 2 or j:
                                pe.wait_ge(s["mid_done" if half else "gate_done"], n - 1)
                            cut = slice((half * KI + t) * P, (half * KI + t + 1) * P)
                            first = True
                            for kk in range(KH):
                                for w, h in ((wu_hi, t_hi), (wu_hi, t_lo), (wu_lo, t_hi)):
                                    last = pe.matmul(bank[:, :], w[:, kk, cut], h[:, kk, :], start=first,
                                                     stop=(kk == KH - 1 and w is wu_lo))
                                    first = False
                            last.then_inc(s["c_ready"], 1)
                    if t == 4 and old:
                        pe.wait_ge(s["xn_done"], 4 * i)
                        for kk in range(KH):
                            for c in range(NC):
                                last = pe.transpose(mi[kk][:, c * CH:(c + 1) * CH], xn[:, c, kk * P:(kk + 1) * P], ident[:, :])
                            last.then_inc(s["dt_ready"], 1)
                if j == 0:
                    pe.wait_ge(s["wd_ready"], 1)
                    pe.wait_ge(s["wf_ready"], 1)
                if old:
                    pe.wait_ge(s["q_done"], i)
                    for n in range(2):
                        for c in range(2):
                            first = True
                            cut = slice((2 * n + c) * CH, (2 * n + c + 1) * CH)
                            for kk in range(KH):
                                for w in (wf_hi, wf_lo):
                                    last = pe.matmul(mi[n][:, c * HID:(c + 1) * HID], q_t[:, kk, cut], w[:, kk, :],
                                                     start=first, stop=(kk == KH - 1 and w is wf_lo))
                                    first = False
                        last.then_inc(s["ff_ready"], 1)
                if has(i + 1):
                    if old:
                        pe.wait_ge(s["f_done"], 2 * i)
                    else:
                        pe.wait_ge(s["t_ready"], 2)
                    transpose_tokens(i + 1)
                if new:
                    pe.wait_ge(s["rest_done"], KI * (i + 1))
                    if j:
                        pe.wait_ge(s["a_done"], 2 * i)
                    for n in range(2):
                        for c in range(2):
                            first = True
                            cut = slice((2 * n + c) * CH, (2 * n + c + 1) * CH)
                            for t in range(KI):
                                for m, w in ((m_hi, wd_hi), (m_hi, wd_lo), (m_lo, wd_hi)):
                                    last = pe.matmul(mo[n][:, c * HID:(c + 1) * HID], m[:, t, cut], w[:, t, :],
                                                     start=first, stop=(t == KI - 1 and m is m_lo))
                                    first = False
                        last.then_inc(s["mo_ready"], 1)

            run(pe, slot)


def adaln_mamba_block(nc, x, w_in, ln1, conv_w, conv_b, a_log, d_par, dt_bias, w_out, mnorm, c_t, w_mod,
                      w_up, w_dn, ln2, w_ff, rram, out):
    h_dram = nc.dram_tensor("h_scratch", [BATCH * SEQ, HID], F32).ap()
    o_dram = nc.dram_tensor("o_scratch", [BATCH * SEQ, HID], F32).ap()
    mod_dram = nc.dram_tensor("mod_scratch", [BATCH, MOD], F32).ap()
    mamba_phase(nc, x, w_in, ln1, conv_w, conv_b, a_log, d_par, dt_bias, w_out, mnorm, c_t, w_mod,
                h_dram, o_dram, mod_dram)
    mlp_phase(nc, x, w_up, w_dn, ln2, w_ff, rram, h_dram, o_dram, mod_dram, out)


def kernel(**inputs):
    import numpy as np
    import concourse.bacc as bacc
    from concourse.bass_utils import run_bass_kernel_spmd

    a = {name: np.asarray(value) for name, value in inputs.items()}

    def by_channel(v):
        return v.reshape((-1, P) + v.shape[1:]).swapaxes(0, 1)

    z0, x0, b0 = 0, DIN, 2 * DIN
    b_rows, c_rows, dt_rows = b0 + np.arange(NS), b0 + NS + np.arange(NS), b0 + 2 * NS + np.arange(HEADS)
    order = [c_rows, c_rows, b_rows, dt_rows, dt_rows]
    for st in range(SPI):
        step = np.arange(TPS * P) + TPS * P * st
        order += [z0 + step, x0 + step]
    order = np.concatenate(order)
    conv = np.concatenate([np.arange(DIN), c_rows - DIN, c_rows - DIN, b_rows - DIN, b_rows - DIN])
    arrays = dict(
        x=a["L0_attn_x"].reshape(BATCH * SEQ, HID),
        w_in=a["L0_attn_in_proj_w"][order].T,
        ln1=by_channel(a["L0_attn_ln1_w"]),
        conv_w=by_channel(a["L0_attn_conv_w"].reshape(-1, TAPS)[conv]),
        conv_b=by_channel(a["L0_attn_conv_b"][conv]),
        a_log=a["L0_attn_A_log"][None],
        d_par=by_channel(np.repeat(a["L0_attn_D_param"], HD)),
        dt_bias=a["L0_attn_dt_bias"][None],
        w_out=a["L0_attn_out_proj_w"].T,
        mnorm=by_channel(a["L0_attn_mnorm_w"]),
        c_t=by_channel(a["L0_c"].T),
        w_mod=a["L0_wmod"],
        w_up=a["L0_attn_mlp_in_w"].T,
        w_dn=a["L0_attn_mlp_out_w"].T,
        ln2=by_channel(a["L0_attn_ln2_w"]),
        w_ff=a["L0_ffn_weight"].T,
        rram=a["L0_ffn_rram_variation"].T,
    )
    arrays = {name: np.ascontiguousarray(v) for name, v in arrays.items()}
    nc = bacc.Bacc("TRN2", target_bir_lowering=False, num_devices=1, dynamic_dma_scratch_size=1024)
    args = [nc.dram_tensor(name, v.shape, F32, kind="ExternalInput").ap() for name, v in arrays.items()]
    out = nc.dram_tensor("out", (BATCH * SEQ, HID), F32, kind="ExternalOutput").ap()
    adaln_mamba_block(nc, *args, out)
    r = run_bass_kernel_spmd(nc, [arrays], core_ids=[0])
    return r.results[0]["out"].reshape(BATCH, SEQ, HID)
```

```python
from contextlib import ExitStack

import concourse.bass as bass
from concourse import mybir

F32 = mybir.dt.float32
F32R = mybir.dt.float32r
BF16 = mybir.dt.bfloat16
ALU = mybir.AluOpType
ACT = mybir.ActivationFunctionType

P = 128
HID = 256
KH = HID // P
BATCH, SEQ = 4, 1024
HEADS, HD, NS = 32, 64, 64
DIN = HEADS * HD
TAPS = 4
INTER = 1024
EPS = 1e-5
T = 512
CH = 128
NC = T // CH
IPB = SEQ // T
NI = BATCH * IPB
YT = DIN // P
TPS = 2
HPS = 2 * TPS
SPI = YT // TPS
SPB = SPI * IPB
NSTEP = SPB * BATCH
WT = 2 + 2 * YT
MOD = 6 * HID
THX, SCX, THW, SCW = 0.33, 0.5, 0.2, 0.6


def wait(eng, sem, value):
    if isinstance(value, int) and value <= 0:
        return
    eng.wait_ge(sem, value)


def wait_apart(eng, sem, value):
    if not isinstance(value, int):
        value = eng.to_reg(value)
        eng.wait_ge(sem, 1)
    eng.wait_ge(sem, value)


def mamba_phase(nc, x, w_in, ln1, conv_w, conv_b, a_log, d_par, dt_bias, w_out, mnorm, c_t, w_mod,
                h_dram, o_dram, mod_dram):
    ctx = ExitStack()
    with ctx:
        def sb(name, shape, dt=F32):
            return ctx.enter_context(nc.sbuf_tensor(name, shape, dt))

        def sem(name):
            return ctx.enter_context(nc.semaphore(name))

        inject = sb("inject", [P, NC, CH])
        ident = inject[:, 0, :]
        select = sb("select", [96, HEADS, P // 2], BF16)
        ones = sb("ones", [P, 1])
        neg_half = sb("neg_half", [P, NC])
        w_hi = sb("w_hi", [P, KH, WT * P], F32R)
        w_lo = sb("w_lo", [P, KH, WT * P], F32R)
        w_o = sb("w_o", [P, YT, HID])
        ln1_c = sb("ln1_c", [P, KH])
        mn_c = sb("mn_c", [P, YT])
        cw = sb("cw", [P, YT + 2, TAPS])
        cb = sb("cb", [P, YT + 2])
        dpar = sb("dpar", [P, YT])
        dtb = sb("dtb", [P, HEADS])
        neg_a = sb("neg_a", [P, HEADS])
        cs_t = sb("cs_t", [P, KH, BATCH])
        mod_row = sb("mod_row", [P, 2, HID])
        xt = sb("xt", [P, NC, HID])
        hs = sb("hs", [P, NC, HID])
        stats = sb("stats", [P, NC, 6])
        mv = sb("mv", [P, NC, 2])
        ve = sb("ve", [P, NC])
        rstd = sb("rstd", [P, NC])
        ssq = sb("ssq", [P, NC])
        ms = sb("ms", [P, NC])
        r1 = sb("r1", [P, NC])
        h_hi = sb("h_hi", [P, KH, T], F32R)
        h_lo = sb("h_lo", [P, KH, T], F32R)
        raw = sb("raw", [P, 2, TAPS - 1 + T])
        tail = sb("tail", [P, YT + 2, TAPS - 1])
        xc = sb("xc", [P, 2, TPS, T])
        cc = sb("cc", [P, 2, T])
        bb = sb("bb", [NS, T])
        u_t = hs[:, :, 0 * HEADS:1 * HEADS]
        a_t = hs[:, :, 1 * HEADS:2 * HEADS]
        e_t = hs[:, :, 2 * HEADS:3 * HEADS]
        l_t = hs[:, :, 3 * HEADS:4 * HEADS]
        m_t = hs[:, :, 4 * HEADS:5 * HEADS]
        dt_s = sb("dt_s", [P, 2, NC, HEADS])
        tl = sb("tl", [96, 2, T])
        zero = sb("zero", [HEADS, CH])
        parts = sb("parts", [96, 2, T], BF16)
        g_s = sb("g_s", [P, 2, NC, CH])
        b_tok = sb("b_tok", [P, 2, NC, NS])
        xdt = sb("xdt", [P, 2, NC, TPS * P])
        xw = sb("xw", [P, NC, TPS * P])
        dec = sb("dec", [P, 2, HPS, T])
        w_end = sb("w_end", [P, NC, HPS])
        p_end = sb("p_end", [P, TPS, NC])
        cp = sb("cp", [P, TPS, T])
        state = sb("state", [P, SPI, TPS, HD])
        s_ch = sb("s_ch", [P, NC - 1, TPS, HD])
        s_blk = sb("s_blk", [P, NC, TPS, P])
        yb = sb("yb", [P, YT, T])
        sq = sb("sq", [P, T])
        acc = sb("acc", [P, T])
        o_acc = sb("o_acc", [P, NC, HID])
        o_ms = sb("o_ms", [P, NC])
        r_y = sb("r_y", [P, NC])
        w_stage = dec[:, :, :, :].rearrange("p a h t -> p (a h t)")
        wm = yb[:, 0:KH * MOD // T, :].rearrange("p a t -> p (a t)")
        mod_s = yb[0:BATCH, 8:11, :].rearrange("p a t -> p (a t)")
        mod_a = yb[0:BATCH, 11:14, :].rearrange("p a t -> p (a t)")

        pj = [ctx.enter_context(nc.psum_tensor(f"pj{i}", [P, T], F32)) for i in range(2)]
        da = [ctx.enter_context(nc.psum_tensor(f"da{i}", [P, T], F32)) for i in range(2)]
        yp = [ctx.enter_context(nc.psum_tensor(f"yp{i}", [P, T], F32)) for i in range(2)]
        ma = ctx.enter_context(nc.psum_tensor("ma", [P, T], F32))
        mb = ctx.enter_context(nc.psum_tensor("mb", [P, T], F32))

        s = {n: sem(n) for n in (
            "const_set consts small_loaded c_silu w_head mod_sign mod_ready mod_fix mod_stored wo_loaded "
            "w_ready wo_ready neg_a_ready misc_set "
            "x_loaded row_loaded bn_done ve_done rstd_done xn_done h_done h_stored ssq_done ms_done r1_done "
            "hs_done ht_ready hh_done hl_done "
            "pj_ready pj_taken halo_done conv_tap x_ready bc_tap bc_halo bc_ready dt_copied "
            "dtt_ready u_done a_done e_done l_done dtc dt_done da_exp dat_ready dat_taken parts_done "
            "g_ready g_taken bt_ready bt_taken "
            "xt_ready xdt_done da_ready scan_done wend_done pend_done cp_done xw_done m_done "
            "ds_ready chain_done blk_done y_ready skip_done gate_done sq_done acc_done "
            "o_ready o_taken q_ready oms_done ry_done o_scaled o_stored").split()}

        w_loaded = [sem(f"w_loaded{n}") for n in range(4)]

        def tile_count(i, idx):
            return WT * i + idx + 1

        class At:

            def __init__(self, b, j):
                self.k = SPB * b + j if not isinstance(b, int) or b else j
                self.js = j % SPB
                self.i = IPB * b + j // SPI if not isinstance(b, int) or b else j // SPI
                self.q = (j // SPI) % IPB
                self.st = j % SPI
                self.b = b

        block = ctx.enter_context(nc.Block())

        HEAD = 5
        TAIL = SPB + HEAD

        def run(eng, slot):
            for j in range(HEAD):
                slot(0, j)
            with eng.Fori(0, BATCH - 1) as b:
                for j in range(HEAD, HEAD + SPB):
                    slot(b, j)
            for j in range(HEAD, TAIL):
                slot(BATCH - 1, j)

        def exists(b, j, back):
            if isinstance(b, int):
                return 0 <= SPB * b + j - back < NSTEP
            return True

        def out_slot(b, j):
            at = At(b, j)
            if at.st == 6 and exists(b, j, 0):
                return True, 0, at.i
            if at.st == 2 and exists(b, j, SPI) :
                return True, 1, at.i - 1
            return None

        def blk_count(b, j):
            base = (2 * SPB + 2 * SPI) * b if not isinstance(b, int) or b else 0
            full = j // SPB
            js = j % SPB
            return base + (2 * SPB + 2 * SPI) * full + 2 * (js + 1) + 2 * max(0, js + 1 - SPI)

        @block.sync
        def _(sp):
            sp.sem_inc(s["o_stored"], 16)
            sp.dma_start(cs_t[:, :, :], c_t).then_inc(s["small_loaded"], 16)
            sp.dma_start(wm.rearrange("p (k n) -> p k n", k=KH), w_mod.rearrange("(k p) n -> p k n", p=P)
                         ).then_inc(s["small_loaded"], 16)
            sp.dma_start(ln1_c[:, :], ln1).then_inc(s["small_loaded"], 16)
            sp.dma_start(neg_a[:, :], a_log.broadcast_to([P, HEADS])
                         ).then_inc(s["small_loaded"], 16)
            sp.dma_start(xt[:, :, :], x[0:T, :].rearrange("(c p) n -> p c n", p=P)).then_inc(s["x_loaded"], 16)
            for n in range(WT // 2):
                if n == 4:
                    sp.wait_ge(s["mod_fix"], 7)
                    sp.dma_start(mod_dram, mod_s).then_inc(s["mod_stored"], 16)
                    sp.wait_ge(s["mod_stored"], 16)
                    sp.dma_start(mod_row[:, :, :].rearrange("p a n -> p (a n)"),
                                 mod_dram[0:1, 0:2 * HID].broadcast_to([P, 2 * HID])).then_inc(s["row_loaded"], 16)
                if n >= 4:
                    sp.wait_ge(s["w_ready"], 2 * (n - 3))
                sp.dma_start(w_stage[:, (n % 4) * 2 * P * KH:(n % 4 + 1) * 2 * P * KH].rearrange("p (k n) -> p k n", k=KH),
                             w_in.rearrange("(k p) n -> p k n", p=P)[:, :, n * 2 * P:(n + 1) * 2 * P]
                             ).then_inc(w_loaded[n % 4], 16)
                if n == 0:
                    for dst, src in ((cw[:, :, :], conv_w),
                                     (cb[:, :], conv_b),
                                     (dpar[:, :], d_par),
                                     (dtb[:, :], dt_bias.broadcast_to([P, HEADS])),
                                     (mn_c[:, :], mnorm)):
                        sp.dma_start(dst, src).then_inc(s["small_loaded"], 16)
            sp.dma_start(w_o[:, :, :], w_out.rearrange("(t p) n -> p t n", p=P)).then_inc(s["wo_loaded"], 16)
            def store_h(i):
                sp.wait_ge(s["h_done"], 2 * i + 2)
                sp.dma_start(h_dram[bass.ds(i * T, T), :].rearrange("(c p) n -> p c n", p=P), xt[:, :, :]
                             ).then_inc(s["h_stored"], 16)

            store_h(0)

            def slot(b, j):
                at = At(b, j)
                if at.st == 2 and exists(b, j, at.st - SPI):
                    nxt = at.i + 1
                    wait_apart(sp, s["h_stored"], 16 * nxt)
                    sp.wait_ge(s["hs_done"], 4 * nxt)
                    sp.dma_start(xt[:, :, :], x[bass.ds(nxt * T, T), :].rearrange("(c p) n -> p c n", p=P)
                                 ).then_inc(s["x_loaded"], 16)
                    if at.q == IPB - 1:
                        row = at.b + 1 + (j // SPB)
                        sp.wait_ge(s["h_done"], 2 * nxt)
                        sp.dma_start(mod_row[:, :, :].rearrange("p a n -> p (a n)"),
                                     mod_dram[bass.ds(row, 1), 0:2 * HID].broadcast_to([P, 2 * HID])
                                     ).then_inc(s["row_loaded"], 16)
                if at.st == 5 and exists(b, j, at.st - SPI):
                    store_h(at.i + 1)
                if at.st == 4 and exists(b, j, 5):
                    if not isinstance(b, int) or b or j >= SPI:
                        sp.wait_ge(s["o_scaled"], 4 * at.i)
                        sp.dma_start(o_dram[bass.ds((at.i - 1) * T, T), :].rearrange("(c p) n -> p c n", p=P),
                                     o_acc[:, :, :]).then_inc(s["o_stored"], 16)

            run(sp, slot)
            sp.wait_ge(s["o_stored"], 16 * (NI + 1))
            sp.wait_ge(s["h_stored"], 16 * NI)

        @block.gpsimd
        def _(pool):
            pool.memset(inject[:, :, :], 0.0).then_inc(s["const_set"], 1)
            pool.memset(select[:, :, :], 0.0).then_inc(s["const_set"], 1)
            pool.memset(ones[:, :], 1.0).then_inc(s["consts"], 1)
            pool.memset(neg_half[:, :], -0.5).then_inc(s["consts"], 1)
            pool.memset(zero[:, :], 0.0).then_inc(s["consts"], 1)
            pool.memset(s_blk[:, :, :, :], 0.0).then_inc(s["consts"], 1)
            pool.wait_ge(s["const_set"], 2)
            pool.affine_select(out=inject[:, :, :], in_=inject[:, :, :], compare_op=ALU.not_equal, fill=1.0, base=0,
                               pattern=[[0, NC], [-1, CH]], channel_multiplier=1).then_inc(s["consts"], 1)
            for r in range(3):
                third = select[32 * r:32 * r + 32, :, :]
                pool.wait_ge(s["consts"], 5 + r)
                pool.affine_select(out=third, in_=third, compare_op=ALU.not_equal, fill=1.0, base=0,
                                   pattern=[[-1, HEADS], [0, P // 2]], channel_multiplier=1).then_inc(s["consts"], 1)
            pool.wait_ge(s["consts"], 8)

            def norm_power(i):
                pool.wait_ge(s["ve_done"], i + 1)
                if not isinstance(i, int) or i:
                    pool.wait_ge(s["xn_done"], 4 * i)
                pool.tensor_tensor(rstd[:, :], ve[:, :], neg_half[:, :], ALU.pow).then_inc(s["rstd_done"], 1)

            def modulate(i, row):
                pool.wait_ge(s["xn_done"], 4 * i + 4)
                pool.wait_ge(s["row_loaded"], 16 * (row + 1))
                pool.tensor_tensor(xt[:, :, :], xt[:, :, :], mod_row[:, 1:2, :].broadcast_to([P, NC, HID]), ALU.mult
                                   ).then_inc(s["h_done"], 1)
                pool.wait_ge(s["h_done"], 2 * i + 1)
                pool.tensor_tensor(xt[:, :, :], xt[:, :, :], mod_row[:, 0:1, :].broadcast_to([P, NC, HID]), ALU.add
                                   ).then_inc(s["h_done"], 1)

            def rms_power(i):
                pool.wait_ge(s["ms_done"], i + 1)
                if not isinstance(i, int) or i:
                    pool.wait_ge(s["hs_done"], 4 * i)
                pool.tensor_tensor(r1[:, :], ms[:, :], neg_half[:, :], ALU.pow).then_inc(s["r1_done"], 1)

            norm_power(0)
            modulate(0, 0)
            rms_power(0)

            def slot(b, j):
                at = At(b, j)
                k = at.k
                nxt = exists(b, j, at.st - SPI)
                new, mid, old = exists(b, j, 0), exists(b, j, 1), exists(b, j, 2)
                if exists(b, j, 3):
                    o = At(b, j - 3)
                    for t in range(TPS):
                        wait_apart(pool, s["sq_done"], 2 * (k - 3) + t + 1)
                        if o.st == 0 and t == 0:
                            if not isinstance(b, int) or k >= SPI:
                                wait_apart(pool, s["q_ready"], o.i)
                            pool.tensor_copy(acc[:, :], sq[:, :]).then_inc(s["acc_done"], 1)
                        else:
                            pool.wait_ge(s["acc_done"], 2 * (k - 3) + t)
                            pool.tensor_tensor(acc[:, :], acc[:, :], sq[:, :], ALU.add).then_inc(s["acc_done"], 1)
                if old:
                    o = At(b, j - 2)
                    for t in range(TPS):
                        pool.wait_ge(s["skip_done"], 2 * (k - 2) + t + 1)
                        pool.wait_ge(s["pj_taken"], tile_count(o.i, 4 + 4 * o.st + t))
                        ytile = yb[:, TPS * o.st + t, :]
                        pool.tensor_tensor(ytile, ytile, xc[:, o.js % 2, t, :], ALU.mult).then_inc(s["gate_done"], 1)
                if mid:
                    m = At(b, j - 1)
                    buf = m.js % 2

                    def decay_matrix(h):
                        d = dec[:, buf, h, :]
                        pool.tensor_tensor(d, d, g_s[:, m.q, :, :].rearrange("p c t -> p (c t)"), ALU.mult
                                           ).then_inc(s["m_done"], 1)

                    pool.wait_ge(s["g_taken"], m.i + 1)
                    pool.wait_ge(s["wend_done"], 2 * (k - 1) + 1)
                    decay_matrix(0)
                    decay_matrix(1)
                    pool.wait_ge(s["wend_done"], 2 * k)
                    pool.wait_ge(s["xdt_done"], 2 * k)
                    if old:
                        pool.wait_ge(s["ds_ready"], k - 1)
                    pool.tensor_tensor(
                        xw[:, :, :].rearrange("p c (h d) -> p (c h) d", d=HD),
                        xdt[:, buf, :, :].rearrange("p c (h d) -> p (c h) d", d=HD),
                        w_end[:, :, :].rearrange("p c h -> p (c h)").unsqueeze(2).broadcast_to([P, NC * HPS, HD]),
                        ALU.mult).then_inc(s["xw_done"], 1)
                    decay_matrix(2)
                    decay_matrix(3)
                if nxt and at.st == 3:
                    norm_power(at.i + 1)
                if nxt and at.st == 4:
                    modulate(at.i + 1, at.b + ((j // SPI + 1) // IPB))
                if at.st == 3 and exists(b, j, 4) and (not isinstance(b, int) or k >= SPI):
                    pool.wait_ge(s["oms_done"], at.i)
                    pool.tensor_tensor(r_y[:, :], o_ms[:, :], neg_half[:, :], ALU.pow).then_inc(s["ry_done"], 1)
                if nxt and at.st == 6:
                    rms_power(at.i + 1)

            run(pool, slot)

        @block.scalar
        def _(act):
            act.wait_ge(s["small_loaded"], 16 * 9)
            act.activation(cs_t[:, :, :], cs_t[:, :, :], ACT.Silu).then_inc(s["c_silu"], 1)
            act.activation(neg_a[:, :], neg_a[:, :], ACT.Exp).then_inc(s["neg_a_ready"], 1)
            act.wait_ge(s["neg_a_ready"], 1)
            act.mul(neg_a[:, :], neg_a[:, :], -1.0).then_inc(s["neg_a_ready"], 1)

            def squares(i):
                act.wait_ge(s["h_done"], 2 * i + 2)
                for c in range(NC):
                    act.activation(hs[:, c, :], xt[:, c, :], ACT.Square, accum_out=ssq[:, c:c + 1]
                                   ).then_inc(s["ssq_done"], 1)

            def scale_h(i):
                act.wait_ge(s["r1_done"], i + 1)
                act.wait_ge(s["ssq_done"], 4 * i + 4)
                for c in range(NC):
                    act.activation(hs[:, c, :], xt[:, c, :], ACT.Copy, scale=r1[:, c:c + 1]).then_inc(s["hs_done"], 1)

            squares(0)
            scale_h(0)

            def start_bc(b, j, i, q):
                for n, rows in ((0, P), (1, NS)):
                    act.wait_ge(s["pj_ready"], tile_count(i, n))
                    if j is not None:
                        k = At(b, j).k
                        act.wait_ge(s["conv_tap"], 6 * k + 5 + n)
                        act.wait_ge(s["halo_done"], 4 * k + 4)
                    if n == 1:
                        act.activation(tl[64:96, 0, :], pj[n][64:96, :], ACT.Copy).then_inc(s["dt_copied"], 1)
                    act.activation(raw[0:rows, n, TAPS - 1:], pj[n][0:rows, :], ACT.Copy).then_inc(s["misc_set"], 1)
                    dst = cc[:, q, :] if n == 0 else bb[:, :]
                    act.activation(dst, pj[n][0:rows, :], ACT.Identity,
                                   bias=cb[0:rows, YT + n:YT + n + 1], scale=cw[0:rows, YT + n, TAPS - 1:TAPS]
                                   ).then_inc(s["pj_taken"], 1)

            def softplus_parts(i):
                act.wait_ge(s["a_done"], i + 1)
                act.activation(e_t[:, :, :], a_t[:, :, :], ACT.Exp, scale=-1.0).then_inc(s["e_done"], 1)
                act.wait_ge(s["e_done"], i + 1)
                act.activation(l_t[:, :, :], e_t[:, :, :], ACT.Ln, bias=1.0).then_inc(s["l_done"], 1)

            start_bc(0, None, 0, 0)
            softplus_parts(0)

            def slot(b, j):
                at = At(b, j)
                k = at.k
                new, mid, old = exists(b, j, 0), exists(b, j, 1), exists(b, j, 2)
                nxt = exists(b, j, at.st - SPI)
                if exists(b, j, 3):
                    o = At(b, j - 3)
                    for t in range(TPS):
                        act.wait_ge(s["gate_done"], 2 * (k - 3) + t + 1)
                        wait(act, s["acc_done"], 2 * (k - 3) + t)
                        act.activation(sq[:, :], yb[:, TPS * o.st + t, :], ACT.Square).then_inc(s["sq_done"], 1)
                if new and at.st == 0:
                    for n, dst in ((0, cc[:, at.q, :]), (1, bb[:, :])):
                        act.wait_ge(s["bc_tap"], 6 * at.i + 5 + n)
                        act.activation(dst, dst, ACT.Silu).then_inc(s["bc_ready"], 1)
                if mid and At(b, j - 1).q:
                    m = At(b, j - 1)
                    act.wait_ge(s["y_ready"], 2 * (k - 1))
                    for half in range(2):
                        r = slice(64 * half, 64 * half + 64)
                        act.activation(s_blk[r, 0, :, 64 * half:64 * half + 64], state[r, m.st, :, :], ACT.Copy
                                       ).then_inc(s["blk_done"], 1)
                if isinstance(b, int) and k == HEAD - 1:
                    act.wait_ge(s["mod_stored"], 16)
                if new:
                    for t in range(TPS):
                        idx = 2 + 4 * at.st + t
                        ch = TPS * at.st + t
                        act.wait_ge(s["pj_ready"], tile_count(at.i, idx))
                        if at.st == 0:
                            act.wait_ge(s["bc_tap"], 6 * at.i + 5 + t)
                            act.wait_ge(s["bc_halo"], 4 * at.i + 4)
                        else:
                            act.wait_ge(s["conv_tap"], 6 * (k - 1) + 5 + t)
                            act.wait_ge(s["halo_done"], 4 * k)
                        act.activation(raw[:, t, TAPS - 1:], pj[idx % 2][:, :], ACT.Copy).then_inc(s["misc_set"], 1)
                        if old:
                            act.wait_ge(s["gate_done"], 2 * (k - 2) + t + 1)
                        act.activation(xc[:, at.js % 2, t, :], pj[idx % 2][:, :], ACT.Identity,
                                       bias=cb[:, ch:ch + 1], scale=cw[:, ch, TAPS - 1:TAPS]).then_inc(s["pj_taken"], 1)
                if new and at.st == 0:
                    act.wait_ge(s["dtc"], 8 * at.i + 8)
                    act.activation(a_t[:, :, :], a_t[:, :, :], ACT.Exp).then_inc(s["da_exp"], 1)
                if new:
                    for t in range(TPS):
                        idx = 4 + 4 * at.st + t
                        act.wait_ge(s["pj_ready"], tile_count(at.i, idx))
                        act.activation(yb[:, TPS * at.st + t, :], pj[idx % 2][:, :], ACT.Silu).then_inc(s["pj_taken"], 1)
                    for t in range(TPS):
                        act.wait_ge(s["conv_tap"], 6 * k + 5 + t)
                        act.activation(xc[:, at.js % 2, t, :], xc[:, at.js % 2, t, :], ACT.Silu).then_inc(s["x_ready"], 1)
                if nxt and at.st == 7:
                    start_bc(b, j, at.i + 1, (at.q + 1) % IPB)
                if mid:
                    wait(act, s["y_ready"], 2 * (k - 1))
                    act.wait_ge(s["chain_done"], 8 * (k - 1) + 6)
                    for half in range(2):
                        r = slice(64 * half, 64 * half + 64)
                        dst = s_blk[r, 1:NC, :, 64 * half:64 * half + 64].rearrange("p c a d -> p (c a) d")
                        act.activation(dst, s_ch[r, :, :, :].rearrange("p c a d -> p (c a) d"), ACT.Copy
                                       ).then_inc(s["blk_done"], 1)
                if nxt and at.st == 7:
                    softplus_parts(at.i + 1)
                if nxt and at.st == 5:
                    squares(at.i + 1)
                if nxt and at.st == 6:
                    scale_h(at.i + 1)

            run(act, slot)

        @block.vector
        def _(dve):
            def token_norm_a(i):
                dve.wait_ge(s["x_loaded"], 16 * (i + 1))
                for c in range(NC):
                    dve.bn_stats(stats[:, c, :], xt[:, c, :]).then_inc(s["bn_done"], 1)
                wait_apart(dve, s["bn_done"], 8 * i + 4)
                for c in range(NC):
                    dve.bn_aggr(mv[:, c, :], stats[:, c, :]).then_inc(s["bn_done"], 1)
                dve.wait_ge(s["bn_done"], 8 * i + 8)
                dve.tensor_scalar(ve[:, :], mv[:, :, 1], EPS, None, ALU.add).then_inc(s["ve_done"], 1)

            def token_norm_b(i):
                dve.wait_ge(s["rstd_done"], i + 1)
                for c in range(NC):
                    dve.tensor_scalar(xt[:, c, :], xt[:, c, :], mv[:, c, 0:1], rstd[:, c:c + 1], ALU.subtract, ALU.mult
                                      ).then_inc(s["xn_done"], 1)

            def token_ms(i):
                dve.wait_ge(s["ssq_done"], 4 * i + 4)
                dve.tensor_scalar(ms[:, :], ssq[:, :], 1.0 / HID, EPS, ALU.mult, ALU.add).then_inc(s["ms_done"], 1)

            token_norm_a(0)
            dve.wait_ge(s["small_loaded"], 16 * 9)
            dve.wait_ge(s["mod_ready"], 3)
            for n in range(3):
                dve.tensor_copy(mod_s[:, n * T:(n + 1) * T], [ma, mb, yp[0]][n][0:BATCH, :]).then_inc(s["mod_fix"], 1)
            dve.wait_ge(s["mod_fix"], 3)
            for o in (1, 4):
                dve.tensor_scalar(mod_s[:, o * HID:(o + 1) * HID], mod_s[:, o * HID:(o + 1) * HID], 1.0, None, ALU.add
                                  ).then_inc(s["mod_fix"], 1)
            for n, o in enumerate((2, 5)):
                g = mod_s[:, o * HID:(o + 1) * HID]
                mag = mod_a[:, 2 * n * HID:(2 * n + 1) * HID]
                sgn = mod_a[:, (2 * n + 1) * HID:(2 * n + 2) * HID]
                dve.scalar_tensor_tensor(mag, g, -1.0, g, ALU.mult, ALU.max).then_inc(s["mod_sign"], 1)
                dve.wait_ge(s["mod_sign"], 3 * n + 1)
                dve.tensor_scalar(mag, mag, 0.25, None, ALU.max).then_inc(s["mod_sign"], 1)
                dve.tensor_scalar(sgn, g, 0.0, 2.0, ALU.is_ge, ALU.mult).then_inc(s["mod_sign"], 1)
                dve.wait_ge(s["mod_sign"], 3 * n + 3)
                dve.scalar_tensor_tensor(g, sgn, -1.0, mag, ALU.add, ALU.mult).then_inc(s["mod_fix"], 1)
            for n in range(WT // 2):
                dve.wait_ge(w_loaded[n % 4], 16 * (n // 4 + 1))
                st_n = w_stage[:, (n % 4) * 2 * P * KH:(n % 4 + 1) * 2 * P * KH].rearrange("p (k n) -> p k n", k=KH)
                for kk in range(KH):
                    dve.tensor_scalar(w_hi[:, kk, n * 2 * P:(n + 1) * 2 * P], st_n[:, kk, :], ln1_c[:, kk:kk + 1], None,
                                      ALU.mult).then_inc(s["w_head"], 1)
                for kk in range(KH):
                    dve.wait_ge(s["w_head"], KH * n + kk + 1)
                    dve.scalar_tensor_tensor(w_lo[:, kk, n * 2 * P:(n + 1) * 2 * P], st_n[:, kk, :], ln1_c[:, kk:kk + 1],
                                             w_hi[:, kk, n * 2 * P:(n + 1) * 2 * P].bitcast(F32), ALU.mult, ALU.subtract
                                             ).then_inc(s["w_ready"], 1)
                if n == 1:
                    token_norm_b(0)
                if n == 8:
                    token_ms(0)
            dve.wait_ge(s["wo_loaded"], 16)
            for t in range(YT):
                dve.tensor_scalar(w_o[:, t, :], w_o[:, t, :], mn_c[:, t:t + 1], None, ALU.mult).then_inc(s["wo_ready"], 1)


            def conv_pair(tiles, halo, taps, halo0, tap0, q):
                if q:
                    dve.wait_ge(halo, halo0)
                for n, (ch, rows, dst) in enumerate(tiles):
                    if q == 0:
                        dve.memset(raw[0:rows, n, 0:TAPS - 1], 0.0).then_inc(halo, 1)
                    else:
                        dve.tensor_copy(raw[0:rows, n, 0:TAPS - 1], tail[0:rows, ch, :]).then_inc(halo, 1)
                for k in range(TAPS - 1):
                    for n, (ch, rows, dst) in enumerate(tiles):
                        dve.wait_ge(halo, halo0 + n + 1) if k == 0 else dve.wait_ge(taps, tap0 + 2 * (k - 1) + n + 1)
                        dve.scalar_tensor_tensor(dst, raw[0:rows, n, k:k + T], cw[0:rows, ch, k:k + 1], dst,
                                                 ALU.mult, ALU.add).then_inc(taps, 1)
                for n, (ch, rows, dst) in enumerate(tiles):
                    dve.tensor_copy(tail[0:rows, ch, :], raw[0:rows, n, T:T + TAPS - 1]).then_inc(halo, 1)

            def split_tokens(i):
                for kk, bank in ((0, mb), (1, ma)):
                    dve.wait_ge(s["ht_ready"], 2 * i + kk + 1)
                    wait(dve, s["pj_ready"], WT * i)
                    dve.tensor_copy(h_hi[:, kk, :], bank[:, :]).then_inc(s["hh_done"], 1)
                    dve.wait_ge(s["hh_done"], 2 * i + kk + 1)
                    dve.tensor_tensor(h_lo[:, kk, :], bank[:, :], h_hi[:, kk, :].bitcast(F32), ALU.subtract
                                      ).then_inc(s["hl_done"], 1)

            def time_step_input(i):
                dve.wait_ge(s["dtt_ready"], i + 1)
                dve.tensor_tensor(u_t[:, :, :], mb[:, 0:NC * HEADS].rearrange("p (c h) -> p c h", c=NC),
                                  dtb[:, :].unsqueeze(1).broadcast_to([P, NC, HEADS]), ALU.add).then_inc(s["u_done"], 1)
                dve.wait_ge(s["u_done"], i + 1)
                dve.scalar_tensor_tensor(a_t[:, :, :], u_t[:, :, :], -1.0, u_t[:, :, :], ALU.mult, ALU.max).then_inc(s["a_done"], 1)

            def conv_bc(i, q):
                dve.wait_ge(s["pj_taken"], tile_count(i, 1))
                conv_pair([(YT, P, cc[:, q, :]), (YT + 1, NS, bb[:, :])], s["bc_halo"], s["bc_tap"], 4 * i, 6 * i, q)

            def time_steps(i, q):
                c0 = 8 * i

                def link(n, ins):
                    ins.then_inc(s["dtc"], 1)
                    dve.wait_ge(s["dtc"], c0 + n)

                dve.wait_ge(s["l_done"], i + 1)
                link(1, dve.tensor_scalar(m_t[:, :, :], e_t[:, :, :], 1.0, 1.0, ALU.add, ALU.is_equal))
                dve.tensor_tensor(l_t[:, :, :], l_t[:, :, :], m_t[:, :, :], ALU.add).then_inc(s["dtc"], 1)
                link(3, dve.tensor_scalar(a_t[:, :, :], e_t[:, :, :], 1.0, 1.0, ALU.add, ALU.subtract))
                link(4, dve.tensor_tensor(a_t[:, :, :], a_t[:, :, :], m_t[:, :, :], ALU.add))
                dve.tensor_tensor(l_t[:, :, :], l_t[:, :, :], e_t[:, :, :], ALU.mult).then_inc(s["dtc"], 1)
                link(6, dve.reciprocal(m_t[:, :, :], a_t[:, :, :]))
                link(7, dve.tensor_tensor(l_t[:, :, :], l_t[:, :, :], m_t[:, :, :], ALU.mult))
                dve.scalar_tensor_tensor(dt_s[:, q, :, :], u_t[:, :, :], 0.0, l_t[:, :, :], ALU.max, ALU.add
                                         ).then_inc(s["dt_done"], 1)
                dve.wait_ge(s["dt_done"], i + 1)
                dve.tensor_tensor(a_t[:, :, :], dt_s[:, q, :, :], neg_a[:, :].unsqueeze(1).broadcast_to([P, NC, HEADS]),
                                  ALU.mult).then_inc(s["dtc"], 1)

            def decays(i, q, k):
                dve.wait_ge(s["dat_ready"], i + 1)
                dve.tensor_copy(tl[0:32, 0, :], mb[0:32, :]).then_inc(s["dat_taken"], 1)
                dve.wait_ge(s["dat_taken"], 6 * i + 1)
                for c in range(NC):
                    dve.tensor_tensor_scan(tl[0:32, 1, c * CH:(c + 1) * CH], tl[0:32, 0, c * CH:(c + 1) * CH], zero[:, :],
                                           1.0, ALU.mult, ALU.add).then_inc(s["dat_taken"], 1)
                dve.wait_ge(s["g_ready"], i + 1)
                dve.tensor_copy(g_s[:, q, :, :], ma[:, :].rearrange("p (c t) -> p c t", c=NC)
                                ).then_inc(s["g_taken"], 1)
                dve.wait_ge(s["dat_taken"], 6 * i + 5)
                dve.memset(tl[0:32, 0, 0::CH], 0.0).then_inc(s["dat_taken"], 1)
                dve.wait_ge(s["dat_taken"], 6 * i + 6)
                wait(dve, s["da_ready"], 6 * k)

                def link_part(n, ins):
                    ins.then_inc(s["parts_done"], 1)
                    dve.wait_ge(s["parts_done"], 5 * i + n)

                link_part(1, dve.tensor_copy(parts[0:32, :, :], tl[0:32, :, :]))
                link_part(2, dve.tensor_tensor(tl[32:64, :, :], tl[0:32, :, :], parts[0:32, :, :], ALU.subtract))
                link_part(3, dve.tensor_copy(parts[32:64, :, :], tl[32:64, :, :]))
                link_part(4, dve.tensor_tensor(tl[64:96, :, :], tl[32:64, :, :], parts[32:64, :, :], ALU.subtract))
                dve.tensor_copy(parts[64:96, :, :], tl[64:96, :, :]).then_inc(s["parts_done"], 1)
                dve.wait_ge(s["bt_ready"], i + 1)
                dve.tensor_copy(b_tok[:, q, :, :], mb[:, 0:NC * NS].rearrange("p (c n) -> p c n", c=NC)
                                ).then_inc(s["bt_taken"], 1)

            split_tokens(0)
            time_step_input(0)
            conv_bc(0, 0)

            def slot(b, j):
                at = At(b, j)
                k = at.k
                new, mid, old = exists(b, j, 0), exists(b, j, 1), exists(b, j, 2)
                nxt = exists(b, j, at.st - SPI)
                m = At(b, j - 1)
                buf = m.js % 2

                def scan_pair(pair):
                    for h in (2 * pair, 2 * pair + 1):
                        dve.wait_ge(s["da_ready"], 6 * (k - 1) + h + 1)
                        dve.tensor_tensor_scan(dec[:, buf, h, :], da[h % 2][:, :], inject[:, :, :].rearrange("p c t -> p (c t)"),
                                               0.0, ALU.mult, ALU.add).then_inc(s["scan_done"], 1)
                    dve.wait_ge(s["scan_done"], 4 * (k - 1) + 2 * pair + 2)
                    if old and pair == 0:
                        dve.wait_ge(s["xw_done"], k - 1)
                    dve.tensor_copy(w_end[:, :, 2 * pair:2 * pair + 2],
                                    dec[:, buf, 2 * pair:2 * pair + 2, CH - 1::CH].rearrange("p h c -> p c h")
                                    ).then_inc(s["wend_done"], 1)

                if mid:
                    scan_pair(0)
                if new and at.st == 0:
                    time_steps(at.i, at.q)
                if old:
                    o = At(b, j - 2)
                    for t in range(TPS):
                        dve.wait_ge(s["y_ready"], 2 * (k - 2) + t + 1)
                        ch = TPS * o.st + t
                        dve.scalar_tensor_tensor(xc[:, o.js % 2, t, :], xc[:, o.js % 2, t, :], dpar[:, ch:ch + 1],
                                                 yp[t][:, :], ALU.mult, ALU.add).then_inc(s["skip_done"], 1)
                if at.st == 3 and exists(b, j, 4) and (not isinstance(b, int) or k >= SPI):
                    dve.wait_ge(s["q_ready"], at.i)
                    dve.tensor_scalar(o_ms[:, :], mb[:, 0:NC], 1.0 / DIN, EPS, ALU.mult, ALU.add).then_inc(s["oms_done"], 1)
                if mid:
                    scan_pair(1)
                    for n, bank in ((0, mb), (1, ma)):
                        dve.wait_ge(s["xt_ready"], 2 * (k - 1) + n + 1)
                        dve.tensor_tensor(
                            xdt[:, buf, 2 * n:2 * n + 2, :].rearrange("p c (h d) -> p c h d", d=HD),
                            bank[:, :].rearrange("p (c h d) -> p c h d", c=2, d=HD),
                            dt_s[:, m.q, 2 * n:2 * n + 2, HPS * m.st:HPS * (m.st + 1)].unsqueeze(3
                                ).broadcast_to([P, 2, HPS, HD]),
                            ALU.mult).then_inc(s["xdt_done"], 1)
                    for t in range(TPS):
                        dve.wait_ge(s["da_ready"], 6 * (k - 1) + HPS + t + 1)
                        if old:
                            dve.wait_ge(s["chain_done"], 8 * (k - 1))
                        dve.tensor_copy(p_end[:, t, :], da[t % 2][:, CH - 1::CH]).then_inc(s["pend_done"], 1)
                        dve.wait_ge(s["bc_ready"], 2 * m.i + 1)
                        dve.tensor_tensor(cp[:, t, :], da[t % 2][:, :], cc[:, m.q, :], ALU.mult).then_inc(s["cp_done"], 1)
                if new and at.st == 0:
                    decays(at.i, at.q, k)
                if new:
                    dve.wait_ge(s["pj_taken"], tile_count(at.i, 2 + 4 * at.st + 1))
                    conv_pair([(TPS * at.st + t, P, xc[:, at.js % 2, t, :]) for t in range(TPS)],
                              s["halo_done"], s["conv_tap"], 4 * k, 6 * k, at.q)
                if out_slot(b, j):
                    half, i = out_slot(b, j)[1:]
                    for n, bank in ((0, mb), (1, ma)):
                        dve.wait_ge(s["o_ready"], 4 * i + 2 * half + n + 1)
                        dst = o_acc[:, 2 * n:2 * n + 2, :].rearrange("p c d -> p (c d)")
                        if half == 0:
                            dve.wait_ge(s["o_stored"], 16 * (i + 1))
                            dve.tensor_copy(dst, bank[:, :]).then_inc(s["o_taken"], 1)
                        else:
                            dve.tensor_tensor(dst, dst, bank[:, :], ALU.add).then_inc(s["o_taken"], 1)
                if at.st == 4 and exists(b, j, 5) and (not isinstance(b, int) or k >= SPI):
                    dve.wait_ge(s["ry_done"], at.i)
                    for c in range(NC):
                        dve.tensor_scalar(o_acc[:, c, :], o_acc[:, c, :], r_y[:, c:c + 1], None, ALU.mult
                                          ).then_inc(s["o_scaled"], 1)
                if nxt and at.st == 7:
                    split_tokens(at.i + 1)
                if mid:
                    dve.wait_ge(s["ds_ready"], k)
                    dve.wait_ge(s["pend_done"], 2 * k)
                    if old:
                        dve.wait_ge(s["blk_done"], blk_count(b, j - 2))
                    for c in range(NC):
                        for t in range(TPS):
                            src = state[:, m.st, t, :] if c == 0 else s_ch[:, c - 1, t, :]
                            dst = state[:, m.st, t, :] if c == NC - 1 else s_ch[:, c, t, :]
                            add = ma[:, (c * TPS + t) * HD:(c * TPS + t + 1) * HD]
                            if c == NC - 1 and t == 0 and m.q:
                                dve.wait_ge(s["blk_done"], blk_count(b, j - 1) - 2)
                            if c == 0 and m.q == 0:
                                dve.tensor_copy(dst, add).then_inc(s["chain_done"], 1)
                            else:
                                if c:
                                    dve.wait_ge(s["chain_done"], 8 * (k - 1) + 2 * (c - 1) + t + 1)
                                dve.scalar_tensor_tensor(dst, src, p_end[:, t, c:c + 1], add, ALU.mult, ALU.add
                                                         ).then_inc(s["chain_done"], 1)
                if nxt and at.st == 7:
                    time_step_input(at.i + 1)
                    conv_bc(at.i + 1, (at.q + 1) % IPB)
                if nxt and at.st == 3:
                    token_norm_a(at.i + 1)
                if nxt and at.st == 4:
                    token_norm_b(at.i + 1)
                if nxt and at.st == 6:
                    token_ms(at.i + 1)

            run(dve, slot)

        @block.tensor
        def _(pe):
            pe.wait_ge(s["consts"], 8)
            pe.wait_ge(s["c_silu"], 1)
            for n, bank in enumerate((ma, mb, yp[0])):
                for kk in range(KH):
                    last = pe.matmul(bank[0:BATCH, :], cs_t[:, kk, :], wm[:, kk * MOD + n * T:kk * MOD + (n + 1) * T],
                                     start=(kk == 0), stop=(kk == KH - 1))
                last.then_inc(s["mod_ready"], 1)

            def project(i, idx, weights=0):
                wait(pe, s["pj_taken"], tile_count(i, idx) - 2)
                if weights:
                    pe.wait_ge(s["w_ready"], weights)
                cols = slice(idx * P, (idx + 1) * P)
                first = True
                for kk in range(KH):
                    for w, h in ((w_hi, h_hi), (w_hi, h_lo), (w_lo, h_hi)):
                        last = pe.matmul(pj[idx % 2][:, :], w[:, kk, cols], h[:, kk, :], start=first,
                                         stop=(kk == KH - 1 and w is w_lo))
                        first = False
                last.then_inc(s["pj_ready"], 1)

            def transpose_tokens(i):
                pe.wait_ge(s["hs_done"], 4 * i + 4)
                for kk, bank in ((0, mb), (1, ma)):
                    for c in range(NC):
                        last = pe.transpose(bank[:, c * CH:(c + 1) * CH], hs[:, c, kk * P:(kk + 1) * P], ident[:, :])
                    last.then_inc(s["ht_ready"], 1)

            def project_bc(i, weights=0):
                pe.wait_ge(s["hl_done"], 2 * i + 2)
                project(i, 0, weights)
                project(i, 1, weights)

            def transpose_dt(i):
                wait_apart(pe, s["dt_copied"], i + 1)
                for c in range(NC):
                    last = pe.transpose(mb[:, c * HEADS:(c + 1) * HEADS], tl[64:96, 0, c * CH:(c + 1) * CH],
                                        ident[64:96, 64:96])
                last.then_inc(s["dtt_ready"], 1)

            def spread_decay(m, h):
                head = HPS * m.st + h
                for half in range(2):
                    last = pe.matmul(da[h % 2][64 * half:64 * half + 64, :], select[:, head, :], parts[:, 0, :],
                                     start=True, stop=True)
                last.then_inc(s["da_ready"], 1)

            pe.wait_ge(s["mod_fix"], 3)
            transpose_tokens(0)
            project_bc(0, KH)
            transpose_dt(0)

            def slot(b, j):
                at = At(b, j)
                k = at.k
                new, mid, old = exists(b, j, 0), exists(b, j, 1), exists(b, j, 2)
                nxt = exists(b, j, at.st - SPI)
                m = At(b, j - 1)
                first_run = isinstance(b, int) and b == 0
                if first_run and k == HEAD - 1:
                    pe.wait_ge(s["wo_ready"], YT)
                if old:
                    o = At(b, j - 2)
                    buf = o.js % 2
                    pe.wait_ge(s["m_done"], 4 * (k - 2) + 4)
                    pe.wait_ge(s["blk_done"], blk_count(b, j - 2))
                    pe.wait_ge(s["cp_done"], 2 * (k - 2) + 2)
                    for t in range(TPS):
                        if exists(b, j, 3):
                            pe.wait_ge(s["skip_done"], 2 * (k - 3) + t + 1)
                        for c in range(NC):
                            for half in range(2):
                                h = 2 * t + half
                                pe.matmul(yp[t][64 * half:64 * half + 64, c * CH:(c + 1) * CH],
                                          xdt[:, buf, c, h * HD:(h + 1) * HD], dec[:, buf, h, c * CH:(c + 1) * CH],
                                          start=(c == 0), stop=False, skip_group_check=True)
                        for c in range(1 if o.q == 0 else 0, NC):
                            last = pe.matmul(yp[t][:, c * CH:(c + 1) * CH], s_blk[:, c, t, :], cp[:, t, c * CH:(c + 1) * CH],
                                             start=False, stop=True, skip_group_check=True)
                        last.then_inc(s["y_ready"], 1)
                if at.st == 3 and exists(b, j, 4) and (not isinstance(b, int) or k >= SPI):
                    pe.wait_ge(s["acc_done"], 2 * SPI * at.i)
                    if mid:
                        pe.wait_ge(s["chain_done"], 8 * (k - 1))
                    else:
                        pe.wait_ge(s["o_taken"], 4 * at.i)
                    for c in range(NC):
                        last = pe.matmul(mb[:, c:c + 1], acc[:, c * CH:(c + 1) * CH], ones[:, :], start=True, stop=True)
                    last.then_inc(s["q_ready"], 1)
                if mid:
                    for h in (2, 3):
                        pe.wait_ge(s["scan_done"], 4 * (k - 1) + h - 1)
                        spread_decay(m, h)
                    pe.wait_ge(s["x_ready"], 2 * (k - 1) + 2)
                    if old:
                        pe.wait_ge(s["chain_done"], 8 * (k - 1))
                    else:
                        pe.wait_ge(s["bt_taken"], 1)
                    if new and at.st == 0:
                        pe.wait_ge(s["u_done"], at.i + 1)
                    if at.st == 3 and exists(b, j, SPI):
                        pe.wait_ge(s["oms_done"], at.i)
                    for n, bank in ((0, mb), (1, ma)):
                        for c in range(2):
                            for t in range(TPS):
                                last = pe.transpose(bank[:, (c * TPS + t) * P:(c * TPS + t + 1) * P],
                                                    xc[:, m.js % 2, t, (2 * n + c) * CH:(2 * n + c + 1) * CH], ident[:, :])
                        last.then_inc(s["xt_ready"], 1)
                if new:
                    for idx in (2 + 4 * at.st, 3 + 4 * at.st):
                        weights = 0
                        if first_run and k < HEAD:
                            weights = WT if k == HEAD - 1 else 2 * (idx // 2 + 1)
                        project(at.i, idx, weights)
                if mid:
                    for t in range(TPS):
                        pe.wait_ge(s["scan_done"], 4 * (k - 1) + HPS - 1 + t)
                        pair = select[:, HPS * m.st + 2 * t:HPS * m.st + 2 * t + 2, :].rearrange("p h n -> p (h n)")
                        pe.matmul(da[t % 2][:, :], pair, parts[:, 1, :], start=True, stop=True
                                  ).then_inc(s["da_ready"], 1)
                if new:
                    for idx in (4 + 4 * at.st, 5 + 4 * at.st):
                        project(at.i, idx, 2 * (idx // 2 + 1) if first_run and k < HEAD else 0)
                if new and at.st == 0:
                    i = at.i
                    if mid:
                        wait_apart(pe, s["xdt_done"], 2 * (k - 1) + 2)
                    else:
                        pe.wait_ge(s["u_done"], 1)
                    pe.wait_ge(s["da_exp"], i + 1)
                    for c in range(NC):
                        last = pe.transpose(mb[0:HEADS, c * CH:(c + 1) * CH], a_t[:, c, :], ident[:, :])
                    last.then_inc(s["dat_ready"], 1)
                    pe.wait_ge(s["bc_ready"], 2 * i + 2)
                    for c in range(NC):
                        last = pe.matmul(ma[:, c * CH:(c + 1) * CH], bb[:, c * CH:(c + 1) * CH],
                                         cc[0:NS, at.q, c * CH:(c + 1) * CH], start=True, stop=True)
                    last.then_inc(s["g_ready"], 1)
                    wait_apart(pe, s["dat_taken"], 6 * i + 1)
                    for c in range(NC):
                        last = pe.transpose(mb[:, c * NS:(c + 1) * NS], bb[:, c * CH:(c + 1) * CH], ident[0:NS, 0:NS])
                    last.then_inc(s["bt_ready"], 1)
                if out_slot(b, j):
                    half, i = out_slot(b, j)[1:]
                    pe.wait_ge(s["gate_done"], 2 * SPI * i + SPI * (half + 1))
                    for n, bank in ((0, mb), (1, ma)):
                        if mid:
                            pe.wait_ge(s["xdt_done"], 2 * (k - 1) + n + 1)
                        for c in range(2):
                            for t in range(YT // 2):
                                tt = YT // 2 * half + t
                                last = pe.matmul(bank[:, c * HID:(c + 1) * HID], yb[:, tt, (2 * n + c) * CH:(2 * n + c + 1) * CH],
                                                 w_o[:, tt, :], start=(t == 0), stop=(t == YT // 2 - 1))
                        last.then_inc(s["o_ready"], 1)
                if nxt and at.st == 7:
                    if mid:
                        pe.wait_ge(s["xdt_done"], 2 * k)
                    transpose_tokens(at.i + 1)
                if mid:
                    pe.wait_ge(s["xw_done"], k)
                    pe.wait_ge(s["bt_taken"], m.i + 1)
                    if new and at.st == 0:
                        pe.wait_ge(s["g_taken"], at.i + 1)
                    if out_slot(b, j):
                        half, i = out_slot(b, j)[1:]
                        pe.wait_ge(s["o_taken"], 4 * i + 2 * half + 2)
                    if nxt and at.st == 7:
                        pe.wait_ge(s["hl_done"], 2 * at.i + 4)
                    for c in range(NC):
                        for half in range(2):
                            last = pe.matmul(
                                ma[64 * half:64 * half + 64, c * TPS * HD:(c + 1) * TPS * HD].rearrange("p (t d) -> p t d", d=HD),
                                b_tok[:, m.q, c, :],
                                xw[:, c, :].rearrange("p (t e d) -> p t e d", t=TPS, e=2)[:, :, half, :],
                                start=True, stop=True)
                    last.then_inc(s["ds_ready"], 1)
                if nxt and at.st == 7:
                    project_bc(at.i + 1)
                    transpose_dt(at.i + 1)
                if new:
                    for h in range(2):
                        if mid:
                            pe.wait_ge(s["cp_done"], 2 * (k - 1) + h + 1)
                        if at.st == 0:
                            pe.wait_ge(s["parts_done"], 5 * (at.i + 1))
                        spread_decay(at, h)

            run(pe, slot)


def mlp_phase(nc, x, w_up, w_dn, ln2, w_ff, rram, h_dram, o_dram, mod_dram, out):
    ctx = ExitStack()
    with ctx:
        def sb(name, shape, dt=F32):
            return ctx.enter_context(nc.sbuf_tensor(name, shape, dt))

        def pb(name):
            return ctx.enter_context(nc.psum_tensor(name, [P, T], F32))

        KI = INTER // P

        ident = sb("ident2", [P, P])
        neg_half = sb("neg_half2", [P, NC])
        wu_hi = sb("wu_hi", [P, KH, 2 * INTER], F32R)
        wu_lo = sb("wu_lo", [P, KH, 2 * INTER], F32R)
        wd_hi = sb("wd_hi", [P, KI, HID], F32R)
        wd_lo = sb("wd_lo", [P, KI, HID], F32R)
        wf_hi = sb("wf_hi", [P, KH, HID], F32R)
        wf_lo = sb("wf_lo", [P, KH, HID], F32R)
        wu_st = sb("wu_st", [P, 2, KH, T])
        wd_st = sb("wd_st", [P, KI, HID])
        wf_st = sb("wf_st", [P, KH, HID])
        rr_st = sb("rr_st", [P, KH, HID])
        wf_a = sb("wf_a", [P, KH, HID])
        wf_b = sb("wf_b", [P, KH, HID])
        ln2_c = sb("ln2_c", [P, KH])
        rows = sb("rows", [P, 2, HID])
        cols = sb("cols", [P, BATCH, 2 * KH])
        x1 = sb("x1", [P, 2, NC, HID])
        hb = sb("hb", [P, NC, HID])
        xb = sb("xb", [P, 2, NC, HID])
        x1r = sb("x1r", [P, NC, HID])
        ssq = sb("ssq2", [P, NC])
        ms = sb("ms2", [P, NC])
        r2 = sb("r2", [P, NC])
        t_hi = sb("t_hi", [P, KH, T], F32R)
        t_lo = sb("t_lo", [P, KH, T], F32R)
        gate = sb("gate", [P, 2, T])
        mid = sb("mid", [P, 2, T])
        m_hi = sb("m_hi", [P, KI, T], F32R)
        m_lo = sb("m_lo", [P, KI, T], F32R)
        a_s = sb("a_s", [P, NC, HID])
        xn = sb("xn", [P, NC, HID])
        stats = sb("stats2", [P, NC, 6])
        mv = sb("mv2", [P, NC, 2])
        ve = sb("ve2", [P, NC])
        rstd = sb("rstd2", [P, NC])
        h2 = sb("h2", [P, KH, T])
        qn = sb("qn", [P, KH, T])
        q_t = sb("q_t", [P, KH, T], F32R)
        f_s = sb("f_s", [P, NC, HID])
        cg = [pb(f"cg{n}") for n in range(2)]
        cu = [pb(f"cu{n}") for n in range(2)]
        mo = [pb(f"mo{n}") for n in range(2)]
        mi = [pb(f"mi{n}") for n in range(2)]

        s = {n: ctx.enter_context(nc.semaphore("m_" + n)) for n in (
            "const_set consts small_loaded wu_loaded0 wu_loaded1 wd_loaded wf_loaded wu_head wu_ready wd_head "
            "wd_ready wf_step wf_ready o_loaded h_loaded x_loaded row_loaded x1_done ssq_done ms_done r2_done "
            "x1r_done bt_ready t_head t_ready c_ready gate_done mid_done head_done rest_done mo_ready a_done "
            "ga_done x2_done bn_done ve_done rstd_done xn_done dt_ready h2_done q_part q_done ff_ready f_done "
            "out_done out_stored").split()}
        block = ctx.enter_context(nc.Block())

        def run(eng, slot):
            slot(0, 0, 0)
            with eng.Fori(0, BATCH - 1) as b:
                for j in range(1, 1 + IPB):
                    slot(IPB * b + j, j, b)
            for j in range(1, 1 + IPB):
                slot(IPB * (BATCH - 1) + j, j, BATCH - 1)

        def known(i):
            return isinstance(i, int)

        def has(i):
            return not known(i) or 0 <= i < NI

        @block.sync
        def _(sp):
            def tokens(dram, i):
                return dram[bass.ds(i * T, T), :].rearrange("(c p) n -> p c n", p=P)

            def load_block(i, j):
                sp.dma_start(x1[:, j % 2, :, :], tokens(o_dram, i)).then_inc(s["o_loaded"], 16)
                sp.dma_start(hb[:, :, :], tokens(h_dram, i)).then_inc(s["h_loaded"], 16)

            def load_x(i, j):
                sp.dma_start(xb[:, j % 2, :, :], tokens(x, i)).then_inc(s["x_loaded"], 16)

            def load_rows(row):
                both = mod_dram.rearrange("b (g m n) -> b g m n", g=2, m=3)[bass.ds(row, 1), :, 2, :]
                sp.dma_start(rows[:, :, :], both.broadcast_to([P, 2, HID])).then_inc(s["row_loaded"], 16)

            sp.dma_start(ln2_c[:, :], ln2).then_inc(s["small_loaded"], 16)
            load_block(0, 0)
            load_x(0, 0)
            for bb in range(BATCH):
                for m, o in enumerate((3, 4)):
                    with nc.allow_non_contiguous_dma(reason="a few hundred numbers, once"):
                        sp.dma_start(cols[:, bb, m * KH:(m + 1) * KH],
                                     mod_dram[bb:bb + 1, o * HID:(o + 1) * HID].rearrange("b (k p) -> p (b k)", p=P)
                                     ).then_inc(s["small_loaded"], 16)
            for n in range(2 * INTER // T):
                if n >= 2:
                    sp.wait_ge(s["wu_ready"], KH * (n - 1))
                sp.dma_start(wu_st[:, n % 2, :, :], w_up.rearrange("(k p) n -> p k n", p=P)[:, :, n * T:(n + 1) * T]
                             ).then_inc(s[f"wu_loaded{n % 2}"], 16)
            sp.dma_start(wd_st[:, :, :], w_dn.rearrange("(k p) n -> p k n", p=P)).then_inc(s["wd_loaded"], 16)
            sp.dma_start(wf_st[:, :, :], w_ff.rearrange("(k p) n -> p k n", p=P)).then_inc(s["wf_loaded"], 16)
            sp.dma_start(rr_st[:, :, :], rram.rearrange("(k p) n -> p k n", p=P)).then_inc(s["wf_loaded"], 16)
            load_rows(0)

            def slot(i, j, row):
                new, nxt, old = has(i), has(i + 1), has(i - 1)
                if nxt:
                    if old:
                        wait_apart(sp, s["a_done"], 2 * i)
                    sp.wait_ge(s["x1_done"], i + 1)
                    load_block(i + 1, j + 1)
                if old:
                    sp.wait_ge(s["out_done"], i)
                    sp.dma_start(tokens(out, i - 1), a_s[:, :, :]).then_inc(s["out_stored"], 16)
                if nxt:
                    load_x(i + 1, j + 1)
                if old and new and j == IPB:
                    load_rows(row + 1)

            sp.sem_inc(s["out_stored"], 16)
            run(sp, slot)
            sp.wait_ge(s["out_stored"], 16 * (NI + 1))
            sp.wait_ge(s["row_loaded"], 16 * BATCH)

        @block.gpsimd
        def _(pool):
            pool.memset(ident[:, :], 0.0).then_inc(s["const_set"], 1)
            pool.memset(neg_half[:, :], -0.5).then_inc(s["consts"], 1)
            pool.wait_ge(s["const_set"], 1)
            pool.affine_select(out=ident[:, :], in_=ident[:, :], compare_op=ALU.not_equal, fill=1.0, base=0,
                               pattern=[[-1, P]], channel_multiplier=1).then_inc(s["consts"], 1)
            pool.wait_ge(s["consts"], 2)

            def residual(i, j):
                pool.wait_ge(s["o_loaded"], 16 * (i + 1))
                pool.wait_ge(s["h_loaded"], 16 * (i + 1))
                pool.tensor_tensor(x1[:, j % 2, :, :], x1[:, j % 2, :, :], hb[:, :, :], ALU.add).then_inc(s["x1_done"], 1)

            def rms_power(i):
                pool.wait_ge(s["ms_done"], i + 1)
                pool.tensor_tensor(r2[:, :], ms[:, :], neg_half[:, :], ALU.pow).then_inc(s["r2_done"], 1)

            residual(0, 0)
            rms_power(0)

            def slot(i, j, row):
                old = has(i - 1)
                if old:
                    p = (j - 1) % 2
                    pool.wait_ge(s["a_done"], 2 * i)
                    pool.wait_ge(s["row_loaded"], 16 * (row + 1))
                    pool.tensor_tensor(a_s[:, :, :], a_s[:, :, :], rows[:, 0:1, :].broadcast_to([P, NC, HID]), ALU.mult
                                       ).then_inc(s["ga_done"], 1)
                    pool.wait_ge(s["ga_done"], i)
                    pool.wait_ge(s["x_loaded"], 16 * i)
                    pool.tensor_tensor(xb[:, p, :, :], xb[:, p, :, :], a_s[:, :, :], ALU.add).then_inc(s["x2_done"], 1)
                    pool.wait_ge(s["ve_done"], i)
                    pool.tensor_tensor(rstd[:, :], ve[:, :], neg_half[:, :], ALU.pow).then_inc(s["rstd_done"], 1)
                if has(i + 1):
                    residual(i + 1, j + 1)
                    rms_power(i + 1)
                if old:
                    pool.wait_ge(s["f_done"], 2 * i)
                    pool.tensor_tensor(a_s[:, :, :], xb[:, p, :, :], f_s[:, :, :], ALU.add).then_inc(s["out_done"], 1)

            run(pool, slot)

        @block.scalar
        def _(act):
            def squares(i, j):
                act.wait_ge(s["x1_done"], i + 1)
                if j:
                    act.wait_ge(s["bt_ready"], 2 * i)
                for c in range(NC):
                    act.activation(x1r[:, c, :], x1[:, j % 2, c, :], ACT.Square, accum_out=ssq[:, c:c + 1]
                                   ).then_inc(s["ssq_done"], 1)

            def scale(i, j):
                act.wait_ge(s["r2_done"], i + 1)
                act.wait_ge(s["ssq_done"], 4 * i + 4)
                for c in range(NC):
                    act.activation(x1r[:, c, :], x1[:, j % 2, c, :], ACT.Copy, scale=r2[:, c:c + 1]
                                   ).then_inc(s["x1r_done"], 1)

            squares(0, 0)
            scale(0, 0)
            act.wait_ge(s["small_loaded"], 16 * 9)

            def slot(i, j, row):
                new = has(i)
                for t in range(KI):
                    if new:
                        n = KI * i + t
                        act.wait_ge(s["c_ready"], 2 * n + 1)
                        if t >= 2 or j:
                            act.wait_ge(s["mid_done"], n - 1)
                        act.activation(gate[:, t % 2, :], cg[t % 2][:, :], ACT.Silu).then_inc(s["gate_done"], 1)
                        act.wait_ge(s["mid_done"], n + 1)
                        if t == 0 and j:
                            act.wait_ge(s["mo_ready"], 2 * i)
                        act.activation(m_hi[:, t, :], mid[:, t % 2, :], ACT.Copy).then_inc(s["head_done"], 1)
                    if t == 2 and has(i + 1):
                        squares(i + 1, j + 1)
                    if t == 4 and has(i - 1):
                        for kk in range(KH):
                            wait_apart(act, s["dt_ready"], 2 * (i - 1) + kk + 1)
                            at = cols[:, bass.ds(row, 1), :].rearrange("p b k -> p (b k)")
                            act.activation(h2[:, kk, :], mi[kk][:, :], ACT.Identity, bias=at[:, kk:kk + 1],
                                           scale=at[:, KH + kk:KH + kk + 1]).then_inc(s["h2_done"], 1)
                    if t == 5 and has(i + 1):
                        scale(i + 1, j + 1)

            run(act, slot)

        @block.vector
        def _(dve):
            def mean_square(i):
                dve.wait_ge(s["ssq_done"], 4 * i + 4)
                dve.tensor_scalar(ms[:, :], ssq[:, :], 1.0 / HID, EPS, ALU.mult, ALU.add).then_inc(s["ms_done"], 1)

            mean_square(0)
            dve.wait_ge(s["small_loaded"], 16 * 9)
            for n in range(2 * INTER // T):
                dve.wait_ge(s[f"wu_loaded{n % 2}"], 16 * (n // 2 + 1))
                cut = slice(n * T, (n + 1) * T)
                for kk in range(KH):
                    dve.tensor_scalar(wu_hi[:, kk, cut], wu_st[:, n % 2, kk, :], ln2_c[:, kk:kk + 1], None, ALU.mult
                                      ).then_inc(s["wu_head"], 1)
                for kk in range(KH):
                    dve.wait_ge(s["wu_head"], KH * n + kk + 1)
                    dve.scalar_tensor_tensor(wu_lo[:, kk, cut], wu_st[:, n % 2, kk, :], ln2_c[:, kk:kk + 1],
                                             wu_hi[:, kk, cut].bitcast(F32), ALU.mult, ALU.subtract
                                             ).then_inc(s["wu_ready"], 1)
            dve.wait_ge(s["wd_loaded"], 16)
            dve.tensor_copy(wd_hi[:, :, :], wd_st[:, :, :]).then_inc(s["wd_head"], 1)
            dve.wait_ge(s["wd_head"], 1)
            dve.tensor_tensor(wd_lo[:, :, :], wd_st[:, :, :], wd_hi[:, :, :].bitcast(F32), ALU.subtract
                              ).then_inc(s["wd_ready"], 1)
            dve.wait_ge(s["wf_loaded"], 32)
            dve.tensor_scalar(wf_a[:, :, :], wf_st[:, :, :], THW, SCW, ALU.is_gt, ALU.mult).then_inc(s["wf_step"], 1)
            dve.tensor_scalar(wf_b[:, :, :], wf_st[:, :, :], -THW, SCW, ALU.is_lt, ALU.mult).then_inc(s["wf_step"], 1)
            dve.wait_ge(s["wf_step"], 2)
            dve.tensor_tensor(wf_a[:, :, :], wf_a[:, :, :], wf_b[:, :, :], ALU.subtract).then_inc(s["wf_step"], 1)
            dve.wait_ge(s["wf_step"], 3)
            dve.tensor_tensor(wf_a[:, :, :], wf_a[:, :, :], rr_st[:, :, :], ALU.add).then_inc(s["wf_step"], 1)
            dve.wait_ge(s["wf_step"], 4)
            dve.tensor_copy(wf_hi[:, :, :], wf_a[:, :, :]).then_inc(s["wf_step"], 1)
            dve.wait_ge(s["wf_step"], 5)
            dve.tensor_tensor(wf_lo[:, :, :], wf_a[:, :, :], wf_hi[:, :, :].bitcast(F32), ALU.subtract
                              ).then_inc(s["wf_ready"], 1)

            def split_tokens(i):
                for kk in range(KH):
                    dve.wait_ge(s["bt_ready"], 2 * i + kk + 1)
                    dve.tensor_copy(t_hi[:, kk, :], mi[kk][:, :]).then_inc(s["t_head"], 1)
                    dve.wait_ge(s["t_head"], 2 * i + kk + 1)
                    dve.tensor_tensor(t_lo[:, kk, :], mi[kk][:, :], t_hi[:, kk, :].bitcast(F32), ALU.subtract
                                      ).then_inc(s["t_ready"], 1)

            split_tokens(0)

            def slot(i, j, row):
                new, old = has(i), has(i - 1)
                if old:
                    p = (j - 1) % 2
                    for n in range(2):
                        dve.wait_ge(s["mo_ready"], 2 * (i - 1) + n + 1)
                        dve.wait_ge(s["out_stored"], 16 * i)
                        dve.tensor_tensor(a_s[:, 2 * n:2 * n + 2, :].rearrange("p c d -> p (c d)"),
                                          mo[n][:, :], x1[:, p, 2 * n:2 * n + 2, :].rearrange("p c d -> p (c d)"), ALU.add
                                          ).then_inc(s["a_done"], 1)
                for t in range(KI):
                    if new:
                        n = KI * i + t
                        dve.wait_ge(s["c_ready"], 2 * n + 2)
                        dve.wait_ge(s["gate_done"], n + 1)
                        if t >= 2 or j:
                            dve.wait_ge(s["rest_done"], n - 1)
                        dve.tensor_tensor(mid[:, t % 2, :], cu[t % 2][:, :], gate[:, t % 2, :], ALU.mult
                                          ).then_inc(s["mid_done"], 1)
                        if t:
                            rest(i, n - 1, t - 1)
                    if t == 1 and old:
                        dve.wait_ge(s["x2_done"], i)
                        for c in range(NC):
                            dve.bn_stats(stats[:, c, :], xb[:, p, c, :]).then_inc(s["bn_done"], 1)
                        wait_apart(dve, s["bn_done"], 8 * (i - 1) + 4)
                        for c in range(NC):
                            dve.bn_aggr(mv[:, c, :], stats[:, c, :]).then_inc(s["bn_done"], 1)
                        dve.wait_ge(s["bn_done"], 8 * i)
                        dve.tensor_scalar(ve[:, :], mv[:, :, 1], EPS, None, ALU.add).then_inc(s["ve_done"], 1)
                    if t == 3 and old:
                        dve.wait_ge(s["rstd_done"], i)
                        for c in range(NC):
                            dve.tensor_scalar(xn[:, c, :], xb[:, p, c, :], mv[:, c, 0:1], rstd[:, c:c + 1],
                                              ALU.subtract, ALU.mult).then_inc(s["xn_done"], 1)
                    if t == 3 and has(i + 1):
                        mean_square(i + 1)
                    if t == 5 and old:
                        dve.wait_ge(s["h2_done"], 2 * i)
                        dve.tensor_scalar(qn[:, :, :], h2[:, :, :], -THX, SCX, ALU.is_lt, ALU.mult).then_inc(s["q_part"], 1)
                        dve.tensor_scalar(h2[:, :, :], h2[:, :, :], THX, SCX, ALU.is_gt, ALU.mult).then_inc(s["q_part"], 1)
                        dve.wait_ge(s["q_part"], 2 * i)
                        dve.tensor_tensor(q_t[:, :, :], h2[:, :, :], qn[:, :, :], ALU.subtract).then_inc(s["q_done"], 1)
                if new:
                    rest(i, KI * i + KI - 1, KI - 1)
                if old:
                    for n in range(2):
                        dve.wait_ge(s["ff_ready"], 2 * (i - 1) + n + 1)
                        dve.tensor_tensor(f_s[:, 2 * n:2 * n + 2, :], mi[n][:, :].rearrange("p (c d) -> p c d", c=2),
                                          rows[:, 1:2, :].broadcast_to([P, 2, HID]), ALU.mult).then_inc(s["f_done"], 1)
                if has(i + 1):
                    split_tokens(i + 1)

            def rest(i, n, t):
                dve.wait_ge(s["head_done"], n + 1)
                dve.tensor_tensor(m_lo[:, t, :], mid[:, t % 2, :], m_hi[:, t, :].bitcast(F32), ALU.subtract
                                  ).then_inc(s["rest_done"], 1)

            run(dve, slot)

        @block.tensor
        def _(pe):
            pe.wait_ge(s["consts"], 2)

            def transpose_tokens(i):
                pe.wait_ge(s["x1r_done"], 4 * i + 4)
                for kk in range(KH):
                    for c in range(NC):
                        last = pe.transpose(mi[kk][:, c * CH:(c + 1) * CH], x1r[:, c, kk * P:(kk + 1) * P], ident[:, :])
                    last.then_inc(s["bt_ready"], 1)

            transpose_tokens(0)

            def slot(i, j, row):
                new, old = has(i), has(i - 1)
                for t in range(KI):
                    if new:
                        n = KI * i + t
                        if t == 0:
                            if j == 0:
                                pe.wait_ge(s["wu_ready"], KH * 2 * INTER // T)
                            pe.wait_ge(s["t_ready"], 2 * i + 2)
                        for bank, half in ((cg[t % 2], 0), (cu[t % 2], 1)):
                            if t >= 2 or j:
                                pe.wait_ge(s["mid_done" if half else "gate_done"], n - 1)
                            cut = slice((half * KI + t) * P, (half * KI + t + 1) * P)
                            first = True
                            for kk in range(KH):
                                for w, h in ((wu_hi, t_hi), (wu_hi, t_lo), (wu_lo, t_hi)):
                                    last = pe.matmul(bank[:, :], w[:, kk, cut], h[:, kk, :], start=first,
                                                     stop=(kk == KH - 1 and w is wu_lo))
                                    first = False
                            last.then_inc(s["c_ready"], 1)
                    if t == 4 and old:
                        pe.wait_ge(s["xn_done"], 4 * i)
                        for kk in range(KH):
                            for c in range(NC):
                                last = pe.transpose(mi[kk][:, c * CH:(c + 1) * CH], xn[:, c, kk * P:(kk + 1) * P], ident[:, :])
                            last.then_inc(s["dt_ready"], 1)
                if j == 0:
                    pe.wait_ge(s["wd_ready"], 1)
                    pe.wait_ge(s["wf_ready"], 1)
                if old:
                    pe.wait_ge(s["q_done"], i)
                    for n in range(2):
                        for c in range(2):
                            first = True
                            cut = slice((2 * n + c) * CH, (2 * n + c + 1) * CH)
                            for kk in range(KH):
                                for w in (wf_hi, wf_lo):
                                    last = pe.matmul(mi[n][:, c * HID:(c + 1) * HID], q_t[:, kk, cut], w[:, kk, :],
                                                     start=first, stop=(kk == KH - 1 and w is wf_lo))
                                    first = False
                        last.then_inc(s["ff_ready"], 1)
                if has(i + 1):
                    if old:
                        pe.wait_ge(s["f_done"], 2 * i)
                    else:
                        pe.wait_ge(s["t_ready"], 2)
                    transpose_tokens(i + 1)
                if new:
                    pe.wait_ge(s["rest_done"], KI * (i + 1))
                    if j:
                        pe.wait_ge(s["a_done"], 2 * i)
                    for n in range(2):
                        for c in range(2):
                            first = True
                            cut = slice((2 * n + c) * CH, (2 * n + c + 1) * CH)
                            for t in range(KI):
                                for m, w in ((m_hi, wd_hi), (m_hi, wd_lo), (m_lo, wd_hi)):
                                    last = pe.matmul(mo[n][:, c * HID:(c + 1) * HID], m[:, t, cut], w[:, t, :],
                                                     start=first, stop=(t == KI - 1 and m is m_lo))
                                    first = False
                        last.then_inc(s["mo_ready"], 1)

            run(pe, slot)


def adaln_mamba_block(nc, x, w_in, ln1, conv_w, conv_b, a_log, d_par, dt_bias, w_out, mnorm, c_t, w_mod,
                      w_up, w_dn, ln2, w_ff, rram, out):
    h_dram = nc.dram_tensor("h_scratch", [BATCH * SEQ, HID], F32).ap()
    o_dram = nc.dram_tensor("o_scratch", [BATCH * SEQ, HID], F32).ap()
    mod_dram = nc.dram_tensor("mod_scratch", [BATCH, MOD], F32).ap()
    mamba_phase(nc, x, w_in, ln1, conv_w, conv_b, a_log, d_par, dt_bias, w_out, mnorm, c_t, w_mod,
                h_dram, o_dram, mod_dram)
    mlp_phase(nc, x, w_up, w_dn, ln2, w_ff, rram, h_dram, o_dram, mod_dram, out)


def kernel(**inputs):
    import numpy as np
    import concourse.bacc as bacc
    from concourse.bass_utils import run_bass_kernel_spmd

    a = {name: np.asarray(value) for name, value in inputs.items()}

    def by_channel(v):
        return v.reshape((-1, P) + v.shape[1:]).swapaxes(0, 1)

    z0, x0, b0 = 0, DIN, 2 * DIN
    b_rows, c_rows, dt_rows = b0 + np.arange(NS), b0 + NS + np.arange(NS), b0 + 2 * NS + np.arange(HEADS)
    order = [c_rows, c_rows, b_rows, dt_rows, dt_rows]
    for st in range(SPI):
        step = np.arange(TPS * P) + TPS * P * st
        order += [x0 + step, z0 + step]
    order = np.concatenate(order)
    conv = np.concatenate([np.arange(DIN), c_rows - DIN, c_rows - DIN, b_rows - DIN, b_rows - DIN])
    arrays = dict(
        x=a["L0_attn_x"].reshape(BATCH * SEQ, HID),
        w_in=a["L0_attn_in_proj_w"][order].T,
        ln1=by_channel(a["L0_attn_ln1_w"]),
        conv_w=by_channel(a["L0_attn_conv_w"].reshape(-1, TAPS)[conv]),
        conv_b=by_channel(a["L0_attn_conv_b"][conv]),
        a_log=a["L0_attn_A_log"][None],
        d_par=by_channel(np.repeat(a["L0_attn_D_param"], HD)),
        dt_bias=a["L0_attn_dt_bias"][None],
        w_out=a["L0_attn_out_proj_w"].T,
        mnorm=by_channel(a["L0_attn_mnorm_w"]),
        c_t=by_channel(a["L0_c"].T),
        w_mod=a["L0_wmod"],
        w_up=a["L0_attn_mlp_in_w"].T,
        w_dn=a["L0_attn_mlp_out_w"].T,
        ln2=by_channel(a["L0_attn_ln2_w"]),
        w_ff=a["L0_ffn_weight"].T,
        rram=a["L0_ffn_rram_variation"].T,
    )
    arrays = {name: np.ascontiguousarray(v) for name, v in arrays.items()}
    nc = bacc.Bacc("TRN2", target_bir_lowering=False, num_devices=1, dynamic_dma_scratch_size=1024)
    args = [nc.dram_tensor(name, v.shape, F32, kind="ExternalInput").ap() for name, v in arrays.items()]
    out = nc.dram_tensor("out", (BATCH * SEQ, HID), F32, kind="ExternalOutput").ap()
    adaln_mamba_block(nc, *args, out)
    r = run_bass_kernel_spmd(nc, [arrays], core_ids=[0])
    return r.results[0]["out"].reshape(BATCH, SEQ, HID)
```

```python
from contextlib import ExitStack

import concourse.bass as bass
from concourse import mybir

F32 = mybir.dt.float32
F32R = mybir.dt.float32r
BF16 = mybir.dt.bfloat16
ALU = mybir.AluOpType
ACT = mybir.ActivationFunctionType

P = 128
HID = 256
KH = HID // P
BATCH, SEQ = 4, 1024
HEADS, HD, NS = 32, 64, 64
DIN = HEADS * HD
TAPS = 4
INTER = 1024
EPS = 1e-5
T = 512
CH = 128
NC = T // CH
IPB = SEQ // T
NI = BATCH * IPB
YT = DIN // P
TPS = 2
HPS = 2 * TPS
SPI = YT // TPS
SPB = SPI * IPB
NSTEP = SPB * BATCH
WT = 2 + 2 * YT
MOD = 6 * HID
THX, SCX, THW, SCW = 0.33, 0.5, 0.2, 0.6


def wait(eng, sem, value):
    if isinstance(value, int) and value <= 0:
        return
    eng.wait_ge(sem, value)


def wait_apart(eng, sem, value):
    if not isinstance(value, int):
        value = eng.to_reg(value)
        eng.wait_ge(sem, 1)
    eng.wait_ge(sem, value)


def mamba_phase(nc, x, w_in, ln1, conv_w, conv_b, a_log, d_par, dt_bias, w_out, mnorm, c_t, w_mod,
                h_dram, o_dram, mod_dram):
    ctx = ExitStack()
    with ctx:
        def sb(name, shape, dt=F32):
            return ctx.enter_context(nc.sbuf_tensor(name, shape, dt))

        def sem(name):
            return ctx.enter_context(nc.semaphore(name))

        inject = sb("inject", [P, NC, CH])
        ident = inject[:, 0, :]
        select = sb("select", [96, HEADS, P // 2], BF16)
        ones = sb("ones", [P, 1])
        neg_half = sb("neg_half", [P, NC])
        w_hi = sb("w_hi", [P, KH, WT * P], F32R)
        w_lo = sb("w_lo", [P, KH, WT * P], F32R)
        w_o = sb("w_o", [P, YT, HID])
        ln1_c = sb("ln1_c", [P, KH])
        mn_c = sb("mn_c", [P, YT])
        cw = sb("cw", [P, YT + 2, TAPS])
        cb = sb("cb", [P, YT + 2])
        dpar = sb("dpar", [P, YT])
        dtb = sb("dtb", [P, HEADS])
        neg_a = sb("neg_a", [P, HEADS])
        cs_t = sb("cs_t", [P, KH, BATCH])
        mod_row = sb("mod_row", [P, 2, HID])
        xt = sb("xt", [P, NC, HID])
        hs = sb("hs", [P, NC, HID])
        stats = sb("stats", [P, NC, 6])
        mv = sb("mv", [P, NC, 2])
        ve = sb("ve", [P, NC])
        rstd = sb("rstd", [P, NC])
        ssq = sb("ssq", [P, NC])
        ms = sb("ms", [P, NC])
        r1 = sb("r1", [P, NC])
        h_hi = sb("h_hi", [P, KH, T], F32R)
        h_lo = sb("h_lo", [P, KH, T], F32R)
        raw = sb("raw", [P, 2, TAPS - 1 + T])
        tail = sb("tail", [P, YT + 2, TAPS - 1])
        xc = sb("xc", [P, 2, TPS, T])
        cc = sb("cc", [P, 2, T])
        bb = sb("bb", [NS, T])
        u_t = hs[:, :, 0 * HEADS:1 * HEADS]
        a_t = hs[:, :, 1 * HEADS:2 * HEADS]
        e_t = hs[:, :, 2 * HEADS:3 * HEADS]
        l_t = hs[:, :, 3 * HEADS:4 * HEADS]
        m_t = hs[:, :, 4 * HEADS:5 * HEADS]
        dt_s = sb("dt_s", [P, 2, NC, HEADS])
        tl = sb("tl", [96, 2, T])
        zero = sb("zero", [HEADS, CH])
        parts = sb("parts", [96, 2, T], BF16)
        g_s = sb("g_s", [P, 2, NC, CH])
        b_tok = sb("b_tok", [P, 2, NC, NS])
        xdt = sb("xdt", [P, 2, NC, TPS * P])
        xw = sb("xw", [P, NC, TPS * P])
        dec = sb("dec", [P, 2, HPS, T])
        w_end = sb("w_end", [P, 2, NC, HPS])
        p_end = sb("p_end", [P, TPS, NC])
        cp = sb("cp", [P, TPS, T])
        state = sb("state", [P, SPI, TPS, HD])
        s_ch = sb("s_ch", [P, NC - 1, TPS, HD])
        s_blk = sb("s_blk", [P, NC, TPS, P])
        yb = sb("yb", [P, YT, T])
        sq = sb("sq", [P, T])
        acc = sb("acc", [P, T])
        o_acc = sb("o_acc", [P, NC, HID])
        o_ms = sb("o_ms", [P, NC])
        r_y = sb("r_y", [P, NC])
        stages = [dec[:, n // HPS, n % HPS, :].rearrange("p (k n) -> p k n", k=KH) for n in range(2 * HPS)]
        wm = yb[:, 0:KH * MOD // T, :].rearrange("p a t -> p (a t)")
        mod_s = yb[0:BATCH, 8:11, :].rearrange("p a t -> p (a t)")
        mod_a = yb[0:BATCH, 11:14, :].rearrange("p a t -> p (a t)")

        pj = [ctx.enter_context(nc.psum_tensor(f"pj{i}", [P, T], F32)) for i in range(2)]
        da = [ctx.enter_context(nc.psum_tensor(f"da{i}", [P, T], F32)) for i in range(2)]
        yp = [ctx.enter_context(nc.psum_tensor(f"yp{i}", [P, T], F32)) for i in range(2)]
        ma = ctx.enter_context(nc.psum_tensor("ma", [P, T], F32))
        mb = ctx.enter_context(nc.psum_tensor("mb", [P, T], F32))

        s = {n: sem(n) for n in (
            "const_set consts mod_in_loaded small_loaded c_silu w_head mod_sign mod_ready mod_fix mod_stored wo_loaded "
            "w_ready wo_ready neg_a_ready misc_set "
            "x_loaded row_loaded bn_done ve_done rstd_done xn_done h_done h_stored ssq_done ms_done r1_done "
            "hs_done ht_ready hh_done hl_done "
            "pj_ready pj_taken halo_done conv_tap x_ready bc_tap bc_halo bc_ready dt_copied "
            "dtt_ready u_done a_done e_done l_done dtc dt_done da_exp dat_ready dat_taken parts_done "
            "g_ready g_taken bt_ready bt_taken "
            "xt_ready xdt_done da_ready scan_done wend_done pend_done cp_done xw_done m_done "
            "ds_ready chain_done blk_done y_ready skip_done gate_done sq_done acc_done "
            "o_ready o_taken q_ready oms_done ry_done o_scaled o_stored").split()}

        w_loaded = [sem(f"w_loaded{n}") for n in range(len(stages))]

        def tile_count(i, idx):
            return WT * i + idx + 1

        class At:

            def __init__(self, b, j):
                self.k = SPB * b + j if not isinstance(b, int) or b else j
                self.js = j % SPB
                self.i = IPB * b + j // SPI if not isinstance(b, int) or b else j // SPI
                self.q = (j // SPI) % IPB
                self.st = j % SPI
                self.b = b

        block = ctx.enter_context(nc.Block())

        HEAD = 5
        TAIL = SPB + HEAD

        def run(eng, slot):
            for j in range(HEAD):
                slot(0, j)
            with eng.Fori(0, BATCH - 1) as b:
                for j in range(HEAD, HEAD + SPB):
                    slot(b, j)
            for j in range(HEAD, TAIL):
                slot(BATCH - 1, j)

        def exists(b, j, back):
            if isinstance(b, int):
                return 0 <= SPB * b + j - back < NSTEP
            return True

        def out_piece(b, j):
            at = At(b, j)
            if at.st >= 5:
                return (0, at.st - 5, at.i) if exists(b, j, 0) else None
            if exists(b, j, SPI):
                return (0, 3, at.i - 1) if at.st == 0 else (1, at.st - 1, at.i - 1)
            return None

        def piece_count(b, j):
            half, c, i = out_piece(b, j)
            return 2 * NC * i + NC * half + c + 1

        def blk_count(b, j):
            base = (2 * SPB + 2 * SPI) * b if not isinstance(b, int) or b else 0
            full = j // SPB
            js = j % SPB
            return base + (2 * SPB + 2 * SPI) * full + 2 * (js + 1) + 2 * max(0, js + 1 - SPI)

        @block.sync
        def _(sp):
            sp.sem_inc(s["o_stored"], 16)
            sp.dma_start(cs_t[:, :, :], c_t).then_inc(s["mod_in_loaded"], 16)
            sp.dma_start(wm.rearrange("p (k n) -> p k n", k=KH), w_mod.rearrange("(k p) n -> p k n", p=P)
                         ).then_inc(s["mod_in_loaded"], 16)
            sp.dma_start(xt[:, :, :], x[0:T, :].rearrange("(c p) n -> p c n", p=P)).then_inc(s["x_loaded"], 16)
            for dst, src in ((ln1_c[:, :], ln1),
                             (neg_a[:, :], a_log.broadcast_to([P, HEADS])),
                             (cw[:, :, :], conv_w),
                             (cb[:, :], conv_b),
                             (dpar[:, :], d_par),
                             (dtb[:, :], dt_bias.broadcast_to([P, HEADS])),
                             (mn_c[:, :], mnorm)):
                sp.dma_start(dst, src).then_inc(s["small_loaded"], 16)

            def load_weights(n):
                sp.dma_start(stages[n % len(stages)],
                             w_in.rearrange("(k p) n -> p k n", p=P)[:, :, n * 2 * P:(n + 1) * 2 * P]
                             ).then_inc(w_loaded[n % len(stages)], 16)

            for n in range(len(stages)):
                load_weights(n)
            sp.wait_ge(s["mod_fix"], 2)
            sp.dma_start(mod_dram[:, 0:2 * HID], mod_s[:, 0:2 * HID]).then_inc(s["mod_stored"], 16)
            sp.wait_ge(s["mod_stored"], 16)
            sp.dma_start(mod_row[:, :, :].rearrange("p a n -> p (a n)"),
                         mod_dram[0:1, 0:2 * HID].broadcast_to([P, 2 * HID])).then_inc(s["row_loaded"], 16)
            for n in range(len(stages), WT // 2):
                sp.wait_ge(s["w_ready"], KH * (n - len(stages) + 1))
                load_weights(n)
            sp.wait_ge(s["mod_fix"], 7)
            sp.dma_start(mod_dram[:, 2 * HID:], mod_s[:, 2 * HID:]).then_inc(s["mod_stored"], 16)
            sp.dma_start(w_o[:, :, :], w_out.rearrange("(t p) n -> p t n", p=P)).then_inc(s["wo_loaded"], 16)
            def store_h(i):
                sp.wait_ge(s["h_done"], 2 * i + 2)
                sp.dma_start(h_dram[bass.ds(i * T, T), :].rearrange("(c p) n -> p c n", p=P), xt[:, :, :]
                             ).then_inc(s["h_stored"], 16)

            store_h(0)

            def slot(b, j):
                at = At(b, j)
                if at.st == 1 and exists(b, j, at.st - SPI):
                    nxt = at.i + 1
                    wait_apart(sp, s["h_stored"], 16 * nxt)
                    sp.wait_ge(s["hs_done"], 4 * nxt)
                    sp.dma_start(xt[:, :, :], x[bass.ds(nxt * T, T), :].rearrange("(c p) n -> p c n", p=P)
                                 ).then_inc(s["x_loaded"], 16)
                    if at.q == IPB - 1:
                        row = at.b + 1 + (j // SPB)
                        sp.wait_ge(s["h_done"], 2 * nxt)
                        sp.dma_start(mod_row[:, :, :].rearrange("p a n -> p (a n)"),
                                     mod_dram[bass.ds(row, 1), 0:2 * HID].broadcast_to([P, 2 * HID])
                                     ).then_inc(s["row_loaded"], 16)
                if at.st == 5 and exists(b, j, at.st - SPI):
                    store_h(at.i + 1)
                if at.st == 4 and exists(b, j, 5):
                    if not isinstance(b, int) or b or j >= SPI:
                        sp.wait_ge(s["o_scaled"], 4 * at.i)
                        sp.dma_start(o_dram[bass.ds((at.i - 1) * T, T), :].rearrange("(c p) n -> p c n", p=P),
                                     o_acc[:, :, :]).then_inc(s["o_stored"], 16)

            run(sp, slot)
            sp.wait_ge(s["o_stored"], 16 * (NI + 1))
            sp.wait_ge(s["h_stored"], 16 * NI)

        @block.gpsimd
        def _(pool):
            pool.memset(inject[:, :, :], 0.0).then_inc(s["const_set"], 1)
            pool.memset(select[:, :, :], 0.0).then_inc(s["const_set"], 1)
            pool.memset(ones[:, :], 1.0).then_inc(s["consts"], 1)
            pool.memset(neg_half[:, :], -0.5).then_inc(s["consts"], 1)
            pool.memset(zero[:, :], 0.0).then_inc(s["consts"], 1)
            pool.memset(s_blk[:, :, :, :], 0.0).then_inc(s["consts"], 1)
            pool.wait_ge(s["const_set"], 2)
            pool.affine_select(out=inject[:, :, :], in_=inject[:, :, :], compare_op=ALU.not_equal, fill=1.0, base=0,
                               pattern=[[0, NC], [-1, CH]], channel_multiplier=1).then_inc(s["consts"], 1)
            for r in range(3):
                third = select[32 * r:32 * r + 32, :, :]
                pool.wait_ge(s["consts"], 5 + r)
                pool.affine_select(out=third, in_=third, compare_op=ALU.not_equal, fill=1.0, base=0,
                                   pattern=[[-1, HEADS], [0, P // 2]], channel_multiplier=1).then_inc(s["consts"], 1)
            pool.wait_ge(s["consts"], 8)

            def norm_power(i):
                pool.wait_ge(s["ve_done"], i + 1)
                if not isinstance(i, int) or i:
                    pool.wait_ge(s["xn_done"], 4 * i)
                pool.tensor_tensor(rstd[:, :], ve[:, :], neg_half[:, :], ALU.pow).then_inc(s["rstd_done"], 1)

            def modulate(i, row, part):
                if part == 0:
                    pool.wait_ge(s["xn_done"], 4 * i + 4)
                    pool.wait_ge(s["row_loaded"], 16 * (row + 1))
                    pool.tensor_tensor(xt[:, :, :], xt[:, :, :], mod_row[:, 1:2, :].broadcast_to([P, NC, HID]), ALU.mult
                                       ).then_inc(s["h_done"], 1)
                else:
                    pool.wait_ge(s["h_done"], 2 * i + 1)
                    pool.tensor_tensor(xt[:, :, :], xt[:, :, :], mod_row[:, 0:1, :].broadcast_to([P, NC, HID]), ALU.add
                                       ).then_inc(s["h_done"], 1)

            def rms_power(i):
                pool.wait_ge(s["ms_done"], i + 1)
                if not isinstance(i, int) or i:
                    pool.wait_ge(s["hs_done"], 4 * i)
                pool.tensor_tensor(r1[:, :], ms[:, :], neg_half[:, :], ALU.pow).then_inc(s["r1_done"], 1)

            norm_power(0)
            modulate(0, 0, 0)
            modulate(0, 0, 1)
            rms_power(0)

            def slot(b, j):
                at = At(b, j)
                k = at.k
                nxt = exists(b, j, at.st - SPI)
                new, mid, old = exists(b, j, 0), exists(b, j, 1), exists(b, j, 2)
                m = At(b, j - 1)
                buf = m.js % 2

                def decay_matrix(h):
                    d = dec[:, buf, h, :]
                    pool.tensor_tensor(d, d, g_s[:, m.q, :, :].rearrange("p c t -> p (c t)"), ALU.mult
                                       ).then_inc(s["m_done"], 1)

                def add_squares(t):
                    o = At(b, j - 3)
                    wait_apart(pool, s["sq_done"], 2 * (k - 3) + t + 1)
                    if o.st == 0 and t == 0:
                        if not isinstance(b, int) or k >= SPI:
                            wait_apart(pool, s["q_ready"], o.i)
                        pool.tensor_copy(acc[:, :], sq[:, :]).then_inc(s["acc_done"], 1)
                    else:
                        pool.wait_ge(s["acc_done"], 2 * (k - 3) + t)
                        pool.tensor_tensor(acc[:, :], acc[:, :], sq[:, :], ALU.add).then_inc(s["acc_done"], 1)

                def gate(t):
                    o = At(b, j - 2)
                    pool.wait_ge(s["skip_done"], 2 * (k - 2) + t + 1)
                    pool.wait_ge(s["pj_taken"], tile_count(o.i, 4 + 4 * o.st + t))
                    ytile = yb[:, TPS * o.st + t, :]
                    pool.tensor_tensor(ytile, ytile, xc[:, o.js % 2, t, :], ALU.mult).then_inc(s["gate_done"], 1)

                if mid:
                    pool.wait_ge(s["g_taken"], m.i + 1)
                    pool.wait_ge(s["wend_done"], 2 * (k - 1) + 1)
                    decay_matrix(0)
                if nxt and at.st == 7:
                    rms_power(at.i + 1)
                if exists(b, j, 3):
                    add_squares(0)
                if old:
                    gate(0)
                if exists(b, j, 3):
                    add_squares(1)
                if mid:
                    pool.wait_ge(s["wend_done"], 2 * k)
                    pool.wait_ge(s["xdt_done"], 2 * k)
                    if old:
                        pool.wait_ge(s["ds_ready"], k - 1)
                    pool.tensor_tensor(
                        xw[:, :, :].rearrange("p c (h d) -> p (c h) d", d=HD),
                        xdt[:, buf, :, :].rearrange("p c (h d) -> p (c h) d", d=HD),
                        w_end[:, buf, :, :].rearrange("p c h -> p (c h)").unsqueeze(2).broadcast_to([P, NC * HPS, HD]),
                        ALU.mult).then_inc(s["xw_done"], 1)
                if old:
                    gate(1)
                if nxt and at.st == 3:
                    norm_power(at.i + 1)
                if mid:
                    for h in range(1, HPS):
                        decay_matrix(h)
                if nxt and at.st in (4, 5):
                    modulate(at.i + 1, at.b + ((j // SPI + 1) // IPB), at.st - 4)
                if at.st == 3 and exists(b, j, 4) and (not isinstance(b, int) or k >= SPI):
                    pool.wait_ge(s["oms_done"], at.i)
                    pool.tensor_tensor(r_y[:, :], o_ms[:, :], neg_half[:, :], ALU.pow).then_inc(s["ry_done"], 1)

            run(pool, slot)

        @block.scalar
        def _(act):
            act.wait_ge(s["mod_in_loaded"], 16 * 2)
            act.activation(cs_t[:, :, :], cs_t[:, :, :], ACT.Silu).then_inc(s["c_silu"], 1)
            act.wait_ge(s["small_loaded"], 16 * 7)
            act.activation(neg_a[:, :], neg_a[:, :], ACT.Exp).then_inc(s["neg_a_ready"], 1)
            act.wait_ge(s["neg_a_ready"], 1)
            act.mul(neg_a[:, :], neg_a[:, :], -1.0).then_inc(s["neg_a_ready"], 1)
            for n in range(WT // 2):
                act.wait_ge(w_loaded[n % len(stages)], 16 * (n // len(stages) + 1))
                for kk in range(KH):
                    act.activation(w_hi[:, kk, n * 2 * P:(n + 1) * 2 * P], stages[n % len(stages)][:, kk, :], ACT.Copy,
                                   scale=ln1_c[:, kk:kk + 1]).then_inc(s["w_head"], 1)

            def squares(i):
                act.wait_ge(s["h_done"], 2 * i + 2)
                for c in range(NC):
                    act.activation(hs[:, c, :], xt[:, c, :], ACT.Square, accum_out=ssq[:, c:c + 1]
                                   ).then_inc(s["ssq_done"], 1)

            def scale_h(i):
                act.wait_ge(s["r1_done"], i + 1)
                act.wait_ge(s["ssq_done"], 4 * i + 4)
                for c in range(NC):
                    act.activation(hs[:, c, :], xt[:, c, :], ACT.Copy, scale=r1[:, c:c + 1]).then_inc(s["hs_done"], 1)

            squares(0)
            scale_h(0)
            act.wait_ge(s["wo_loaded"], 16)
            for t in range(YT):
                act.activation(w_o[:, t, :], w_o[:, t, :], ACT.Copy, scale=mn_c[:, t:t + 1]).then_inc(s["wo_ready"], 1)

            def start_bc(b, j, i, q):
                for n, rows, ch, dst in ((0, NS, YT + 1, bb[:, :]), (1, P, YT, cc[:, q, :])):
                    act.wait_ge(s["pj_ready"], tile_count(i, n))
                    if j is not None:
                        k = At(b, j).k
                        act.wait_ge(s["conv_tap"], 6 * k + 5 + n)
                        act.wait_ge(s["halo_done"], 4 * k + 4)
                    if n == 0:
                        act.activation(tl[64:96, 0, :], pj[n][64:96, :], ACT.Copy).then_inc(s["dt_copied"], 1)
                    act.activation(raw[0:rows, n, TAPS - 1:], pj[n][0:rows, :], ACT.Copy).then_inc(s["misc_set"], 1)
                    act.activation(dst, pj[n][0:rows, :], ACT.Identity,
                                   bias=cb[0:rows, ch:ch + 1], scale=cw[0:rows, ch, TAPS - 1:TAPS]
                                   ).then_inc(s["pj_taken"], 1)

            def softplus_parts(i):
                act.wait_ge(s["a_done"], i + 1)
                act.activation(e_t[:, :, :], a_t[:, :, :], ACT.Exp, scale=-1.0).then_inc(s["e_done"], 1)
                act.wait_ge(s["e_done"], i + 1)
                act.activation(l_t[:, :, :], e_t[:, :, :], ACT.Ln, bias=1.0).then_inc(s["l_done"], 1)

            start_bc(0, None, 0, 0)
            softplus_parts(0)

            def slot(b, j):
                at = At(b, j)
                k = at.k
                new, mid, old = exists(b, j, 0), exists(b, j, 1), exists(b, j, 2)
                nxt = exists(b, j, at.st - SPI)
                for t in range(TPS):
                    if exists(b, j, 3):
                        o = At(b, j - 3)
                        act.wait_ge(s["gate_done"], 2 * (k - 3) + t + 1)
                        wait(act, s["acc_done"], 2 * (k - 3) + t)
                        act.activation(sq[:, :], yb[:, TPS * o.st + t, :], ACT.Square).then_inc(s["sq_done"], 1)
                    if new and at.st == 0 and t == 0:
                        act.wait_ge(s["dtc"], 8 * at.i + 8)
                        act.activation(a_t[:, :, :], a_t[:, :, :], ACT.Exp).then_inc(s["da_exp"], 1)
                if new and at.st == 0:
                    for n, dst in ((0, bb[:, :]), (1, cc[:, at.q, :])):
                        act.wait_ge(s["bc_tap"], 6 * at.i + 5 + n)
                        act.activation(dst, dst, ACT.Silu).then_inc(s["bc_ready"], 1)
                if mid and At(b, j - 1).q:
                    m = At(b, j - 1)
                    act.wait_ge(s["y_ready"], 2 * (k - 1))
                    for half in range(2):
                        r = slice(64 * half, 64 * half + 64)
                        act.activation(s_blk[r, 0, :, 64 * half:64 * half + 64], state[r, m.st, :, :], ACT.Copy
                                       ).then_inc(s["blk_done"], 1)
                if nxt and at.st == 7:
                    scale_h(at.i + 1)
                if isinstance(b, int) and k == HEAD - 1:
                    act.wait_ge(s["mod_stored"], 32)
                if new:
                    for t in range(TPS):
                        idx = 2 + 4 * at.st + t
                        ch = TPS * at.st + t
                        act.wait_ge(s["pj_ready"], tile_count(at.i, idx))
                        if at.st == 0:
                            act.wait_ge(s["bc_tap"], 6 * at.i + 5 + t)
                            act.wait_ge(s["bc_halo"], 4 * at.i + 4)
                        else:
                            act.wait_ge(s["conv_tap"], 6 * (k - 1) + 5 + t)
                            act.wait_ge(s["halo_done"], 4 * k)
                        act.activation(raw[:, t, TAPS - 1:], pj[idx % 2][:, :], ACT.Copy).then_inc(s["misc_set"], 1)
                        if old:
                            act.wait_ge(s["gate_done"], 2 * (k - 2) + t + 1)
                        act.activation(xc[:, at.js % 2, t, :], pj[idx % 2][:, :], ACT.Identity,
                                       bias=cb[:, ch:ch + 1], scale=cw[:, ch, TAPS - 1:TAPS]).then_inc(s["pj_taken"], 1)

                def lay_out_states():
                    wait(act, s["y_ready"], 2 * (k - 1))
                    act.wait_ge(s["chain_done"], 8 * (k - 1) + 6)
                    for half in range(2):
                        r = slice(64 * half, 64 * half + 64)
                        dst = s_blk[r, 1:NC, :, 64 * half:64 * half + 64].rearrange("p c a d -> p (c a) d")
                        act.activation(dst, s_ch[r, :, :, :].rearrange("p c a d -> p (c a) d"), ACT.Copy
                                       ).then_inc(s["blk_done"], 1)

                if mid and at.st != 7:
                    lay_out_states()
                if new:
                    for t in range(TPS):
                        idx = 4 + 4 * at.st + t
                        act.wait_ge(s["pj_ready"], tile_count(at.i, idx))
                        act.activation(yb[:, TPS * at.st + t, :], pj[idx % 2][:, :], ACT.Silu).then_inc(s["pj_taken"], 1)
                if mid and at.st == 7:
                    lay_out_states()
                if nxt and at.st == 6:
                    squares(at.i + 1)
                if new:
                    for t in range(TPS):
                        act.wait_ge(s["conv_tap"], 6 * k + 5 + t)
                        act.activation(xc[:, at.js % 2, t, :], xc[:, at.js % 2, t, :], ACT.Silu).then_inc(s["x_ready"], 1)
                if nxt and at.st == 7:
                    start_bc(b, j, at.i + 1, (at.q + 1) % IPB)
                    softplus_parts(at.i + 1)

            run(act, slot)

        @block.vector
        def _(dve):
            def token_norm_a(i):
                dve.wait_ge(s["x_loaded"], 16 * (i + 1))
                for c in range(NC):
                    dve.bn_stats(stats[:, c, :], xt[:, c, :]).then_inc(s["bn_done"], 1)
                wait_apart(dve, s["bn_done"], 8 * i + 4)
                for c in range(NC):
                    dve.bn_aggr(mv[:, c, :], stats[:, c, :]).then_inc(s["bn_done"], 1)
                dve.wait_ge(s["bn_done"], 8 * i + 8)
                dve.tensor_scalar(ve[:, :], mv[:, :, 1], EPS, None, ALU.add).then_inc(s["ve_done"], 1)

            def token_norm_b(i):
                dve.wait_ge(s["rstd_done"], i + 1)
                for c in range(NC):
                    dve.tensor_scalar(xt[:, c, :], xt[:, c, :], mv[:, c, 0:1], rstd[:, c:c + 1], ALU.subtract, ALU.mult
                                      ).then_inc(s["xn_done"], 1)

            def token_ms(i):
                dve.wait_ge(s["ssq_done"], 4 * i + 4)
                dve.tensor_scalar(ms[:, :], ssq[:, :], 1.0 / HID, EPS, ALU.mult, ALU.add).then_inc(s["ms_done"], 1)

            token_norm_a(0)
            token_norm_b(0)

            def take_mod(n, bank):
                dve.wait_ge(s["mod_ready"], n + 1)
                dve.tensor_copy(mod_s[:, n * T:(n + 1) * T], bank[0:BATCH, :]).then_inc(s["mod_fix"], 1)

            def add_one(o):
                dve.tensor_scalar(mod_s[:, o * HID:(o + 1) * HID], mod_s[:, o * HID:(o + 1) * HID], 1.0, None, ALU.add
                                  ).then_inc(s["mod_fix"], 1)

            take_mod(0, ma)
            dve.wait_ge(s["mod_fix"], 1)
            add_one(1)
            take_mod(1, mb)
            take_mod(2, yp[0])
            dve.wait_ge(s["mod_fix"], 4)
            add_one(4)
            for n, o in enumerate((2, 5)):
                g = mod_s[:, o * HID:(o + 1) * HID]
                mag = mod_a[:, 2 * n * HID:(2 * n + 1) * HID]
                sgn = mod_a[:, (2 * n + 1) * HID:(2 * n + 2) * HID]
                dve.scalar_tensor_tensor(mag, g, -1.0, g, ALU.mult, ALU.max).then_inc(s["mod_sign"], 1)
                dve.wait_ge(s["mod_sign"], 3 * n + 1)
                dve.tensor_scalar(mag, mag, 0.25, None, ALU.max).then_inc(s["mod_sign"], 1)
                dve.tensor_scalar(sgn, g, 0.0, 2.0, ALU.is_ge, ALU.mult).then_inc(s["mod_sign"], 1)
                dve.wait_ge(s["mod_sign"], 3 * n + 3)
                dve.scalar_tensor_tensor(g, sgn, -1.0, mag, ALU.add, ALU.mult).then_inc(s["mod_fix"], 1)
            for n in range(WT // 2):
                for kk in range(KH):
                    dve.wait_ge(s["w_head"], KH * n + kk + 1)
                    dve.scalar_tensor_tensor(w_lo[:, kk, n * 2 * P:(n + 1) * 2 * P], stages[n % len(stages)][:, kk, :],
                                             ln1_c[:, kk:kk + 1], w_hi[:, kk, n * 2 * P:(n + 1) * 2 * P].bitcast(F32),
                                             ALU.mult, ALU.subtract).then_inc(s["w_ready"], 1)
            token_ms(0)

            def conv_pair(tiles, halo, taps, halo0, tap0, q, between=None):
                if q:
                    dve.wait_ge(halo, halo0)
                for n, (ch, rows, dst) in enumerate(tiles):
                    if q == 0:
                        dve.memset(raw[0:rows, n, 0:TAPS - 1], 0.0).then_inc(halo, 1)
                    else:
                        dve.tensor_copy(raw[0:rows, n, 0:TAPS - 1], tail[0:rows, ch, :]).then_inc(halo, 1)
                for k in range(TAPS - 1):
                    if between and k == TAPS - 2:
                        between()
                    for n, (ch, rows, dst) in enumerate(tiles):
                        dve.wait_ge(halo if k == 0 else taps,
                                    halo0 + n + 1 if k == 0 else tap0 + 2 * (k - 1) + n + 1)
                        dve.scalar_tensor_tensor(dst, raw[0:rows, n, k:k + T], cw[0:rows, ch, k:k + 1], dst,
                                                 ALU.mult, ALU.add).then_inc(taps, 1)
                for n, (ch, rows, dst) in enumerate(tiles):
                    dve.tensor_copy(tail[0:rows, ch, :], raw[0:rows, n, T:T + TAPS - 1]).then_inc(halo, 1)

            def conv_bc(i, q):
                dve.wait_ge(s["pj_taken"], tile_count(i, 1))
                conv_pair([(YT + 1, NS, bb[:, :]), (YT, P, cc[:, q, :])], s["bc_halo"], s["bc_tap"], 4 * i, 6 * i, q)

            def split_tokens(i):
                for kk, bank in ((0, pj[0]), (1, pj[1])):
                    dve.wait_ge(s["ht_ready"], 2 * i + kk + 1)
                    wait(dve, s["pj_ready"], WT * i)
                    dve.tensor_copy(h_hi[:, kk, :], bank[:, :]).then_inc(s["hh_done"], 1)
                    dve.wait_ge(s["hh_done"], 2 * i + kk + 1)
                    dve.tensor_tensor(h_lo[:, kk, :], bank[:, :], h_hi[:, kk, :].bitcast(F32), ALU.subtract
                                      ).then_inc(s["hl_done"], 1)

            def time_step_input(i):
                dve.wait_ge(s["dtt_ready"], i + 1)
                dve.tensor_tensor(u_t[:, :, :], mb[:, 0:NC * HEADS].rearrange("p (c h) -> p c h", c=NC),
                                  dtb[:, :].unsqueeze(1).broadcast_to([P, NC, HEADS]), ALU.add).then_inc(s["u_done"], 1)
                dve.wait_ge(s["u_done"], i + 1)
                dve.scalar_tensor_tensor(a_t[:, :, :], u_t[:, :, :], -1.0, u_t[:, :, :], ALU.mult, ALU.max).then_inc(s["a_done"], 1)

            def time_steps(i, q):
                c0 = 8 * i

                def link(n, ins):
                    ins.then_inc(s["dtc"], 1)
                    dve.wait_ge(s["dtc"], c0 + n)

                dve.wait_ge(s["l_done"], i + 1)
                link(1, dve.tensor_scalar(m_t[:, :, :], e_t[:, :, :], 1.0, 1.0, ALU.add, ALU.is_equal))
                dve.tensor_tensor(l_t[:, :, :], l_t[:, :, :], m_t[:, :, :], ALU.add).then_inc(s["dtc"], 1)
                link(3, dve.tensor_scalar(a_t[:, :, :], e_t[:, :, :], 1.0, 1.0, ALU.add, ALU.subtract))
                link(4, dve.tensor_tensor(a_t[:, :, :], a_t[:, :, :], m_t[:, :, :], ALU.add))
                dve.tensor_tensor(l_t[:, :, :], l_t[:, :, :], e_t[:, :, :], ALU.mult).then_inc(s["dtc"], 1)
                link(6, dve.reciprocal(m_t[:, :, :], a_t[:, :, :]))
                link(7, dve.tensor_tensor(l_t[:, :, :], l_t[:, :, :], m_t[:, :, :], ALU.mult))
                dve.scalar_tensor_tensor(dt_s[:, q, :, :], u_t[:, :, :], 0.0, l_t[:, :, :], ALU.max, ALU.add
                                         ).then_inc(s["dt_done"], 1)
                dve.wait_ge(s["dt_done"], i + 1)
                dve.tensor_tensor(a_t[:, :, :], dt_s[:, q, :, :], neg_a[:, :].unsqueeze(1).broadcast_to([P, NC, HEADS]),
                                  ALU.mult).then_inc(s["dtc"], 1)

            def decays(i, q, k):
                dve.wait_ge(s["dat_ready"], i + 1)
                dve.tensor_copy(tl[0:32, 0, :], mb[0:32, :]).then_inc(s["dat_taken"], 1)
                dve.wait_ge(s["dat_taken"], 6 * i + 1)
                for c in range(NC):
                    dve.tensor_tensor_scan(tl[0:32, 1, c * CH:(c + 1) * CH], tl[0:32, 0, c * CH:(c + 1) * CH], zero[:, :],
                                           1.0, ALU.mult, ALU.add).then_inc(s["dat_taken"], 1)
                dve.wait_ge(s["dat_taken"], 6 * i + 5)
                dve.memset(tl[0:32, 0, 0::CH], 0.0).then_inc(s["dat_taken"], 1)
                dve.wait_ge(s["dat_taken"], 6 * i + 6)
                wait(dve, s["da_ready"], 6 * k)

                def link_part(n, ins):
                    ins.then_inc(s["parts_done"], 1)
                    dve.wait_ge(s["parts_done"], 5 * i + n)

                link_part(1, dve.tensor_copy(parts[0:32, :, :], tl[0:32, :, :]))
                link_part(2, dve.tensor_tensor(tl[32:64, :, :], tl[0:32, :, :], parts[0:32, :, :], ALU.subtract))
                link_part(3, dve.tensor_copy(parts[32:64, :, :], tl[32:64, :, :]))
                link_part(4, dve.tensor_tensor(tl[64:96, :, :], tl[32:64, :, :], parts[32:64, :, :], ALU.subtract))
                dve.tensor_copy(parts[64:96, :, :], tl[64:96, :, :]).then_inc(s["parts_done"], 1)

            def take_b_and_g(i, q):
                dve.wait_ge(s["bt_ready"], i + 1)
                dve.tensor_copy(b_tok[:, q, :, :], mb[:, 0:NC * NS].rearrange("p (c n) -> p c n", c=NC)
                                ).then_inc(s["bt_taken"], 1)
                dve.wait_ge(s["g_ready"], i + 1)
                dve.tensor_copy(g_s[:, q, :, :], pj[1][:, :].rearrange("p (c t) -> p c t", c=NC)
                                ).then_inc(s["g_taken"], 1)

            split_tokens(0)
            time_step_input(0)
            conv_bc(0, 0)
            time_steps(0, 0)

            def slot(b, j):
                at = At(b, j)
                k = at.k
                new, mid, old = exists(b, j, 0), exists(b, j, 1), exists(b, j, 2)
                nxt = exists(b, j, at.st - SPI)
                m = At(b, j - 1)
                buf = m.js % 2

                def scan_pair(ks, bs, pair):
                    for h in (2 * pair, 2 * pair + 1):
                        dve.wait_ge(s["da_ready"], 6 * ks + h + 1)
                        dve.tensor_tensor_scan(dec[:, bs, h, :], da[h % 2][:, :], inject[:, :, :].rearrange("p c t -> p (c t)"),
                                               0.0, ALU.mult, ALU.add).then_inc(s["scan_done"], 1)
                    dve.wait_ge(s["scan_done"], 4 * ks + 2 * pair + 2)
                    dve.tensor_copy(w_end[:, bs, :, 2 * pair:2 * pair + 2],
                                    dec[:, bs, 2 * pair:2 * pair + 2, CH - 1::CH].rearrange("p h c -> p c h")
                                    ).then_inc(s["wend_done"], 1)

                if at.st == 3 and exists(b, j, 4) and (not isinstance(b, int) or k >= SPI):
                    dve.wait_ge(s["q_ready"], at.i)
                    dve.tensor_scalar(o_ms[:, :], mb[:, 0:NC], 1.0 / DIN, EPS, ALU.mult, ALU.add).then_inc(s["oms_done"], 1)
                for t in range(TPS):
                    if old:
                        o = At(b, j - 2)
                        dve.wait_ge(s["y_ready"], 2 * (k - 2) + t + 1)
                        ch = TPS * o.st + t
                        dve.scalar_tensor_tensor(xc[:, o.js % 2, t, :], xc[:, o.js % 2, t, :], dpar[:, ch:ch + 1],
                                                 yp[t][:, :], ALU.mult, ALU.add).then_inc(s["skip_done"], 1)
                    if mid and t == 0:
                        for n, bank in ((0, mb), (1, ma)):
                            dve.wait_ge(s["xt_ready"], 2 * (k - 1) + n + 1)
                            dve.tensor_tensor(
                                xdt[:, buf, 2 * n:2 * n + 2, :].rearrange("p c (h d) -> p c h d", d=HD),
                                bank[:, :].rearrange("p (c h d) -> p c h d", c=2, d=HD),
                                dt_s[:, m.q, 2 * n:2 * n + 2, HPS * m.st:HPS * (m.st + 1)].unsqueeze(3
                                    ).broadcast_to([P, 2, HPS, HD]),
                                ALU.mult).then_inc(s["xdt_done"], 1)
                if mid:
                    if new and at.st == 0:
                        time_steps(at.i, at.q)
                    for t in range(TPS):
                        dve.wait_ge(s["da_ready"], 6 * (k - 1) + HPS + t + 1)
                        if old:
                            dve.wait_ge(s["chain_done"], 8 * (k - 1))
                        dve.tensor_copy(p_end[:, t, :], da[t % 2][:, CH - 1::CH]).then_inc(s["pend_done"], 1)
                        dve.wait_ge(s["bc_ready"], 2 * m.i + 2)
                        dve.tensor_tensor(cp[:, t, :], da[t % 2][:, :], cc[:, m.q, :], ALU.mult).then_inc(s["cp_done"], 1)
                if new and at.st == 0:
                    decays(at.i, at.q, k)
                elif new:
                    scan_pair(k, at.js % 2, 0)

                def chain_states():
                    dve.wait_ge(s["ds_ready"], k)
                    dve.wait_ge(s["pend_done"], 2 * k)
                    if old:
                        dve.wait_ge(s["blk_done"], blk_count(b, j - 2))
                    for c in range(NC):
                        for t in range(TPS):
                            src = state[:, m.st, t, :] if c == 0 else s_ch[:, c - 1, t, :]
                            dst = state[:, m.st, t, :] if c == NC - 1 else s_ch[:, c, t, :]
                            add = ma[:, (c * TPS + t) * HD:(c * TPS + t + 1) * HD]
                            if c == NC - 1 and t == 0 and m.q:
                                dve.wait_ge(s["blk_done"], blk_count(b, j - 1) - 2)
                            if c == 0 and m.q == 0:
                                dve.tensor_copy(dst, add).then_inc(s["chain_done"], 1)
                            else:
                                if c:
                                    dve.wait_ge(s["chain_done"], 8 * (k - 1) + 2 * (c - 1) + t + 1)
                                dve.scalar_tensor_tensor(dst, src, p_end[:, t, c:c + 1], add, ALU.mult, ALU.add
                                                         ).then_inc(s["chain_done"], 1)

                def take_piece():
                    half, c, i = out_piece(b, j)
                    dve.wait_ge(s["o_ready"], piece_count(b, j))
                    if half == 0:
                        if c == 0:
                            dve.wait_ge(s["o_stored"], 16 * (i + 1))
                        dve.tensor_copy(o_acc[:, c, :], mb[:, 0:HID]).then_inc(s["o_taken"], 1)
                    else:
                        dve.tensor_tensor(o_acc[:, c, :], o_acc[:, c, :], mb[:, 0:HID], ALU.add).then_inc(s["o_taken"], 1)

                if new:
                    dve.wait_ge(s["pj_taken"], tile_count(at.i, 2 + 4 * at.st + 1))
                    conv_pair([(TPS * at.st + t, P, xc[:, at.js % 2, t, :]) for t in range(TPS)],
                              s["halo_done"], s["conv_tap"], 4 * k, 6 * k, at.q, chain_states if mid else None)
                elif mid:
                    chain_states()
                if new and at.st == 0:
                    scan_pair(k, at.js % 2, 0)
                if out_piece(b, j) and at.st != 7:
                    take_piece()
                if new and at.st == 0:
                    take_b_and_g(at.i, at.q)
                if nxt and at.st == 7:
                    split_tokens(at.i + 1)
                if new:
                    scan_pair(k, at.js % 2, 1)
                if at.st == 4 and exists(b, j, 5) and (not isinstance(b, int) or k >= SPI):
                    dve.wait_ge(s["ry_done"], at.i)
                    dve.wait_ge(s["o_taken"], 2 * NC * at.i)
                    for c in range(NC):
                        dve.tensor_scalar(o_acc[:, c, :], o_acc[:, c, :], r_y[:, c:c + 1], None, ALU.mult
                                          ).then_inc(s["o_scaled"], 1)
                if out_piece(b, j) and at.st == 7:
                    take_piece()
                if nxt and at.st == 7:
                    time_step_input(at.i + 1)
                    conv_bc(at.i + 1, (at.q + 1) % IPB)
                if nxt and at.st == 2:
                    token_norm_a(at.i + 1)
                if nxt and at.st == 3:
                    token_norm_b(at.i + 1)
                if nxt and at.st == 6:
                    token_ms(at.i + 1)

            run(dve, slot)

        @block.tensor
        def _(pe):
            pe.wait_ge(s["c_silu"], 1)
            for n, bank in enumerate((ma, mb, yp[0])):
                for kk in range(KH):
                    last = pe.matmul(bank[0:BATCH, :], cs_t[:, kk, :], wm[:, kk * MOD + n * T:kk * MOD + (n + 1) * T],
                                     start=(kk == 0), stop=(kk == KH - 1))
                last.then_inc(s["mod_ready"], 1)

            def project(i, idx, weights=0):
                wait(pe, s["pj_taken"], tile_count(i, idx) - 2)
                if weights:
                    pe.wait_ge(s["w_ready"], weights)
                cols = slice(idx * P, (idx + 1) * P)
                first = True
                for kk in range(KH):
                    for w, h in ((w_hi, h_hi), (w_hi, h_lo), (w_lo, h_hi)):
                        last = pe.matmul(pj[idx % 2][:, :], w[:, kk, cols], h[:, kk, :], start=first,
                                         stop=(kk == KH - 1 and w is w_lo))
                        first = False
                last.then_inc(s["pj_ready"], 1)

            def transpose_tokens(i):
                pe.wait_ge(s["hs_done"], 4 * i + 4)
                for kk, bank in ((0, pj[0]), (1, pj[1])):
                    for c in range(NC):
                        last = pe.transpose(bank[:, c * CH:(c + 1) * CH], hs[:, c, kk * P:(kk + 1) * P], ident[:, :])
                    last.then_inc(s["ht_ready"], 1)

            def project_bc(i, weights=0):
                pe.wait_ge(s["hl_done"], 2 * i + 2)
                project(i, 0, weights)
                project(i, 1, weights)

            def transpose_dt(i):
                wait_apart(pe, s["dt_copied"], i + 1)
                for c in range(NC):
                    last = pe.transpose(mb[:, c * HEADS:(c + 1) * HEADS], tl[64:96, 0, c * CH:(c + 1) * CH],
                                        ident[64:96, 64:96])
                last.then_inc(s["dtt_ready"], 1)

            def spread_decay(m, h):
                head = HPS * m.st + h
                for half in range(2):
                    last = pe.matmul(da[h % 2][64 * half:64 * half + 64, :], select[:, head, :], parts[:, 0, :],
                                     start=True, stop=True)
                last.then_inc(s["da_ready"], 1)

            pe.wait_ge(s["mod_fix"], 4)
            pe.wait_ge(s["consts"], 8)
            transpose_tokens(0)
            project_bc(0, KH)
            transpose_dt(0)

            def slot(b, j):
                at = At(b, j)
                k = at.k
                new, mid, old = exists(b, j, 0), exists(b, j, 1), exists(b, j, 2)
                nxt = exists(b, j, at.st - SPI)
                m = At(b, j - 1)
                first_run = isinstance(b, int) and b == 0
                if first_run and k == HEAD - 1:
                    pe.wait_ge(s["wo_ready"], YT)

                def spread_product(t):
                    pe.wait_ge(s["scan_done"], 4 * (k - 1) + HPS - 1 + t)
                    pair = select[:, HPS * m.st + 2 * t:HPS * m.st + 2 * t + 2, :].rearrange("p h n -> p (h n)")
                    pe.matmul(da[t % 2][:, :], pair, parts[:, 1, :], start=True, stop=True
                              ).then_inc(s["da_ready"], 1)

                if old:
                    o = At(b, j - 2)
                    buf = o.js % 2
                    pe.wait_ge(s["m_done"], 4 * (k - 2) + 4)
                    pe.wait_ge(s["blk_done"], blk_count(b, j - 2))
                    pe.wait_ge(s["cp_done"], 2 * (k - 2) + 2)
                if at.st == 3 and exists(b, j, 4) and (not isinstance(b, int) or k >= SPI):
                    pe.wait_ge(s["acc_done"], 2 * SPI * at.i)
                    pe.wait_ge(s["o_taken"], piece_count(b, j - 1))
                    if mid:
                        pe.wait_ge(s["chain_done"], 8 * (k - 1))
                    for c in range(NC):
                        last = pe.matmul(mb[:, c:c + 1], acc[:, c * CH:(c + 1) * CH], ones[:, :], start=True, stop=True)
                    last.then_inc(s["q_ready"], 1)
                for t in range(TPS):
                    if old:
                        if exists(b, j, 3):
                            pe.wait_ge(s["skip_done"], 2 * (k - 3) + t + 1)
                        for c in range(NC):
                            for half in range(2):
                                h = 2 * t + half
                                pe.matmul(yp[t][64 * half:64 * half + 64, c * CH:(c + 1) * CH],
                                          xdt[:, buf, c, h * HD:(h + 1) * HD], dec[:, buf, h, c * CH:(c + 1) * CH],
                                          start=(c == 0), stop=False, skip_group_check=True)
                        for c in range(1 if o.q == 0 else 0, NC):
                            last = pe.matmul(yp[t][:, c * CH:(c + 1) * CH], s_blk[:, c, t, :], cp[:, t, c * CH:(c + 1) * CH],
                                             start=False, stop=True, skip_group_check=True)
                        last.then_inc(s["y_ready"], 1)
                    if t == 0 and mid:
                        pe.wait_ge(s["x_ready"], 2 * (k - 1) + 2)
                        if old:
                            pe.wait_ge(s["chain_done"], 8 * (k - 1))
                        if new and at.st == 0:
                            pe.wait_ge(s["u_done"], at.i + 1)
                        if m.st == 0:
                            pe.wait_ge(s["bt_taken"], m.i + 1)
                        if out_piece(b, j - 1):
                            pe.wait_ge(s["o_taken"], piece_count(b, j - 1))
                        if at.st == 3 and exists(b, j, SPI):
                            pe.wait_ge(s["oms_done"], at.i)
                        for n, bank in ((0, mb), (1, ma)):
                            for c in range(2):
                                for t in range(TPS):
                                    last = pe.transpose(bank[:, (c * TPS + t) * P:(c * TPS + t + 1) * P],
                                                        xc[:, m.js % 2, t, (2 * n + c) * CH:(2 * n + c + 1) * CH], ident[:, :])
                            last.then_inc(s["xt_ready"], 1)
                        spread_product(0)
                        spread_product(1)

                def project_tile(n):
                    idx = 2 + 4 * at.st + n
                    weights = 0
                    if first_run and k < HEAD:
                        weights = WT if k == HEAD - 1 else 2 * (idx // 2 + 1)
                    project(at.i, idx, weights)

                def spread_two(h0):
                    for h in (h0, h0 + 1):
                        if h0:
                            pe.wait_ge(s["scan_done"], 4 * k + h - 1)
                        elif mid:
                            pe.wait_ge(s["cp_done"], 2 * (k - 1) + h + 1)
                        spread_decay(at, h)

                def multiply_piece():
                    half, c, i = out_piece(b, j)
                    pe.wait_ge(s["gate_done"], 2 * SPI * i + SPI * (half + 1))
                    if new and at.st == 0:
                        pe.wait_ge(s["dat_taken"], 6 * at.i + 1)
                    elif mid:
                        pe.wait_ge(s["xdt_done"], 2 * (k - 1) + 1)
                    else:
                        pe.wait_ge(s["o_taken"], piece_count(b, j - 1))
                        if at.st == 3:
                            pe.wait_ge(s["oms_done"], at.i)
                    for t in range(YT // 2):
                        tt = YT // 2 * half + t
                        last = pe.matmul(mb[:, 0:HID], yb[:, tt, c * CH:(c + 1) * CH], w_o[:, tt, :],
                                         start=(t == 0), stop=(t == YT // 2 - 1))
                    last.then_inc(s["o_ready"], 1)

                if new:
                    project_tile(0)
                    if at.st != 0:
                        spread_two(0)
                    if exists(b, j, 1) and m.st == 0:
                        pe.wait_ge(s["g_taken"], m.i + 1)
                    project_tile(1)
                if new:
                    if at.st == 0:
                        if mid:
                            wait_apart(pe, s["xdt_done"], 2 * (k - 1) + 1)
                        else:
                            pe.wait_ge(s["u_done"], 1)
                        pe.wait_ge(s["da_exp"], at.i + 1)
                        for c in range(NC):
                            last = pe.transpose(mb[0:HEADS, c * CH:(c + 1) * CH], a_t[:, c, :], ident[:, :])
                        last.then_inc(s["dat_ready"], 1)
                if mid:
                    pe.wait_ge(s["xw_done"], k)
                    pe.wait_ge(s["bt_taken"], m.i + 1)
                    for c in range(NC):
                        for half in range(2):
                            last = pe.matmul(
                                ma[64 * half:64 * half + 64, c * TPS * HD:(c + 1) * TPS * HD].rearrange("p (t d) -> p t d", d=HD),
                                b_tok[:, m.q, c, :],
                                xw[:, c, :].rearrange("p (t e d) -> p t e d", t=TPS, e=2)[:, :, half, :],
                                start=True, stop=True)
                    last.then_inc(s["ds_ready"], 1)
                if out_piece(b, j) and at.st != 7:
                    multiply_piece()
                if new:
                    project_tile(2)
                    if at.st == 0:
                        pe.wait_ge(s["parts_done"], 5 * (at.i + 1))
                        spread_two(0)
                    project_tile(3)
                if new and at.st == 0:
                    i = at.i
                    if out_piece(b, j):
                        wait_apart(pe, s["o_taken"], piece_count(b, j))
                    pe.wait_ge(s["dat_taken"], 6 * i + 1)
                    pe.wait_ge(s["bc_ready"], 2 * i + 2)
                    for c in range(NC):
                        last = pe.transpose(mb[:, c * NS:(c + 1) * NS], bb[:, c * CH:(c + 1) * CH], ident[0:NS, 0:NS])
                    last.then_inc(s["bt_ready"], 1)
                    pe.wait_ge(s["pj_taken"], tile_count(i, 5))
                    for c in range(NC):
                        last = pe.matmul(pj[1][:, c * CH:(c + 1) * CH], bb[:, c * CH:(c + 1) * CH],
                                         cc[0:NS, at.q, c * CH:(c + 1) * CH], start=True, stop=True)
                    last.then_inc(s["g_ready"], 1)
                if new:
                    spread_two(2)
                if nxt and at.st == 7:
                    pe.wait_ge(s["pj_taken"], tile_count(at.i, 5 + 4 * at.st))
                    transpose_tokens(at.i + 1)
                if out_piece(b, j) and at.st == 7:
                    multiply_piece()
                if nxt and at.st == 7:
                    project_bc(at.i + 1)
                    pe.wait_ge(s["o_taken"], piece_count(b, j))
                    transpose_dt(at.i + 1)

            run(pe, slot)


def mlp_phase(nc, x, w_up, w_dn, ln2, w_ff, rram, h_dram, o_dram, mod_dram, out):
    ctx = ExitStack()
    with ctx:
        def sb(name, shape, dt=F32):
            return ctx.enter_context(nc.sbuf_tensor(name, shape, dt))

        def pb(name):
            return ctx.enter_context(nc.psum_tensor(name, [P, T], F32))

        KI = INTER // P
        UP_ORDER = (0, 2, 1, 3)

        ident = sb("ident2", [P, P])
        neg_half = sb("neg_half2", [P, NC])
        wu_hi = sb("wu_hi", [P, KH, 2 * INTER], F32R)
        wu_lo = sb("wu_lo", [P, KH, 2 * INTER], F32R)
        wd_hi = sb("wd_hi", [P, KI, HID], F32R)
        wd_lo = sb("wd_lo", [P, KI, HID], F32R)
        wf_hi = sb("wf_hi", [P, KH, HID], F32R)
        wf_lo = sb("wf_lo", [P, KH, HID], F32R)
        wu_st = sb("wu_st", [P, len(UP_ORDER), KH, T])
        wd_st = sb("wd_st", [P, KI, HID])
        wf_st = sb("wf_st", [P, KH, HID])
        rr_st = sb("rr_st", [P, KH, HID])
        wf_a = sb("wf_a", [P, KH, HID])
        wf_b = sb("wf_b", [P, KH, HID])
        ln2_c = sb("ln2_c", [P, KH])
        rows = sb("rows", [P, 2, HID])
        cols = sb("cols", [P, BATCH, 2 * KH])
        x1 = sb("x1", [P, 2, NC, HID])
        hb = sb("hb", [P, NC, HID])
        xb = sb("xb", [P, 2, NC, HID])
        x1r = sb("x1r", [P, NC, HID])
        ssq = sb("ssq2", [P, NC])
        ms = sb("ms2", [P, NC])
        r2 = sb("r2", [P, NC])
        t_hi = sb("t_hi", [P, KH, T], F32R)
        t_lo = sb("t_lo", [P, KH, T], F32R)
        gate = sb("gate", [P, 2, T])
        mid = sb("mid", [P, 2, T])
        m_hi = sb("m_hi", [P, KI, T], F32R)
        m_lo = sb("m_lo", [P, KI, T], F32R)
        a_s = sb("a_s", [P, NC, HID])
        xn = sb("xn", [P, NC, HID])
        stats = sb("stats2", [P, NC, 6])
        mv = sb("mv2", [P, NC, 2])
        ve = sb("ve2", [P, NC])
        rstd = sb("rstd2", [P, NC])
        h2 = sb("h2", [P, KH, T])
        qn = sb("qn", [P, KH, T])
        q_t = sb("q_t", [P, KH, T], F32R)
        f_s = sb("f_s", [P, NC, HID])
        cg = [pb(f"cg{n}") for n in range(2)]
        cu = [pb(f"cu{n}") for n in range(2)]
        mo = [pb(f"mo{n}") for n in range(2)]
        mi = [pb(f"mi{n}") for n in range(2)]

        s = {n: ctx.enter_context(nc.semaphore("m_" + n)) for n in (
            "const_set consts small_loaded wu_loaded0 wu_loaded1 wu_loaded2 wu_loaded3 wd_loaded wf_loaded wu_head wu_ready wd_head "
            "wd_ready wf_step wf_ready o_loaded h_loaded x_loaded row_loaded x1_done ssq_done ms_done r2_done "
            "x1r_done bt_ready t_head t_ready c_ready gate_done mid_done head_done rest_done mo_ready a_done "
            "ga_done x2_done bn_done ve_done rstd_done xn_done dt_ready h2_done q_part q_done ff_ready f_done "
            "out_done out_stored").split()}
        block = ctx.enter_context(nc.Block())

        def run(eng, slot):
            slot(0, 0, 0)
            with eng.Fori(0, BATCH - 1) as b:
                for j in range(1, 1 + IPB):
                    slot(IPB * b + j, j, b)
            for j in range(1, 1 + IPB):
                slot(IPB * (BATCH - 1) + j, j, BATCH - 1)

        def known(i):
            return isinstance(i, int)

        def has(i):
            return not known(i) or 0 <= i < NI

        @block.sync
        def _(sp):
            def tokens(dram, i):
                return dram[bass.ds(i * T, T), :].rearrange("(c p) n -> p c n", p=P)

            def load_block(i, j):
                sp.dma_start(x1[:, j % 2, :, :], tokens(o_dram, i)).then_inc(s["o_loaded"], 16)
                sp.dma_start(hb[:, :, :], tokens(h_dram, i)).then_inc(s["h_loaded"], 16)

            def load_x(i, j):
                sp.dma_start(xb[:, j % 2, :, :], tokens(x, i)).then_inc(s["x_loaded"], 16)

            def load_rows(row):
                both = mod_dram.rearrange("b (g m n) -> b g m n", g=2, m=3)[bass.ds(row, 1), :, 2, :]
                sp.dma_start(rows[:, :, :], both.broadcast_to([P, 2, HID])).then_inc(s["row_loaded"], 16)

            sp.dma_start(ln2_c[:, :], ln2).then_inc(s["small_loaded"], 16)
            load_block(0, 0)
            load_x(0, 0)
            for bb in range(BATCH):
                for m, o in enumerate((3, 4)):
                    with nc.allow_non_contiguous_dma(reason="a few hundred numbers, once"):
                        sp.dma_start(cols[:, bb, m * KH:(m + 1) * KH],
                                     mod_dram[bb:bb + 1, o * HID:(o + 1) * HID].rearrange("b (k p) -> p (b k)", p=P)
                                     ).then_inc(s["small_loaded"], 16)
            for m, n in enumerate(UP_ORDER):
                sp.dma_start(wu_st[:, m, :, :], w_up.rearrange("(k p) n -> p k n", p=P)[:, :, n * T:(n + 1) * T]
                             ).then_inc(s[f"wu_loaded{m}"], 16)
            sp.dma_start(wd_st[:, :, :], w_dn.rearrange("(k p) n -> p k n", p=P)).then_inc(s["wd_loaded"], 16)
            sp.dma_start(wf_st[:, :, :], w_ff.rearrange("(k p) n -> p k n", p=P)).then_inc(s["wf_loaded"], 16)
            sp.dma_start(rr_st[:, :, :], rram.rearrange("(k p) n -> p k n", p=P)).then_inc(s["wf_loaded"], 16)
            load_rows(0)

            def slot(i, j, row):
                new, nxt, old = has(i), has(i + 1), has(i - 1)
                if nxt:
                    if old:
                        wait_apart(sp, s["a_done"], 2 * i)
                    sp.wait_ge(s["x1_done"], i + 1)
                    load_block(i + 1, j + 1)
                if old:
                    sp.wait_ge(s["out_done"], i)
                    sp.dma_start(tokens(out, i - 1), a_s[:, :, :]).then_inc(s["out_stored"], 16)
                if nxt:
                    load_x(i + 1, j + 1)
                if old and new and j == IPB:
                    load_rows(row + 1)

            sp.sem_inc(s["out_stored"], 16)
            run(sp, slot)
            sp.wait_ge(s["out_stored"], 16 * (NI + 1))
            sp.wait_ge(s["row_loaded"], 16 * BATCH)

        @block.gpsimd
        def _(pool):
            pool.memset(ident[:, :], 0.0).then_inc(s["const_set"], 1)
            pool.memset(neg_half[:, :], -0.5).then_inc(s["consts"], 1)
            pool.wait_ge(s["const_set"], 1)
            pool.affine_select(out=ident[:, :], in_=ident[:, :], compare_op=ALU.not_equal, fill=1.0, base=0,
                               pattern=[[-1, P]], channel_multiplier=1).then_inc(s["consts"], 1)
            pool.wait_ge(s["consts"], 2)

            def residual(i, j):
                pool.wait_ge(s["o_loaded"], 16 * (i + 1))
                pool.wait_ge(s["h_loaded"], 16 * (i + 1))
                pool.tensor_tensor(x1[:, j % 2, :, :], x1[:, j % 2, :, :], hb[:, :, :], ALU.add).then_inc(s["x1_done"], 1)

            def rms_power(i):
                pool.wait_ge(s["ms_done"], i + 1)
                pool.tensor_tensor(r2[:, :], ms[:, :], neg_half[:, :], ALU.pow).then_inc(s["r2_done"], 1)

            residual(0, 0)
            rms_power(0)

            def slot(i, j, row):
                old = has(i - 1)
                if old:
                    p = (j - 1) % 2
                    pool.wait_ge(s["a_done"], 2 * i)
                    pool.wait_ge(s["row_loaded"], 16 * (row + 1))
                    pool.tensor_tensor(a_s[:, :, :], a_s[:, :, :], rows[:, 0:1, :].broadcast_to([P, NC, HID]), ALU.mult
                                       ).then_inc(s["ga_done"], 1)
                    pool.wait_ge(s["ga_done"], i)
                    pool.wait_ge(s["x_loaded"], 16 * i)
                    pool.tensor_tensor(xb[:, p, :, :], xb[:, p, :, :], a_s[:, :, :], ALU.add).then_inc(s["x2_done"], 1)
                    pool.wait_ge(s["ve_done"], i)
                    pool.tensor_tensor(rstd[:, :], ve[:, :], neg_half[:, :], ALU.pow).then_inc(s["rstd_done"], 1)
                if has(i + 1):
                    residual(i + 1, j + 1)
                    rms_power(i + 1)
                if old:
                    pool.wait_ge(s["f_done"], 2 * i)
                    pool.tensor_tensor(a_s[:, :, :], xb[:, p, :, :], f_s[:, :, :], ALU.add).then_inc(s["out_done"], 1)

            run(pool, slot)

        @block.scalar
        def _(act):
            def squares(i, j, chunks=range(NC)):
                act.wait_ge(s["x1_done"], i + 1)
                if j:
                    act.wait_ge(s["bt_ready"], 2 * i)
                for c in chunks:
                    act.activation(x1r[:, c, :], x1[:, j % 2, c, :], ACT.Square, accum_out=ssq[:, c:c + 1]
                                   ).then_inc(s["ssq_done"], 1)

            def scale(i, j, chunks=range(NC)):
                act.wait_ge(s["r2_done"], i + 1)
                act.wait_ge(s["ssq_done"], 4 * i + 4)
                for c in chunks:
                    act.activation(x1r[:, c, :], x1[:, j % 2, c, :], ACT.Copy, scale=r2[:, c:c + 1]
                                   ).then_inc(s["x1r_done"], 1)

            def head_up(m):
                n = UP_ORDER[m]
                act.wait_ge(s[f"wu_loaded{m}"], 16)
                for kk in range(KH):
                    act.activation(wu_hi[:, kk, n * T:(n + 1) * T], wu_st[:, m, kk, :], ACT.Copy,
                                   scale=ln2_c[:, kk:kk + 1]).then_inc(s["wu_head"], 1)

            act.wait_ge(s["small_loaded"], 16 * 9)
            squares(0, 0)
            head_up(0)
            head_up(1)
            scale(0, 0)
            head_up(2)
            head_up(3)
            act.wait_ge(s["wd_loaded"], 16)
            act.activation(wd_hi[:, :, :], wd_st[:, :, :], ACT.Copy).then_inc(s["wd_head"], 1)

            def slot(i, j, row):
                new = has(i)
                for t in range(KI):
                    if new:
                        n = KI * i + t
                        act.wait_ge(s["c_ready"], 2 * n + 1)
                        if t >= 2 or j:
                            act.wait_ge(s["mid_done"], n - 1)
                        act.activation(gate[:, t % 2, :], cg[t % 2][:, :], ACT.Silu).then_inc(s["gate_done"], 1)
                        act.wait_ge(s["mid_done"], n + 1)
                        if t == 0 and j:
                            act.wait_ge(s["mo_ready"], 2 * i)
                        act.activation(m_hi[:, t, :], mid[:, t % 2, :], ACT.Copy).then_inc(s["head_done"], 1)
                    if t == 3 and has(i + 1):
                        squares(i + 1, j + 1)
                    if t == 5 and has(i - 1):
                        for kk in range(KH):
                            wait_apart(act, s["dt_ready"], 2 * (i - 1) + kk + 1)
                            at = cols[:, bass.ds(row, 1), :].rearrange("p b k -> p (b k)")
                            act.activation(h2[:, kk, :], mi[kk][:, :], ACT.Identity, bias=at[:, kk:kk + 1],
                                           scale=at[:, KH + kk:KH + kk + 1]).then_inc(s["h2_done"], 1)
                    if t == 6 and has(i + 1):
                        scale(i + 1, j + 1)

            run(act, slot)

        @block.vector
        def _(dve):
            def mean_square(i):
                dve.wait_ge(s["ssq_done"], 4 * i + 4)
                dve.tensor_scalar(ms[:, :], ssq[:, :], 1.0 / HID, EPS, ALU.mult, ALU.add).then_inc(s["ms_done"], 1)

            mean_square(0)
            dve.wait_ge(s["small_loaded"], 16 * 9)

            def rest_up(m):
                n = UP_ORDER[m]
                for kk in range(KH):
                    dve.wait_ge(s["wu_head"], KH * m + kk + 1)
                    dve.scalar_tensor_tensor(wu_lo[:, kk, n * T:(n + 1) * T], wu_st[:, m, kk, :], ln2_c[:, kk:kk + 1],
                                             wu_hi[:, kk, n * T:(n + 1) * T].bitcast(F32), ALU.mult, ALU.subtract
                                             ).then_inc(s["wu_ready"], 1)

            def rest_down():
                dve.wait_ge(s["wd_head"], 1)
                dve.tensor_tensor(wd_lo[:, :, :], wd_st[:, :, :], wd_hi[:, :, :].bitcast(F32), ALU.subtract
                                  ).then_inc(s["wd_ready"], 1)

            def ternary_weights():
                dve.wait_ge(s["wf_loaded"], 32)
                dve.tensor_scalar(wf_a[:, :, :], wf_st[:, :, :], THW, SCW, ALU.is_gt, ALU.mult).then_inc(s["wf_step"], 1)
                dve.tensor_scalar(wf_b[:, :, :], wf_st[:, :, :], -THW, SCW, ALU.is_lt, ALU.mult).then_inc(s["wf_step"], 1)
                dve.wait_ge(s["wf_step"], 2)
                dve.tensor_tensor(wf_a[:, :, :], wf_a[:, :, :], wf_b[:, :, :], ALU.subtract).then_inc(s["wf_step"], 1)
                dve.wait_ge(s["wf_step"], 3)
                dve.tensor_tensor(wf_a[:, :, :], wf_a[:, :, :], rr_st[:, :, :], ALU.add).then_inc(s["wf_step"], 1)
                dve.wait_ge(s["wf_step"], 4)
                dve.tensor_copy(wf_hi[:, :, :], wf_a[:, :, :]).then_inc(s["wf_step"], 1)
                dve.wait_ge(s["wf_step"], 5)
                dve.tensor_tensor(wf_lo[:, :, :], wf_a[:, :, :], wf_hi[:, :, :].bitcast(F32), ALU.subtract
                                  ).then_inc(s["wf_ready"], 1)

            def split_tokens(i):
                for kk in range(KH):
                    dve.wait_ge(s["bt_ready"], 2 * i + kk + 1)
                    dve.tensor_copy(t_hi[:, kk, :], mi[kk][:, :]).then_inc(s["t_head"], 1)
                    dve.wait_ge(s["t_head"], 2 * i + kk + 1)
                    dve.tensor_tensor(t_lo[:, kk, :], mi[kk][:, :], t_hi[:, kk, :].bitcast(F32), ALU.subtract
                                      ).then_inc(s["t_ready"], 1)

            rest_up(0)
            rest_up(1)
            split_tokens(0)
            rest_up(2)
            rest_up(3)

            def slot(i, j, row):
                new, old = has(i), has(i - 1)
                if old:
                    p = (j - 1) % 2
                    for n in range(2):
                        dve.wait_ge(s["mo_ready"], 2 * (i - 1) + n + 1)
                        dve.wait_ge(s["out_stored"], 16 * i)
                        dve.tensor_tensor(a_s[:, 2 * n:2 * n + 2, :].rearrange("p c d -> p (c d)"),
                                          mo[n][:, :], x1[:, p, 2 * n:2 * n + 2, :].rearrange("p c d -> p (c d)"), ALU.add
                                          ).then_inc(s["a_done"], 1)
                for t in range(KI):
                    if new:
                        n = KI * i + t
                        dve.wait_ge(s["c_ready"], 2 * n + 2)
                        dve.wait_ge(s["gate_done"], n + 1)
                        if t >= 2 or j:
                            dve.wait_ge(s["rest_done"], n - 1)
                        dve.tensor_tensor(mid[:, t % 2, :], cu[t % 2][:, :], gate[:, t % 2, :], ALU.mult
                                          ).then_inc(s["mid_done"], 1)
                        if t:
                            rest(i, n - 1, t - 1)
                    if t == 2 and j == 0:
                        rest_down()
                    if t == 1 and old:
                        dve.wait_ge(s["x2_done"], i)
                        for c in range(NC):
                            dve.bn_stats(stats[:, c, :], xb[:, p, c, :]).then_inc(s["bn_done"], 1)
                        wait_apart(dve, s["bn_done"], 8 * (i - 1) + 4)
                        for c in range(NC):
                            dve.bn_aggr(mv[:, c, :], stats[:, c, :]).then_inc(s["bn_done"], 1)
                        dve.wait_ge(s["bn_done"], 8 * i)
                        dve.tensor_scalar(ve[:, :], mv[:, :, 1], EPS, None, ALU.add).then_inc(s["ve_done"], 1)
                    if t == 3 and old:
                        dve.wait_ge(s["rstd_done"], i)
                        for c in range(NC):
                            dve.tensor_scalar(xn[:, c, :], xb[:, p, c, :], mv[:, c, 0:1], rstd[:, c:c + 1],
                                              ALU.subtract, ALU.mult).then_inc(s["xn_done"], 1)
                    if t == 4 and has(i + 1):
                        mean_square(i + 1)
                    if t == 6 and old:
                        dve.wait_ge(s["h2_done"], 2 * i)
                        dve.tensor_scalar(qn[:, :, :], h2[:, :, :], -THX, SCX, ALU.is_lt, ALU.mult).then_inc(s["q_part"], 1)
                        dve.tensor_scalar(h2[:, :, :], h2[:, :, :], THX, SCX, ALU.is_gt, ALU.mult).then_inc(s["q_part"], 1)
                        dve.wait_ge(s["q_part"], 2 * i)
                        dve.tensor_tensor(q_t[:, :, :], h2[:, :, :], qn[:, :, :], ALU.subtract).then_inc(s["q_done"], 1)
                if new:
                    rest(i, KI * i + KI - 1, KI - 1)
                if j == 0:
                    ternary_weights()
                if old:
                    for n in range(2):
                        dve.wait_ge(s["ff_ready"], 2 * (i - 1) + n + 1)
                        dve.tensor_tensor(f_s[:, 2 * n:2 * n + 2, :], mo[n][:, :].rearrange("p (c d) -> p c d", c=2),
                                          rows[:, 1:2, :].broadcast_to([P, 2, HID]), ALU.mult).then_inc(s["f_done"], 1)
                if has(i + 1):
                    split_tokens(i + 1)

            def rest(i, n, t):
                dve.wait_ge(s["head_done"], n + 1)
                dve.tensor_tensor(m_lo[:, t, :], mid[:, t % 2, :], m_hi[:, t, :].bitcast(F32), ALU.subtract
                                  ).then_inc(s["rest_done"], 1)

            run(dve, slot)

        @block.tensor
        def _(pe):
            pe.wait_ge(s["consts"], 2)

            def transpose_tokens(i):
                pe.wait_ge(s["x1r_done"], 4 * i + 4)
                for kk in range(KH):
                    for c in range(NC):
                        last = pe.transpose(mi[kk][:, c * CH:(c + 1) * CH], x1r[:, c, kk * P:(kk + 1) * P], ident[:, :])
                    last.then_inc(s["bt_ready"], 1)

            transpose_tokens(0)

            def slot(i, j, row):
                new, old = has(i), has(i - 1)
                for t in range(KI):
                    if new:
                        n = KI * i + t
                        if t == 0:
                            if j == 0:
                                pe.wait_ge(s["wu_ready"], KH * 2)
                            pe.wait_ge(s["t_ready"], 2 * i + 2)
                        if t == KI // 2 and j == 0:
                            pe.wait_ge(s["wu_ready"], KH * 4)
                        for bank, half in ((cg[t % 2], 0), (cu[t % 2], 1)):
                            if t >= 2 or j:
                                pe.wait_ge(s["mid_done" if half else "gate_done"], n - 1)
                            cut = slice((half * KI + t) * P, (half * KI + t + 1) * P)
                            first = True
                            for kk in range(KH):
                                for w, h in ((wu_hi, t_hi), (wu_hi, t_lo), (wu_lo, t_hi)):
                                    last = pe.matmul(bank[:, :], w[:, kk, cut], h[:, kk, :], start=first,
                                                     stop=(kk == KH - 1 and w is wu_lo))
                                    first = False
                            last.then_inc(s["c_ready"], 1)
                    if t == 5 and old:
                        pe.wait_ge(s["xn_done"], 4 * i)
                        for kk in range(KH):
                            for c in range(NC):
                                last = pe.transpose(mi[kk][:, c * CH:(c + 1) * CH], xn[:, c, kk * P:(kk + 1) * P], ident[:, :])
                            last.then_inc(s["dt_ready"], 1)
                if j == 0:
                    pe.wait_ge(s["wd_ready"], 1)
                if has(i + 1):
                    if old:
                        pe.wait_ge(s["h2_done"], 2 * i)
                    else:
                        pe.wait_ge(s["t_ready"], 2)
                    transpose_tokens(i + 1)
                if old:
                    if j == 1:
                        pe.wait_ge(s["wf_ready"], 1)
                    pe.wait_ge(s["q_done"], i)
                    pe.wait_ge(s["a_done"], 2 * i)
                    for n in range(2):
                        for c in range(2):
                            first = True
                            cut = slice((2 * n + c) * CH, (2 * n + c + 1) * CH)
                            for kk in range(KH):
                                for w in (wf_hi, wf_lo):
                                    last = pe.matmul(mo[n][:, c * HID:(c + 1) * HID], q_t[:, kk, cut], w[:, kk, :],
                                                     start=first, stop=(kk == KH - 1 and w is wf_lo))
                                    first = False
                        last.then_inc(s["ff_ready"], 1)
                if new:
                    pe.wait_ge(s["rest_done"], KI * (i + 1))
                    if j:
                        pe.wait_ge(s["f_done"], 2 * i)
                    for n in range(2):
                        for c in range(2):
                            first = True
                            cut = slice((2 * n + c) * CH, (2 * n + c + 1) * CH)
                            for t in range(KI):
                                for m, w in ((m_hi, wd_hi), (m_hi, wd_lo), (m_lo, wd_hi)):
                                    last = pe.matmul(mo[n][:, c * HID:(c + 1) * HID], m[:, t, cut], w[:, t, :],
                                                     start=first, stop=(t == KI - 1 and m is m_lo))
                                    first = False
                        last.then_inc(s["mo_ready"], 1)

            run(pe, slot)


def adaln_mamba_block(nc, x, w_in, ln1, conv_w, conv_b, a_log, d_par, dt_bias, w_out, mnorm, c_t, w_mod,
                      w_up, w_dn, ln2, w_ff, rram, out):
    h_dram = nc.dram_tensor("h_scratch", [BATCH * SEQ, HID], F32).ap()
    o_dram = nc.dram_tensor("o_scratch", [BATCH * SEQ, HID], F32).ap()
    mod_dram = nc.dram_tensor("mod_scratch", [BATCH, MOD], F32).ap()
    mamba_phase(nc, x, w_in, ln1, conv_w, conv_b, a_log, d_par, dt_bias, w_out, mnorm, c_t, w_mod,
                h_dram, o_dram, mod_dram)
    mlp_phase(nc, x, w_up, w_dn, ln2, w_ff, rram, h_dram, o_dram, mod_dram, out)


def kernel(**inputs):
    import numpy as np
    import concourse.bacc as bacc
    from concourse.bass_utils import run_bass_kernel_spmd

    a = {name: np.asarray(value) for name, value in inputs.items()}

    def by_channel(v):
        return v.reshape((-1, P) + v.shape[1:]).swapaxes(0, 1)

    z0, x0, b0 = 0, DIN, 2 * DIN
    b_rows, c_rows, dt_rows = b0 + np.arange(NS), b0 + NS + np.arange(NS), b0 + 2 * NS + np.arange(HEADS)
    order = [b_rows, dt_rows, dt_rows, c_rows, c_rows]
    for st in range(SPI):
        step = np.arange(TPS * P) + TPS * P * st
        order += [x0 + step, z0 + step]
    order = np.concatenate(order)
    conv = np.concatenate([np.arange(DIN), c_rows - DIN, c_rows - DIN, b_rows - DIN, b_rows - DIN])
    arrays = dict(
        x=a["L0_attn_x"].reshape(BATCH * SEQ, HID),
        w_in=a["L0_attn_in_proj_w"][order].T,
        ln1=by_channel(a["L0_attn_ln1_w"]),
        conv_w=by_channel(a["L0_attn_conv_w"].reshape(-1, TAPS)[conv]),
        conv_b=by_channel(a["L0_attn_conv_b"][conv]),
        a_log=a["L0_attn_A_log"][None],
        d_par=by_channel(np.repeat(a["L0_attn_D_param"], HD)),
        dt_bias=a["L0_attn_dt_bias"][None],
        w_out=a["L0_attn_out_proj_w"].T,
        mnorm=by_channel(a["L0_attn_mnorm_w"]),
        c_t=by_channel(a["L0_c"].T),
        w_mod=a["L0_wmod"],
        w_up=a["L0_attn_mlp_in_w"].T,
        w_dn=a["L0_attn_mlp_out_w"].T,
        ln2=by_channel(a["L0_attn_ln2_w"]),
        w_ff=a["L0_ffn_weight"].T,
        rram=a["L0_ffn_rram_variation"].T,
    )
    arrays = {name: np.ascontiguousarray(v) for name, v in arrays.items()}
    nc = bacc.Bacc("TRN2", target_bir_lowering=False, num_devices=1, dynamic_dma_scratch_size=1024)
    args = [nc.dram_tensor(name, v.shape, F32, kind="ExternalInput").ap() for name, v in arrays.items()]
    out = nc.dram_tensor("out", (BATCH * SEQ, HID), F32, kind="ExternalOutput").ap()
    adaln_mamba_block(nc, *args, out)
    r = run_bass_kernel_spmd(nc, [arrays], core_ids=[0])
    return r.results[0]["out"].reshape(BATCH, SEQ, HID)
```
